# Optimizing a Trainium2 kernel written in Bass

```python
import numpy as np
import jax
import jax.numpy as jnp

def _softmax(x, axis=-1):
    return jax.nn.softmax(x, axis=axis)

def _gelu(x):
    return jax.nn.gelu(x, approximate=True)

def _silu(x):
    return jax.nn.silu(x)

def _sigmoid(x):
    return jax.nn.sigmoid(x)

def _layernorm(x, axis=-1, eps=1e-05):
    m = jnp.mean(x, axis=axis, keepdims=True)
    v = jnp.var(x, axis=axis, keepdims=True)
    return (x - m) / jnp.sqrt(v + eps)

def _scatter_add(tgt, idx, src, axis=0):
    return tgt.at[idx].add(src)

def _segment_sum(src, seg, n):
    return jax.ops.segment_sum(src, seg, n)
kernel_name = 'mk_xattn_ffn_d1_seqx_r4_072202'

def setup_inputs(seed: int=0):
    np.random.seed(seed)
    _w = jnp.asarray

    def _rec_inputs():
        import jax
        import jax.numpy as jnp
        _rk = jax.random.key(seed)
        x = -0.0002928 + 1 * jax.random.normal(jax.random.fold_in(_rk, 1), (2, 1024, 256), jnp.float32)
        _lenS = 1024 - jax.random.randint(jax.random.fold_in(_rk, 7), (2,), 0, max(1, 1024 // 4) + 1, jnp.int32)
        _lenS2 = 154 - jax.random.randint(jax.random.fold_in(_rk, 8), (2,), 0, max(1, 154 // 4) + 1, jnp.int32)
        _ctx_1024P = jax.random.normal(jax.random.fold_in(_rk, 11), (2, 16, 256), jnp.float32)
        _ctx_1024c = jax.random.dirichlet(jax.random.fold_in(_rk, 511), 0.3 * jnp.ones((16,), jnp.float32), (2, 154))
        _ctx_1024t = jnp.einsum('bsk,bkd->bsd', _ctx_1024c, _ctx_1024P)
        _ctx_1024t = _ctx_1024t * jax.lax.rsqrt(jnp.mean(jnp.square(_ctx_1024t)) + 1e-12) * 0.953939
        ctx_1024 = 0.000227908 + 0.99994 * (_ctx_1024t + 0.3 * jax.random.normal(jax.random.fold_in(_rk, 611), (2, 154, 256), jnp.float32))
        _validS = jnp.arange(1024)[None, :] < _lenS[:, None]
        _validS2 = jnp.arange(154)[None, :] < _lenS2[:, None]
        _causal = jnp.tril(jnp.ones((1024, 1024), dtype=bool))
        mask_SxS_bc0 = jnp.logical_not(jnp.broadcast_to(_causal[:, :], (1024, 1024)))
        return (x, ctx_1024, mask_SxS_bc0)
    x, ctx_1024, mask_SxS_bc0 = _rec_inputs()

    def _L0_xattn_setup():
        import jax, jax.numpy as jnp
        import numpy as np
        from jax import lax
        H = 16
        K1, K2 = (3, 3)
        LN_EPS = 1e-05

        def _ln(x, g, b):
            m = jnp.mean(x, axis=-1, keepdims=True)
            v = jnp.mean(jnp.square(x - m), axis=-1, keepdims=True)
            return (x - m) * lax.rsqrt(v + LN_EPS) * g + b

        def _gelu(x):
            return jax.nn.gelu(x, approximate=False)
        key = jax.random.key(seed)
        B, T, D, Th = (4, 256, 256, 64)
        C = 2 * D
        ks = jax.random.split(key, 16)

        def w(k, shape):
            fan_in = shape[0]
            return (jax.random.normal(k, shape, jnp.float32) / np.sqrt(fan_in)).astype(jnp.float32)
        inp = {'x': jax.random.normal(ks[0], (B, T, D), jnp.float32), 'historical_data': jax.random.normal(ks[1], (B, Th, D), jnp.float32), 'Wq': w(ks[2], (D, D)), 'Wk': w(ks[3], (D, D)), 'Wv': w(ks[4], (D, D)), 'hist_W': w(ks[5], (D, C)), 'hist_b': jnp.zeros((C,), jnp.float32), 'hist_ln_g': jnp.ones((C,), jnp.float32), 'hist_ln_b': jnp.zeros((C,), jnp.float32), 'ctx_W1': w(ks[6], (C, C // 4)), 'ctx_b1': jnp.zeros((C // 4,), jnp.float32), 'ctx_W2': w(ks[7], (C // 4, 1)), 'ctx_b2': jnp.zeros((1,), jnp.float32), 'kg_W1': w(ks[8], (C, D)), 'kg_b1': jnp.zeros((D,), jnp.float32), 'kg_ln_g': jnp.ones((D,), jnp.float32), 'kg_ln_b': jnp.zeros((D,), jnp.float32), 'kg_W2': w(ks[9], (D, H * K1 * K2)), 'kg_b2': jnp.zeros((H * K1 * K2,), jnp.float32), 'proj_W': w(ks[10], (D, D)), 'proj_b': jnp.zeros((D,), jnp.float32), 'causal_mask': jnp.triu(jnp.ones((T, T), bool), k=1)}
        return inp
    _L0_xattn_all = _L0_xattn_setup()
    _L0_xattn_in = {k: v for k, v in _L0_xattn_all.items() if k in ('Wq', 'Wk', 'Wv', 'hist_W', 'hist_b', 'hist_ln_g', 'hist_ln_b', 'ctx_W1', 'ctx_b1', 'ctx_W2', 'ctx_b2', 'kg_W1', 'kg_b1', 'kg_ln_g', 'kg_ln_b', 'kg_W2', 'kg_b2', 'proj_W', 'proj_b')}
    del _L0_xattn_all

    def _L0_ffn_setup():
        import jax, jax.numpy as jnp
        import numpy as np
        LOOPS = 2
        NUM_GROUPS = 4
        EXPERTS_PER_GROUP = 2
        NUM_EXPERTS = NUM_GROUPS * EXPERTS_PER_GROUP
        GROUPS_TOP_K = 2
        TOP_K = 1
        RMS_EPS = 1e-06
        EPS = 1e-09

        def _rmsnorm(x, w):
            return x * jax.lax.rsqrt(jnp.mean(x * x, axis=-1, keepdims=True) + RMS_EPS) * w

        def _combine_weights(x_flat, w_macro, w_micro):
            T = x_flat.shape[0]
            macro = jax.nn.softmax(x_flat @ w_macro.T, axis=-1)
            mvals, midx = jax.lax.top_k(macro, GROUPS_TOP_K)
            mvals = mvals / (jnp.sum(mvals, axis=-1, keepdims=True) + EPS)
            micro = jax.nn.softmax(jnp.einsum('td,ged->tge', x_flat, w_micro), axis=-1)
            uvals, uidx = jax.lax.top_k(micro, TOP_K)
            uvals = uvals / (jnp.sum(uvals, axis=-1, keepdims=True) + EPS)
            tok = jnp.arange(T)
            combine = jnp.zeros((T, NUM_EXPERTS), x_flat.dtype)
            for s in range(GROUPS_TOP_K):
                g = midx[:, s]
                wg = mvals[:, s:s + 1]
                li = uidx[tok, g]
                lv = uvals[tok, g]
                eidx = g[:, None] * EXPERTS_PER_GROUP + li
                combine = combine.at[tok[:, None], eidx].add(lv * wg)
            return combine
        key = jax.random.key(seed)
        ks = jax.random.split(key, 6)
        B, S, D, F = (2, 256, 256, 512)
        return {'z': jax.random.normal(ks[0], (B, S, D), jnp.float32), 'norm_w': jnp.ones((D,), jnp.float32), 'w_macro': jax.random.normal(ks[1], (NUM_GROUPS, D), jnp.float32) * D ** (-0.5), 'w_micro': jax.random.normal(ks[2], (NUM_GROUPS, EXPERTS_PER_GROUP, D), jnp.float32) * D ** (-0.5), 'w1': jax.random.normal(ks[3], (NUM_EXPERTS, F, D), jnp.float32) * D ** (-0.5), 'w2': jax.random.normal(ks[4], (NUM_EXPERTS, D, F), jnp.float32) * F ** (-0.5)}
    _L0_ffn_all = _L0_ffn_setup()
    _L0_ffn_in = {k: v for k, v in _L0_ffn_all.items() if k in ('norm_w', 'w_macro', 'w_micro', 'w1', 'w2')}
    del _L0_ffn_all
    return {'x': x, 'ctx_1024': ctx_1024, 'mask_SxS_bc0': mask_SxS_bc0, 'L0_xattn_Wq': _L0_xattn_in['Wq'], 'L0_xattn_Wk': _L0_xattn_in['Wk'], 'L0_xattn_Wv': _L0_xattn_in['Wv'], 'L0_xattn_hist_W': _L0_xattn_in['hist_W'], 'L0_xattn_hist_b': _L0_xattn_in['hist_b'], 'L0_xattn_hist_ln_g': _L0_xattn_in['hist_ln_g'], 'L0_xattn_hist_ln_b': _L0_xattn_in['hist_ln_b'], 'L0_xattn_ctx_W1': _L0_xattn_in['ctx_W1'], 'L0_xattn_ctx_b1': _L0_xattn_in['ctx_b1'], 'L0_xattn_ctx_W2': _L0_xattn_in['ctx_W2'], 'L0_xattn_ctx_b2': _L0_xattn_in['ctx_b2'], 'L0_xattn_kg_W1': _L0_xattn_in['kg_W1'], 'L0_xattn_kg_b1': _L0_xattn_in['kg_b1'], 'L0_xattn_kg_ln_g': _L0_xattn_in['kg_ln_g'], 'L0_xattn_kg_ln_b': _L0_xattn_in['kg_ln_b'], 'L0_xattn_kg_W2': _L0_xattn_in['kg_W2'], 'L0_xattn_kg_b2': _L0_xattn_in['kg_b2'], 'L0_xattn_proj_W': _L0_xattn_in['proj_W'], 'L0_xattn_proj_b': _L0_xattn_in['proj_b'], 'L0_ffn_norm_w': _L0_ffn_in['norm_w'], 'L0_ffn_w_macro': _L0_ffn_in['w_macro'], 'L0_ffn_w_micro': _L0_ffn_in['w_micro'], 'L0_ffn_w1': _L0_ffn_in['w1'], 'L0_ffn_w2': _L0_ffn_in['w2']}

def reference(x, ctx_1024, mask_SxS_bc0, L0_xattn_Wq, L0_xattn_Wk, L0_xattn_Wv, L0_xattn_hist_W, L0_xattn_hist_b, L0_xattn_hist_ln_g, L0_xattn_hist_ln_b, L0_xattn_ctx_W1, L0_xattn_ctx_b1, L0_xattn_ctx_W2, L0_xattn_ctx_b2, L0_xattn_kg_W1, L0_xattn_kg_b1, L0_xattn_kg_ln_g, L0_xattn_kg_ln_b, L0_xattn_kg_W2, L0_xattn_kg_b2, L0_xattn_proj_W, L0_xattn_proj_b, L0_ffn_norm_w, L0_ffn_w_macro, L0_ffn_w_micro, L0_ffn_w1, L0_ffn_w2):
    import jax
    import jax.numpy as jnp

    def _L0_xattn_ref(x, historical_data, Wq, Wk, Wv, hist_W, hist_b, hist_ln_g, hist_ln_b, ctx_W1, ctx_b1, ctx_W2, ctx_b2, kg_W1, kg_b1, kg_ln_g, kg_ln_b, kg_W2, kg_b2, proj_W, proj_b, causal_mask):
        import jax, jax.numpy as jnp
        import numpy as np
        from jax import lax
        H = 16
        K1, K2 = (3, 3)
        LN_EPS = 1e-05

        def _ln(x, g, b):
            m = jnp.mean(x, axis=-1, keepdims=True)
            v = jnp.mean(jnp.square(x - m), axis=-1, keepdims=True)
            return (x - m) * lax.rsqrt(v + LN_EPS) * g + b

        def _gelu(x):
            return jax.nn.gelu(x, approximate=False)
        B, T, D = x.shape
        hd = D // H
        scale = hd ** (-0.5)
        q = (x @ Wq).reshape(B, T, H, hd).transpose(0, 2, 1, 3)
        k = (x @ Wk).reshape(B, T, H, hd).transpose(0, 2, 1, 3)
        v = (x @ Wv).reshape(B, T, H, hd).transpose(0, 2, 1, 3)
        attn = jnp.einsum('bhqd,bhkd->bhqk', q, k) * scale
        eh = _gelu(_ln(historical_data @ hist_W + hist_b, hist_ln_g, hist_ln_b))
        aw = _gelu(eh @ ctx_W1 + ctx_b1) @ ctx_W2 + ctx_b2
        aw = jax.nn.softmax(aw, axis=1)
        cc = jnp.sum(eh * aw, axis=1)
        kp = _gelu(_ln(cc @ kg_W1 + kg_b1, kg_ln_g, kg_ln_b)) @ kg_W2 + kg_b2
        kernels = jax.nn.softmax(kp.reshape(B, H, K1 * K2), axis=-1)
        kernels = kernels.reshape(B * H, 1, K1, K2)
        mask = causal_mask[None, None]
        attn0 = jnp.where(mask, 0.0, attn).reshape(1, B * H, T, T)
        attn = lax.conv_general_dilated(attn0, kernels, window_strides=(1, 1), padding=((K1 // 2, K1 // 2), (K2 // 2, K2 // 2)), feature_group_count=B * H, dimension_numbers=('NCHW', 'OIHW', 'NCHW')).reshape(B, H, T, T)
        attn = jnp.where(mask, -jnp.inf, attn)
        p = jax.nn.softmax(attn, axis=-1)
        out = jnp.einsum('bhqk,bhkd->bhqd', p, v)
        out = out.transpose(0, 2, 1, 3).reshape(B, T, D)
        return out @ proj_W + proj_b

    def _L0_ffn_ref(z, norm_w, w_macro, w_micro, w1, w2):
        import jax, jax.numpy as jnp
        import numpy as np
        LOOPS = 2
        NUM_GROUPS = 4
        EXPERTS_PER_GROUP = 2
        NUM_EXPERTS = NUM_GROUPS * EXPERTS_PER_GROUP
        GROUPS_TOP_K = 2
        TOP_K = 1
        RMS_EPS = 1e-06
        EPS = 1e-09

        def _rmsnorm(x, w):
            return x * jax.lax.rsqrt(jnp.mean(x * x, axis=-1, keepdims=True) + RMS_EPS) * w

        def _combine_weights(x_flat, w_macro, w_micro):
            T = x_flat.shape[0]
            macro = jax.nn.softmax(x_flat @ w_macro.T, axis=-1)
            mvals, midx = jax.lax.top_k(macro, GROUPS_TOP_K)
            mvals = mvals / (jnp.sum(mvals, axis=-1, keepdims=True) + EPS)
            micro = jax.nn.softmax(jnp.einsum('td,ged->tge', x_flat, w_micro), axis=-1)
            uvals, uidx = jax.lax.top_k(micro, TOP_K)
            uvals = uvals / (jnp.sum(uvals, axis=-1, keepdims=True) + EPS)
            tok = jnp.arange(T)
            combine = jnp.zeros((T, NUM_EXPERTS), x_flat.dtype)
            for s in range(GROUPS_TOP_K):
                g = midx[:, s]
                wg = mvals[:, s:s + 1]
                li = uidx[tok, g]
                lv = uvals[tok, g]
                eidx = g[:, None] * EXPERTS_PER_GROUP + li
                combine = combine.at[tok[:, None], eidx].add(lv * wg)
            return combine
        B, S, D = z.shape
        T = B * S
        for _ in range(LOOPS):
            zn = _rmsnorm(z, norm_w)
            x = zn.reshape(T, D)
            combine = _combine_weights(x, w_macro, w_micro)
            h = jax.nn.silu(jnp.einsum('td,efd->tef', x, w1))
            y = jnp.einsum('tef,edf->ted', h, w2)
            mixed = jnp.einsum('ted,te->td', y, combine)
            z = z + mixed.reshape(B, S, D)
        return z
    x = x + _L0_xattn_ref(_layernorm(x, axis=-1), ctx_1024, L0_xattn_Wq, L0_xattn_Wk, L0_xattn_Wv, L0_xattn_hist_W, L0_xattn_hist_b, L0_xattn_hist_ln_g, L0_xattn_hist_ln_b, L0_xattn_ctx_W1, L0_xattn_ctx_b1, L0_xattn_ctx_W2, L0_xattn_ctx_b2, L0_xattn_kg_W1, L0_xattn_kg_b1, L0_xattn_kg_ln_g, L0_xattn_kg_ln_b, L0_xattn_kg_W2, L0_xattn_kg_b2, L0_xattn_proj_W, L0_xattn_proj_b, mask_SxS_bc0)
    x = x + _L0_ffn_ref(_layernorm(x, axis=-1), L0_ffn_norm_w, L0_ffn_w_macro, L0_ffn_w_micro, L0_ffn_w1, L0_ffn_w2)
    return x

_drawn_inputs = setup_inputs


def setup_inputs(seed=0):
    import zlib

    import numpy as np

    out = dict(_drawn_inputs(seed))
    spreads = {'L0_xattn_hist_b': (0.0, 0.571),
     'L0_xattn_hist_ln_g': (1.0, 0.6),
     'L0_xattn_hist_ln_b': (0.0, 1.257),
     'L0_xattn_ctx_b1': (0.0, 2.0),
     'L0_xattn_kg_b1': (0.0, 0.98),
     'L0_xattn_kg_ln_g': (1.0, 0.6),
     'L0_xattn_kg_ln_b': (0.0, 0.8),
     'L0_xattn_kg_b2': (0.0, 0.429),
     'L0_xattn_proj_b': (0.0, 0.1),
     'L0_ffn_norm_w': (1.0, 0.2)}
    factors = {'L0_xattn_ctx_W1': 3.838, 'L0_xattn_ctx_W2': 4.291}
    for name, (base, spread) in spreads.items():
        noise = np.random.default_rng([zlib.crc32(name.encode()), seed]).standard_normal(out[name].shape)
        drawn = base * np.exp(spread * noise) if base else spread * noise
        out[name] = jnp.asarray(drawn.astype(out[name].dtype))
    for name, factor in factors.items():
        out[name] = (out[name] * factor).astype(out[name].dtype)
    return out
```

```python
from contextlib import ExitStack

import concourse.bass as bass
from concourse import mybir

ALU = mybir.AluOpType
ACT = mybir.ActivationFunctionType
F32 = mybir.dt.float32
F32R = mybir.dt.float32r
BF16 = mybir.dt.bfloat16
X = mybir.AxisListType.X

P = 128
B, T, D = 2, 1024, 256
H, HD = 16, 16
DC = D // P
NT = B * T // P
TB = T // P
LPAD, RPAD = 3, 1
W = LPAD + T + RPAD
TAPS = 9
S2, CW = 77, 512
NCT = 4
UH = 8
NU = 2 * B
GH = 4
NG = NU * UH // GH
QB = 512
NQB = T // QB
VW = HD + 1
KROWS = 3 * HD
MROW = 2 * KROWS
BIG = 1.0e30
E, F, GROUPS = 8, 512, 4
FC = F // P
NB = B * T // QB
LOOPS = 2
LN_EPS, RMS_EPS, TOP_EPS = 1e-5, 1e-6, 1e-9

VEC = {}
_at = 0
for _name, _n in (("proj_b", D), ("norm_w", D), ("hist_b", CW), ("hist_g", CW), ("hist_beta", CW),
                  ("ctx_b1", CW // 4), ("ctx_W2", CW // 4), ("ctx_b2", 1), ("kg_b1", D), ("kg_g", D),
                  ("kg_beta", D), ("kg_b2", H * TAPS)):
    VEC[_name] = (_at, _at + _n)
    _at += _n
NVEC = _at
NKEEP = VEC["norm_w"][1]


class Steps:

    def __init__(self, engine, sem):
        self.engine, self.sem, self.n = engine, sem, 0

    def mark(self, ins):
        ins.then_inc(self.sem, 1)
        self.n += 1
        return self.n

    def link(self, ins):
        self.mark(ins)
        self.engine.wait_ge(self.sem, self.n)


def qblock_items():
    return [(qb, kt) for qb in range(NQB) for kt in range((qb + 1) * QB // P)]


ITEMS = qblock_items()
NI = len(ITEMS)
HALF_SLOTS = 5
FIRST_MAX, LAST_MAX = 2, NI - 3
CHUNKS = [(h, qt, c) for h in range(GH) for qt in range(TB) for c in range((qt * P) // QB + 1)]


def chunk_column(qt, c):
    return qt if c == 0 else TB + qt - QB // P


def load_keys(sp, K, ks_d, u, h, slot, loaded):
    r = HD * h
    for part in range(2):
        base = ks_d[part, u, r:r + HD, LPAD - 1:LPAD - 1 + T]
        src = bass.AP(base.tensor, base.offset, [[W, HD], [1, 3], [1, T]])
        sp.dma_start(K[part * KROWS:(part + 1) * KROWS, slot, :].bitcast(F32), src).then_inc(loaded, 16)


def build(nc, x, ctxT, hist_W, ctx_W1, kg_W1, kg_W2, Wq, Wk, Wv, proj_W, vecs, wrT, w1T, w2T, mask, out,
          debug=None):
    kern_d = nc.dram_tensor("kern_scratch", (B, H * TAPS), F32, kind="Internal").ap()
    qs_d = nc.dram_tensor("q_parts_scratch", (2, NU, P, 3, T), F32, kind="Internal").ap()
    ks_d = nc.dram_tensor("k_parts_scratch", (2, NU, P, W), F32, kind="Internal").ap()
    ao_d = nc.dram_tensor("attn_scratch", (B * T, D), F32, kind="Internal").ap()
    qk_d = nc.dram_tensor("general_qk_scratch", (2, NU * P, W), F32, kind="Internal").ap()
    v_d = nc.dram_tensor("general_v_scratch", (B * H, P, TB, HD), F32, kind="Internal").ap()
    oh_d = nc.dram_tensor("general_out_scratch", (B * H, P, TB, HD), F32, kind="Internal").ap()
    x1_d = nc.dram_tensor("residual_scratch", (B * T, D), F32, kind="Internal").ap()

    with ExitStack() as whole:
        def sem(name):
            return whole.enter_context(nc.semaphore(name))

        def keep(name, shape, dt=F32):
            return whole.enter_context(nc.sbuf_tensor(name, shape, dt))

        ident = keep("ident", [P, P])
        vkeep = keep("vkeep", [P, NKEEP])
        ones = keep("ones", [P, 1])
        const_ready = sem("const_ready")
        vkeep_in = sem("vkeep_in")

        with ExitStack() as two:
            def sb2(name, shape, dt=F32):
                return two.enter_context(nc.sbuf_tensor(name, shape, dt))

            qT = sb2("qT", [P, NU, W])
            kT = sb2("kT", [P, NU, W])
            vaug = sb2("vaug", [P, NT * H * VW + 32])
            vaug_t = vaug[:, 0:NT * H * VW].rearrange("p (t h e) -> p t h e", t=NT, h=H)
            mask_flag = sb2("mask_flag", [1, 1], mybir.dt.int32)
            kerP = sb2("kerP", [P, NU, TAPS])
            identb = sb2("identb", [P, P], BF16)
            mask_q = sb2("mask_q", [P, P + 2], BF16)
            mask_k = sb2("mask_k", [P, P + 2], BF16)
            first_neg = sb2("first_neg", [P, 1])
            sumsel = sb2("sumsel", [P, UH])
            khi, klo = (sb2(n, [P, W], F32R) for n in ("khi", "klo"))
            K = sb2("K", [MROW + 1, 2 * GH, T], F32R)
            consts = (identb, mask_q, mask_k, first_neg, sumsel)
            block1(nc, sem, ident, ones, vkeep, const_ready, vkeep_in, qT, kT, vaug, vaug_t, kerP,
                   consts, khi, klo, K, ks_d, kern_d, x, ctxT, hist_W, ctx_W1, kg_W1, kg_W2, Wq, Wk, Wv, vecs, mask, mask_flag)
            if debug and debug("b1", locals()):
                return
            other_mask = nc.values_load(mask_flag[0:1, 0:1], min_val=0, max_val=P)
            with nc.If(other_mask > 0):
                general_attention(nc, sem, ident, qT, kT, vaug_t, mask, kern_d, qk_d, v_d, oh_d, ao_d)
            with nc.Else():
                block2(nc, sem, ident, qT, kT, vaug, vaug_t, kerP, consts, khi, klo, K, qs_d, ks_d, ao_d)
        if debug and debug("b2", locals()):
            return
        block3(nc, sem, ident, vkeep, x, ao_d, x1_d, proj_W, wrT, w1T, w2T, out)

def block1(nc, sem, ident, ones, vkeep, const_ready, vkeep_in, qT, kT, vaug, vaug_t, kerP,
           consts, khi, klo, K, ks_d, kern_d, x, ctxT, hist_W, ctx_W1, kg_W1, kg_W2, Wq, Wk, Wv, vecs, mask, mask_flag):
    identb, mask_q, mask_k, first_neg, sumsel = consts
    with ExitStack() as ctx:
        def sb(name, shape, dt=F32):
            return ctx.enter_context(nc.sbuf_tensor(name, shape, dt))

        x_sb = sb("x_sb", [P, NT, D])
        xnT = sb("xnT", [P, DC, NT * P])
        ctx_sb = sb("ctx_sb", [P, DC, NCT * S2])
        hist_w = sb("hist_w", [P, DC, CW])
        ctx_w1 = sb("ctx_w1", [P, CW // P, CW // 4])
        kg_w1 = sb("kg_w1", [P, CW // P, D])
        kg_w2 = sb("kg_w2", [P, DC, H * TAPS])
        wq, wk, wv = (sb(n, [P, DC, D]) for n in ("wq", "wk", "wv"))
        vrow = sb("vrow", [P, NVEC])
        stats = sb("stats", [P, 6])
        mv = sb("mv", [P, NT, 2])
        rstd = sb("rstd", [P, NT])
        tmpn = sb("tmpn", [P, NT])
        eh = sb("eh", [S2, NCT, CW])
        estats = sb("estats", [S2, 6])
        emv = sb("emv", [S2, NCT, 2])
        erstd = sb("erstd", [S2, NCT])
        ehT = sb("ehT", [P, NCT, CW // P, S2])
        ag = sb("ag", [S2, NCT, CW // 4])
        awc = sb("awc", [S2, NCT])
        awr = sb("awr", [1, B, 2 * S2])
        aws = sb("aws", [1, 4 * B])
        ccT = sb("ccT", [P, CW // P, B])
        kg = sb("kg", [B, D])
        kstats = sb("kstats", [B, 8])
        kgT = sb("kgT", [P, DC, B])
        kp = sb("kp", [B, H, TAPS])
        ks = sb("ks", [B, 2 * H])
        mask_words = sb("mask_words", [P, TB, T // 4], mybir.dt.int32)
        causal = sb("causal", [P, 2 * T], BF16)
        differs = sb("differs", [P, T], BF16)
        diff_max = sb("diff_max", [P, TB + 1])
        banks = [ctx.enter_context(nc.psum_tensor(f"work{i}", [P, 512], F32)) for i in range(4)]
        cbank = [ctx.enter_context(nc.psum_tensor(f"ctxb{i}", [P, 512], F32)) for i in range(4)]

        dve_steps, pool_steps = sem("dve_steps"), sem("pool_steps")
        x_in = [sem(f"x_in{i}") for i in range(4)]
        hist_in, cw_in, qkv_in, vrow_in = sem("hist_in"), sem("cw_in"), sem("qkv_in"), sem("vrow_in")
        pads_ready = sem("pads_ready")
        mask_in, causal_ready, diff_ready, flag_ready = (sem(n) for n in (
            "mask_in", "causal_ready", "diff_ready", "flag_ready"))
        xvar_ready, xstd_ready, xn_ready = sem("xvar_ready"), sem("xstd_ready"), sem("xn_ready")
        work_full, work_free = sem("work_full"), sem("work_free")
        ctx_pe, ctx_dve, ctx_act = sem("ctx_pe"), sem("ctx_dve"), sem("ctx_act")
        kern_out, kern_in = sem("kern_out"), sem("kern_in")
        khilo_ready, k_out, k0_in = sem("khilo_ready1"), sem("k_out1"), sem("k0_in")

        ring = [("xT", c, n) for n in range(4) for c in range(DC)]
        ring += [("qk", which, u, blk) for u in range(NU) for which in range(2) for blk in range(2)]
        ring += [("v", t) for t in range(NT)]
        before_keys = ring.index(("qk", 1, 0, 1)) + 1
        before = [0, 12, 16, 20, 24, 28, 32, 36]

        block = ctx.enter_context(nc.Block())

        def vec(name, rows):
            a, b = VEC[name]
            return vrow[0:rows, a:b]

        @block.sync
        def _(sp):
            sp.dma_start(ctx_sb[:], ctxT.rearrange("(c p) s -> p c s", p=P)).then_inc(hist_in, 16)
            sp.dma_start(hist_w[:], hist_W.rearrange("(c p) n -> p c n", p=P)).then_inc(hist_in, 16)
            for n in range(4):
                src = x[n * 512:(n + 1) * 512, :].rearrange("(t p) d -> p t d", p=P)
                sp.dma_start(x_sb[:, 4 * n:4 * n + 4, :], src).then_inc(x_in[n], 16)
            sp.dma_start(vrow[:], vecs.partition_broadcast(P)).then_inc(vrow_in, 16)
            for w, dram in ((wq, Wq), (wk, Wk), (wv, Wv)):
                sp.dma_start(w[:], dram.rearrange("(c p) n -> p c n", p=P)).then_inc(qkv_in, 16)
            for w, dram in ((ctx_w1, ctx_W1), (kg_w1, kg_W1), (kg_w2, kg_W2)):
                sp.dma_start(w[:], dram.rearrange("(c p) n -> p c n", p=P)).then_inc(cw_in, 16)
            sp.dma_start(mask_words[:], mask.rearrange("(t p) k -> p t k", p=P)).then_inc(mask_in, 16)
            sp.wait_ge(khilo_ready, 2)
            for part, t in enumerate((khi, klo)):
                sp.dma_start(ks_d[part, 0], t[:].bitcast(F32)).then_inc(k_out, 16)
            sp.wait_ge(k_out, 32)
            for h in range(UH):
                load_keys(sp, K, ks_d, 0, h, h, k0_in)
            sp.wait_ge(ctx_dve, 12)
            sp.dma_start(kern_d, kp[:].rearrange("b h t -> b (h t)")).then_inc(kern_out, 16)
            sp.wait_ge(kern_out, 16)
            for u in range(NU):
                b, half = divmod(u, 2)
                row = kern_d[b:b + 1, half * UH * TAPS:(half + 1) * UH * TAPS]
                src = bass.AP(row.tensor, row.offset, [[TAPS, UH], [0, HD], [1, TAPS]])
                sp.dma_start(kerP[:, u, :], src).then_inc(kern_in, 16)
            sp.wait_ge(kern_in, 16 * NU)
            sp.wait_ge(k0_in, 16 * 2 * UH)

        @block.gpsimd
        def _(pool):
            nc.gpsimd.memset(ident[:], 0.0).then_inc(pool_steps, 1)
            pool.wait_ge(pool_steps, 1)
            nc.gpsimd.affine_select(out=ident[:], in_=ident[:], compare_op=ALU.not_equal, fill=1.0, base=0,
                                    pattern=[[-1, P]], channel_multiplier=1).then_inc(const_ready, 1)
            nc.gpsimd.memset(ones[:], 1.0).then_inc(const_ready, 1)
            nc.gpsimd.memset(vaug[:], 1.0).then_inc(pads_ready, 1)
            for t in (qT, kT):
                nc.gpsimd.memset(t[:, :, 0:LPAD], 0.0).then_inc(pads_ready, 1)
                nc.gpsimd.memset(t[:, :, LPAD + T:W], 0.0).then_inc(pads_ready, 1)
            nc.gpsimd.memset(causal[:], 0.0).then_inc(pool_steps, 1)
            pool.wait_ge(pool_steps, 2)
            nc.gpsimd.affine_select(out=causal[:], in_=causal[:], compare_op=ALU.is_ge, fill=1.0, base=T,
                                    pattern=[[-1, 2 * T]], channel_multiplier=1).then_inc(causal_ready, 1)
            s = Steps(pool, pool_steps)
            s.n = 2
            pool.wait_ge(const_ready, 1)
            nc.gpsimd.tensor_copy(identb[:], ident[:])
            for m in (mask_q, mask_k, first_neg, sumsel):
                s.mark(nc.gpsimd.memset(m[:], 1.0 if m is sumsel else 0.0))
            pool.wait_ge(pool_steps, s.n)
            nc.gpsimd.affine_select(out=mask_q[:], in_=mask_q[:], compare_op=ALU.is_ge, fill=-BIG, base=0,
                                    pattern=[[-1, P + 2]], channel_multiplier=1)
            nc.gpsimd.affine_select(out=mask_k[:], in_=mask_k[:], compare_op=ALU.is_ge, fill=-BIG, base=-2,
                                    pattern=[[1, P + 2]], channel_multiplier=-1)
            nc.gpsimd.affine_select(out=first_neg[:], in_=first_neg[:], compare_op=ALU.is_ge, fill=-BIG, base=-1,
                                    pattern=[[0, 1]], channel_multiplier=1)
            s.link(nc.gpsimd.affine_select(out=sumsel[:], in_=sumsel[:], compare_op=ALU.is_ge, fill=0.0, base=0,
                                           pattern=[[-HD, UH]], channel_multiplier=1))
            s.link(nc.gpsimd.affine_select(out=sumsel[:], in_=sumsel[:], compare_op=ALU.is_ge, fill=0.0, base=HD - 1,
                                    pattern=[[HD, UH]], channel_multiplier=-1))
            for h in range(0, 2 * GH, GH):
                s.link(nc.gpsimd.memset(K[MROW:MROW + 1, h:h + GH, :].bitcast(F32), 1.0))
            pool.wait_ge(work_free, before_keys)
            pool.wait_ge(pads_ready, 5)
            nc.gpsimd.tensor_copy(khi[:], kT[:, 0, :]).then_inc(khilo_ready, 1)
            pool.wait_ge(khilo_ready, 1)
            nc.gpsimd.tensor_tensor(klo[:], kT[:, 0, :], khi[:].bitcast(F32), ALU.subtract).then_inc(khilo_ready, 1)

        @block.tensor
        def _(pe):
            pe.wait_ge(const_ready, 2)
            done = [0]

            def take():
                i = done[0]
                done[0] += 1
                bank = banks[i % 4]
                item = ring[i]
                if i >= 4:
                    pe.wait_ge(work_free, i - 3)
                if item[0] == "xT":
                    _, c, n = item
                    pe.wait_ge(xn_ready, 4 * n + 4)
                    for k in range(4):
                        last = nc.tensor.transpose(bank[:, k * P:(k + 1) * P],
                                                   x_sb[:, 4 * n + k, c * P:(c + 1) * P], ident[:])
                elif item[0] == "qk":
                    _, which, u, blk = item
                    b, half = divmod(u, 2)
                    if i == 8:
                        pe.wait_ge(qkv_in, 48)
                        pe.wait_ge(work_free, 8)
                    t0 = b * T + blk * QB
                    for c in range(DC):
                        last = nc.tensor.matmul(bank[:], (wq, wk)[which][:, c, half * P:(half + 1) * P],
                                                xnT[:, c, t0:t0 + QB], start=(c == 0), stop=(c == DC - 1))
                else:
                    t = item[1]
                    for c in range(DC):
                        last = nc.tensor.matmul(bank[:, 0:D], xnT[:, c, t * P:(t + 1) * P], wv[:, c, :],
                                                start=(c == 0), stop=(c == DC - 1))
                last.then_inc(work_full, 1)

            def ring_to(n):
                while done[0] < n:
                    take()

            pe.wait_ge(hist_in, 32)
            for t in range(NCT):
                for c in range(DC):
                    last = nc.tensor.matmul(cbank[t][0:S2, :], ctx_sb[:, c, t * S2:(t + 1) * S2],
                                            hist_w[:, c, :], start=(c == 0), stop=(c == DC - 1))
            last.then_inc(ctx_pe, 1)
            ring_to(before[1])
            pe.wait_ge(ctx_act, 2)
            for t in range(NCT):
                for c in range(CW // P):
                    last = nc.tensor.transpose(cbank[t][:, c * S2:(c + 1) * S2], eh[:, t, c * P:(c + 1) * P],
                                               ident[0:S2, 0:S2])
            last.then_inc(ctx_pe, 1)
            ring_to(before[2])
            pe.wait_ge(ctx_dve, 3)
            pe.wait_ge(cw_in, 48)
            for t in range(NCT):
                for c in range(CW // P):
                    last = nc.tensor.matmul(cbank[0][0:S2, t * P:(t + 1) * P], ehT[:, t, c, :],
                                            ctx_w1[:, c, :], start=(c == 0), stop=(c == CW // P - 1))
            last.then_inc(ctx_pe, 1)
            ring_to(before[3])
            pe.wait_ge(ctx_dve, 5)
            for t in range(NCT):
                last = nc.tensor.matmul(cbank[1][0:1, t * S2:(t + 1) * S2], awc[:, t:t + 1],
                                        ident[0:S2, 0:S2], start=True, stop=True)
            last.then_inc(ctx_pe, 1)
            ring_to(before[4])
            pe.wait_ge(diff_ready, 1)
            nc.tensor.matmul(cbank[0][0:1, 0:1], diff_max[:, TB:TB + 1], ones[:], start=True,
                             stop=True).then_inc(flag_ready, 1)
            pe.wait_ge(ctx_dve, 7)
            for t in range(NCT):
                b, part = divmod(t, 2)
                last = nc.tensor.matmul(cbank[2][0:S2, t:t + 1], awr[0:1, b, part * S2:(part + 1) * S2],
                                        ones[0:1, 0:1], start=True, stop=True)
            last.then_inc(ctx_pe, 1)
            pe.wait_ge(ctx_dve, 8)
            for c in range(CW // P):
                for t in range(NCT):
                    b, part = divmod(t, 2)
                    last = nc.tensor.matmul(cbank[3][:, c * B + b:c * B + b + 1], eh[:, t, c * P:(c + 1) * P],
                                            awc[:, t:t + 1], start=(part == 0), stop=(part == 1))
            last.then_inc(ctx_pe, 1)
            ring_to(before[5])
            pe.wait_ge(flag_ready, 2)
            pe.wait_ge(ctx_act, 5)
            for c in range(CW // P):
                last = nc.tensor.matmul(cbank[0][0:B, 0:D], ccT[:, c, :], kg_w1[:, c, :],
                                        start=(c == 0), stop=(c == CW // P - 1))
            last.then_inc(ctx_pe, 1)
            ring_to(before[6])
            pe.wait_ge(ctx_act, 7)
            for c in range(DC):
                last = nc.tensor.transpose(cbank[1][:, c * B:(c + 1) * B], kg[:, c * P:(c + 1) * P],
                                           ident[0:B, 0:B])
            last.then_inc(ctx_pe, 1)
            pe.wait_ge(ctx_act, 8)
            for c in range(DC):
                last = nc.tensor.matmul(cbank[2][0:B, 0:H * TAPS], kgT[:, c, :], kg_w2[:, c, :],
                                        start=(c == 0), stop=(c == DC - 1))
            last.then_inc(ctx_pe, 1)
            ring_to(len(ring))

        @block.scalar
        def _(act):
            done = [0]

            def take():
                i = done[0]
                done[0] += 1
                bank, item = banks[i % 4], ring[i]
                act.wait_ge(work_full, i + 1)
                if item[0] == "xT":
                    _, c, n = item
                    ins = nc.scalar.copy(xnT[:, c, n * 512:(n + 1) * 512], bank[:])
                elif item[0] == "qk":
                    _, which, u, blk = item
                    if i == 8:
                        act.wait_ge(pads_ready, 5)
                    dst = (qT, kT)[which][:, u, LPAD + blk * QB:LPAD + (blk + 1) * QB]
                    ins = nc.scalar.mul(dst, bank[:], HD ** -0.5 if which == 0 else 1.0)
                else:
                    t = item[1]
                    ins = nc.scalar.copy(vaug_t[:, t, :, 0:HD], bank[:, 0:D].rearrange("p (h d) -> p h d", d=HD))
                ins.then_inc(work_free, 1)

            def ring_to(n):
                while done[0] < n:
                    take()

            act.wait_ge(xvar_ready, 1)
            nc.scalar.activation(rstd[:], tmpn[:], ACT.Sqrt).then_inc(xstd_ready, 1)
            act.wait_ge(ctx_dve, 1)
            nc.scalar.activation(erstd[:], erstd[:], ACT.Sqrt).then_inc(ctx_act, 1)
            ring_to(8)
            act.wait_ge(ctx_dve, 2)
            nc.scalar.activation(eh[:], eh[:], ACT.Gelu).then_inc(ctx_act, 1)
            ring_to(before[2] + 2)
            act.wait_ge(ctx_dve, 4)
            nc.scalar.activation(ag[:], ag[:], ACT.Gelu).then_inc(ctx_act, 1)
            ring_to(before[3] + 2)
            act.wait_ge(ctx_dve, 6)
            nc.scalar.activation(awr[:], awr[:], ACT.Exp).then_inc(ctx_act, 1)
            ring_to(before[4])
            act.wait_ge(ctx_pe, 6)
            nc.scalar.copy(ccT[:], cbank[3][:, 0:CW // P * B].rearrange("p (c b) -> p c b", b=B)).then_inc(ctx_act, 1)
            ring_to(before[5])
            act.wait_ge(ctx_dve, 9)
            nc.scalar.activation(kstats[:, 7:8], kstats[:, 7:8], ACT.Sqrt).then_inc(ctx_act, 1)
            act.wait_ge(ctx_dve, 10)
            nc.scalar.activation(kg[:], kg[:], ACT.Gelu).then_inc(ctx_act, 1)
            ring_to(before[6])
            act.wait_ge(ctx_pe, 8)
            nc.scalar.copy(kgT[:], cbank[1][:, 0:DC * B].rearrange("p (c b) -> p c b", b=B)).then_inc(ctx_act, 1)
            act.wait_ge(ctx_dve, 11)
            nc.scalar.activation(kp[:], kp[:], ACT.Exp).then_inc(ctx_act, 1)
            ring_to(len(ring))

        @block.vector
        def _(dve):
            s = Steps(dve, dve_steps)

            def compare_mask(a, b_):
                for t in range(a, b_):
                    if t == 0:
                        dve.wait_ge(mask_in, 16)
                        dve.wait_ge(causal_ready, 1)
                    s.link(nc.vector.tensor_tensor(differs[:], mask_words[:, t, :].bitcast(mybir.dt.uint8), causal[:, T - t * P:2 * T - t * P],
                                                   ALU.not_equal))
                    s.link(nc.vector.tensor_reduce(diff_max[:, t:t + 1], differs[:], X, ALU.max))

            for t in range(NT):
                if t % 4 == 0:
                    dve.wait_ge(x_in[t // 4], 16)
                s.link(nc.vector.bn_stats(stats[:], x_sb[:, t, :]))
                s.link(nc.vector.bn_aggr(mv[:, t, :], stats[:]))
            nc.vector.tensor_scalar(tmpn[:], mv[:, :, 1], LN_EPS, None, ALU.add).then_inc(xvar_ready, 1)
            dve.wait_ge(xstd_ready, 1)
            s.link(nc.vector.reciprocal(rstd[:], rstd[:]))
            newton(nc, s, rstd[:], tmpn[:])
            for t in range(NT):
                nc.vector.tensor_scalar(x_sb[:, t, :], x_sb[:, t, :], mv[:, t, 0:1], rstd[:, t:t + 1],
                                        ALU.subtract, ALU.mult).then_inc(xn_ready, 1)
            dve.wait_ge(ctx_pe, 1)
            dve.wait_ge(vrow_in, 16)
            for t in range(NCT):
                s.mark(nc.vector.tensor_tensor(eh[:, t, :], cbank[t][0:S2, :], vec("hist_b", S2), ALU.add))
            for t in range(NCT):
                dve.wait_ge(dve_steps, s.n)
                s.link(nc.vector.bn_stats(estats[:], eh[:, t, :]))
                s.link(nc.vector.bn_aggr(emv[:, t, :], estats[:]))
            s.link(nc.vector.tensor_scalar(emv[:, :, 1], emv[:, :, 1], LN_EPS, None, ALU.add))
            nc.vector.tensor_copy(erstd[:], emv[:, :, 1]).then_inc(ctx_dve, 1)
            dve.wait_ge(ctx_act, 1)
            s.link(nc.vector.reciprocal(erstd[:], erstd[:]))
            newton(nc, s, erstd[:], emv[:, :, 1])
            for t in range(NCT):
                s.mark(nc.vector.tensor_scalar(eh[:, t, :], eh[:, t, :], emv[:, t, 0:1], erstd[:, t:t + 1],
                                               ALU.subtract, ALU.mult))
            dve.wait_ge(dve_steps, s.n)
            for t in range(NCT):
                s.mark(nc.vector.tensor_tensor(eh[:, t, :], eh[:, t, :], vec("hist_g", S2), ALU.mult))
            dve.wait_ge(dve_steps, s.n)
            for t in range(NCT):
                last = nc.vector.tensor_tensor(eh[:, t, :], eh[:, t, :], vec("hist_beta", S2), ALU.add)
                s.mark(last) if t < NCT - 1 else last.then_inc(ctx_dve, 1)
            compare_mask(0, 4)
            dve.wait_ge(ctx_pe, 2)
            for t in range(NCT):
                last = nc.vector.tensor_copy(ehT[:, t, :, :].rearrange("p c s -> p (c s)"), cbank[t][:, 0:CW // P * S2])
                s.mark(last) if t < NCT - 1 else last.then_inc(ctx_dve, 1)
            dve.wait_ge(ctx_pe, 3)
            b1 = vec("ctx_b1", S2).unsqueeze(1).to_broadcast([S2, NCT, CW // 4])
            nc.vector.tensor_tensor(ag[:], cbank[0][0:S2, :].rearrange("p (t n) -> p t n", t=NCT), b1,
                                    ALU.add).then_inc(ctx_dve, 1)
            compare_mask(4, TB)
            nc.vector.tensor_reduce(diff_max[:, TB:TB + 1], diff_max[:, 0:TB], X, ALU.max).then_inc(diff_ready, 1)
            dve.wait_ge(ctx_act, 3)
            w2 = vec("ctx_W2", S2).unsqueeze(1).to_broadcast([S2, NCT, CW // 4])
            s.link(nc.vector.tensor_tensor(ag[:], ag[:], w2, ALU.mult))
            s.link(nc.vector.tensor_reduce(awc[:], ag[:], X, ALU.add))
            nc.vector.tensor_scalar(awc[:], awc[:], vec("ctx_b2", S2), None, ALU.add).then_inc(ctx_dve, 1)
            dve.wait_ge(ctx_pe, 4)
            scores = cbank[1][0:1, 0:NCT * S2].rearrange("p (b s) -> p b s", b=B)
            s.link(nc.vector.tensor_reduce(aws[:, 0:B], scores, X, ALU.max))
            nc.vector.tensor_tensor(awr[:], scores, aws[:, 0:B].unsqueeze(2).to_broadcast([1, B, 2 * S2]),
                                    ALU.subtract).then_inc(ctx_dve, 1)
            dve.wait_ge(flag_ready, 1)
            nc.vector.tensor_copy(mask_flag[:], cbank[0][0:1, 0:1]).then_inc(flag_ready, 1)
            dve.wait_ge(ctx_act, 4)
            s.link(nc.vector.tensor_reduce(aws[:, B:2 * B], awr[:], X, ALU.add))
            s.link(nc.vector.reciprocal(aws[:, 2 * B:3 * B], aws[:, B:2 * B]))
            nc.vector.tensor_tensor(awr[:], awr[:], aws[:, 2 * B:3 * B].unsqueeze(2).to_broadcast([1, B, 2 * S2]),
                                    ALU.mult).then_inc(ctx_dve, 1)
            dve.wait_ge(ctx_pe, 5)
            nc.vector.tensor_copy(awc[:], cbank[2][0:S2, 0:NCT]).then_inc(ctx_dve, 1)
            dve.wait_ge(ctx_pe, 7)
            s.link(nc.vector.tensor_tensor(kg[:], cbank[0][0:B, 0:D], vec("kg_b1", B), ALU.add))
            s.link(nc.vector.bn_stats(kstats[:, 0:6], kg[:]))
            s.link(nc.vector.bn_aggr(ks[:, 0:2], kstats[:, 0:6]))
            s.link(nc.vector.tensor_scalar(ks[:, 1:2], ks[:, 1:2], LN_EPS, None, ALU.add))
            nc.vector.tensor_copy(kstats[:, 7:8], ks[:, 1:2]).then_inc(ctx_dve, 1)
            dve.wait_ge(ctx_act, 6)
            s.link(nc.vector.reciprocal(kstats[:, 7:8], kstats[:, 7:8]))
            newton(nc, s, kstats[:, 7:8], ks[:, 1:2])
            s.link(nc.vector.tensor_scalar(kg[:], kg[:], ks[:, 0:1], kstats[:, 7:8], ALU.subtract, ALU.mult))
            s.link(nc.vector.tensor_tensor(kg[:], kg[:], vec("kg_g", B), ALU.mult))
            nc.vector.tensor_tensor(kg[:], kg[:], vec("kg_beta", B), ALU.add).then_inc(ctx_dve, 1)
            dve.wait_ge(ctx_pe, 9)
            kpf = kp[:].rearrange("b h t -> b (h t)")
            s.link(nc.vector.tensor_tensor(kpf, cbank[2][0:B, 0:H * TAPS], vec("kg_b2", B), ALU.add))
            s.link(nc.vector.tensor_reduce(ks[:, 0:H], kp[:], X, ALU.max))
            nc.vector.tensor_tensor(kp[:], kp[:], ks[:, 0:H].unsqueeze(2).to_broadcast([B, H, TAPS]),
                                    ALU.subtract).then_inc(ctx_dve, 1)
            dve.wait_ge(ctx_act, 9)
            s.link(nc.vector.tensor_reduce(ks[:, 0:H], kp[:], X, ALU.add))
            s.link(nc.vector.reciprocal(ks[:, H:2 * H], ks[:, 0:H]))
            nc.vector.tensor_tensor(kp[:], kp[:], ks[:, H:2 * H].unsqueeze(2).to_broadcast([B, H, TAPS]),
                                    ALU.mult).then_inc(ctx_dve, 1)
            dve.wait_ge(vrow_in, 16)
            nc.vector.tensor_copy(vkeep[:], vrow[:, 0:NKEEP]).then_inc(vkeep_in, 1)


def newton(nc, s, r, v):
    with ExitStack() as c:
        t = c.enter_context(nc.sbuf_tensor(f"newton{s.n}", [r.shape[0], r.shape[1]], F32))
        s.link(nc.vector.tensor_tensor(t[:], r, r, ALU.mult))
        s.link(nc.vector.tensor_tensor(t[:], t[:], v, ALU.mult))
        s.link(nc.vector.tensor_scalar(t[:], t[:], -0.5, 1.5, ALU.mult, ALU.add))
        s.link(nc.vector.tensor_tensor(r, r, t[:], ALU.mult))

def block2(nc, sem, ident, qT, kT, vaug, vaug_t, kerP, consts, khi, klo, K, qs_d, ks_d, ao_d):
    identb, mask_q, mask_k, first_neg, sumsel = consts
    with ExitStack() as ctx:
        def sb(name, shape, dt=F32):
            return ctx.enter_context(nc.sbuf_tensor(name, shape, dt))

        Q1 = sb("Q1", [MROW + 1, 2 * GH, T], F32R)
        Q2 = sb("Q2", [MROW, 2, GH, QB], F32R)
        qf = sb("qf", [P, 3, QB])
        q1a, q2a, q2b = (sb(n, [P, QB]) for n in ("q1a", "q2a", "q2b"))
        qhi, qlo = (sb(n, [P, 3, QB], F32R) for n in ("qhi", "qlo"))
        pa = sb("pa", [P, QB])
        dprod = sb("dprod", [P, 2, T])
        d01 = sb("d01", [P, 2, TB, UH])
        mx = sb("mx", [P, GH, TB + (T - QB) // P])
        nm = sb("nm", [P, GH, TB])
        mrow = sb("mrow", [GH * TB, P])
        e01 = sb("e01", [P, 2, 2, TB, GH])
        esum = sb("esum", [P, 2, TB, GH])
        vprev = sb("vprev", [P, TB, GH, HD])
        own = sb("own", [P, 2, TB, GH, HD])
        Pt = sb("Pt", [P, 2, GH, QB])
        oT = sb("oT", [P, 2, QB])
        rl = sb("rl", [P, 4, GH])
        num = sb("num", [P, 4, GH, HD])
        ao = sb("ao", [P, 2, 4, GH, HD])

        spair = [ctx.enter_context(nc.psum_tensor(f"spair{i}", [P, 2, QB], F32)) for i in range(2)]
        ringb = [ctx.enter_context(nc.psum_tensor(f"ring{i}", [P, QB], F32)) for i in range(2)]
        pv = [ctx.enter_context(nc.psum_tensor(f"pv{i}", [P, QB], F32)) for i in range(NQB)]

        dve_steps, pool_steps = sem("dve_steps2"), sem("pool_steps2")
        taps_done = sem("taps_done")
        qhi_ready, qlo_ready = sem("qhi_ready"), sem("qlo_ready")
        khilo_ready = sem("khilo_ready")
        dprod_ready = sem("dprod_ready")
        qhi_out, qlo_out, k_out = sem("qhi_out"), sem("qlo_out"), sem("k_out")
        kq1_in = [sem(f"kq1_in{i}") for i in range(2 * GH)]
        q2_in = [sem(f"q2_in{i}") for i in range(2)]
        ring_full, ring_free = sem("ring_full"), sem("ring_free")
        nm_ready, mrow_in = sem("nm_ready"), sem("mrow_in")
        dless_ready, e01_ready = sem("dless_ready"), sem("e01_ready")
        vprev_in, own_ready = sem("vprev_in"), sem("own_ready")
        s_full, p_ready, pv_done = sem("s_full"), sem("p_ready"), sem("pv_done")
        o_ready = sem("o_ready")
        ao_ready, ao_out = sem("ao_ready"), [sem(f"ao_out{i}") for i in range(2)]

        def ucol(t, u, t0, shift):
            return t[:, u, LPAD + t0 + shift:LPAD + t0 + shift + QB]

        def stage_ring(g):
            out = []
            nxt = g + 1
            if nxt < NG:
                if nxt % 2 == 0 and g >= 0:
                    out.append((0, ("diag", nxt // 2)))
                first = FIRST_MAX if g >= 0 else 0
                per = -(-len(CHUNKS) // (LAST_MAX + 1 - FIRST_MAX)) if g >= 0 else len(CHUNKS)
                for n, c in enumerate(CHUNKS):
                    out.append((first + n // per, ("max", nxt, c)))
                if g < 0:
                    out.append((0, ("diag", nxt // 2)))
                out.append((NI if g < 0 else LAST_MAX + 1, ("turn_m", nxt)))
            if g >= 0:
                out.append((7, ("out", g, 0)))
            if g >= 1:
                out.append((3, ("out", g - 1, 1)))
            return sorted(out, key=lambda a: a[0])

        rings = {g: stage_ring(g) for g in range(-1, NG + 1)}
        rings[NG] = [(0, ("out", NG - 1, 1))]

        def stage_items(g, slot):
            return [it for s_, it in rings[g] if s_ == slot]

        flat = [it for g in range(-1, NG + 1) for s_ in range(NI + 1) for it in stage_items(g, s_)]
        ring_index = {it: n for n, it in enumerate(flat)}

        block = ctx.enter_context(nc.Block())

        @block.sync
        def _(sp):
            def write_parts(n):
                u, half = divmod(n, 2)
                t0 = half * QB
                sp.wait_ge(qhi_ready, n + 1)
                sp.dma_start(qs_d[0, u, :, :, t0:t0 + QB], qhi[:].bitcast(F32)).then_inc(qhi_out, 16)
                sp.wait_ge(qlo_ready, n + 1)
                sp.dma_start(qs_d[1, u, :, :, t0:t0 + QB], qlo[:].bitcast(F32)).then_inc(qlo_out, 16)
                if half == 0 and u:
                    sp.wait_ge(khilo_ready, 2 * u)
                    sp.dma_start(ks_d[0, u], khi[:].bitcast(F32)).then_inc(k_out, 16)
                    sp.dma_start(ks_d[1, u], klo[:].bitcast(F32)).then_inc(k_out, 16)

            def load_kq1(g):
                u, h0 = g // 2, GH * (g % 2)
                if g >= 2:
                    sp.wait_ge(pv_done, NI * (g - 1))
                    sp.wait_ge(s_full, 2 * NI * (g - 1))
                if u:
                    sp.wait_ge(k_out, 32 * u)
                sp.wait_ge(qhi_out, 32 * (u + 1))
                for h in range(GH):
                    slot, r = GH * (g % 2) + h, HD * (h0 + h)
                    if u:
                        load_keys(sp, K, ks_d, u, h0 + h, slot, kq1_in[slot])
                    for part in range(2):
                        sp.dma_start(Q1[part * KROWS:(part + 1) * KROWS, slot, :].bitcast(F32),
                                     qs_d[0, u, r:r + HD]).then_inc(kq1_in[slot], 16)

            def load_q2(g, qb):
                u, h0 = g // 2, GH * (g % 2)
                if g >= 1:
                    sp.wait_ge(s_full, 2 * (NI * (g - 1) + (QB // P if qb == 0 else NI)))
                sp.wait_ge(qlo_out, 32 * (u + 1))
                for h in range(GH):
                    r = HD * (h0 + h)
                    for part in range(2):
                        sp.dma_start(Q2[part * KROWS:(part + 1) * KROWS, qb, h, :].bitcast(F32),
                                     qs_d[1, u, r:r + HD, :, qb * QB:(qb + 1) * QB]).then_inc(q2_in[qb], 16)

            def load_vprev(g):
                b, h0 = g // 4, GH * (g % 4)
                if g >= 1:
                    sp.wait_ge(own_ready, 3 * g)
                for k in range(TB):
                    sp.dma_start(vprev[1:P, k, :, :],
                                 vaug_t[0:P - 1, b * TB + k, h0:h0 + GH, 0:HD]).then_inc(vprev_in, 16)
                    sp.dma_start(vprev[0:1, k, :, :],
                                 vaug_t[P - 1:P, b * TB + max(k - 1, 0), h0:h0 + GH, 0:HD]).then_inc(vprev_in, 16)

            def place_max(g):
                sp.wait_ge(ring_free, ring_index[("turn_m", g)] + 1)
                s0 = GH * (g % 2)
                sp.dma_start(Q1[MROW:MROW + 1, s0:s0 + GH, :].bitcast(F32), mrow[:]).then_inc(mrow_in, 16)

            def write_ao(g, qb):
                n = 2 * g + qb
                sp.wait_ge(ao_ready, n + 1)
                b, h0 = g // 4, GH * (g % 4)
                r0 = b * T + qb * QB
                dst = ao_d[r0:r0 + QB, h0 * HD:(h0 + GH) * HD].rearrange("(k p) d -> p k d", p=P)
                sp.dma_start(dst, ao[:, n % 2, :, :, :].rearrange("p k h d -> p k (h d)")).then_inc(ao_out[n % 2], 16)

            write_parts(0)
            write_parts(1)
            load_kq1(0)
            load_kq1(1)
            load_q2(0, 0)
            load_q2(0, 1)
            load_vprev(0)
            place_max(0)
            for g in range(NG):
                if g + 1 < NG and g >= 1:
                    load_kq1(g + 1)
                if g >= 1:
                    write_ao(g - 1, 1)
                if g + 1 < NG:
                    load_vprev(g + 1)
                more = g % 2 == 0 and g // 2 + 1 < NU
                if more:
                    write_parts(g + 2)
                if g + 1 < NG:
                    load_q2(g + 1, 0)
                write_ao(g, 0)
                if g + 1 < NG:
                    place_max(g + 1)
                if more:
                    write_parts(g + 3)
                if g + 1 < NG:
                    load_q2(g + 1, 1)
            write_ao(NG - 1, 1)
            for done in ao_out:
                sp.wait_ge(done, 16 * NG)

        @block.gpsimd
        def _(pool):
            s = Steps(pool, pool_steps)
            def prepare(u):
                if u:
                    if u > 1:
                        pool.wait_ge(k_out, 32 * (u - 1))
                    nc.gpsimd.tensor_copy(khi[:], kT[:, u, :]).then_inc(khilo_ready, 1)
                    pool.wait_ge(khilo_ready, 2 * u - 1)
                    nc.gpsimd.tensor_tensor(klo[:], kT[:, u, :], khi[:].bitcast(F32),
                                            ALU.subtract).then_inc(khilo_ready, 1)
                if u:
                    pool.wait_ge(ring_full, ring_index[("diag", u - 1)] + 1)
                for half in range(2):
                    t0 = half * QB
                    pool.wait_ge(taps_done, 2 * u + half + 1)
                    for kind, terms in enumerate((((qf[:, 0, :], -1), (q1a[:], 0), (q2a[:], 1)),
                                                  ((qf[:, 0, :], -2), (qf[:, 1, :], -1), (q2b[:], 0)))):
                        dp = dprod[:, kind, t0:t0 + QB]
                        s.mark(nc.gpsimd.tensor_tensor(dp, terms[0][0], ucol(kT, u, t0, terms[0][1]), ALU.mult))
                        s.link(nc.gpsimd.tensor_tensor(pa[:], terms[1][0], ucol(kT, u, t0, terms[1][1]), ALU.mult))
                        s.link(nc.gpsimd.tensor_tensor(dp, dp, pa[:], ALU.add))
                        s.link(nc.gpsimd.tensor_tensor(pa[:], terms[2][0], ucol(kT, u, t0, terms[2][1]), ALU.mult))
                        nc.gpsimd.tensor_tensor(dp, dp, pa[:], ALU.add).then_inc(dprod_ready, 1)
                        pool.wait_ge(dprod_ready, 2 * (2 * u + half) + kind + 1)

            def own_terms(g):
                b, h0, w = g // 4, GH * (g % 4), g % 2
                pool.wait_ge(e01_ready, g + 1)
                if g >= 2:
                    pool.wait_ge(ao_ready, 2 * (g - 1))
                e = [e01[:, w, k, :, :].unsqueeze(3).to_broadcast([P, TB, GH, HD]) for k in range(2)]
                nc.gpsimd.tensor_tensor(esum[:, w], e01[:, w, 0], e01[:, w, 1], ALU.add).then_inc(own_ready, 1)
                s.mark(nc.gpsimd.tensor_tensor(own[:, w], vaug_t[:, b * TB:(b + 1) * TB, h0:h0 + GH, 0:HD], e[0],
                                               ALU.mult))
                pool.wait_ge(vprev_in, 16 * 2 * TB * (g + 1))
                nc.gpsimd.tensor_tensor(vprev[:], vprev[:], e[1], ALU.mult).then_inc(own_ready, 1)
                pool.wait_ge(own_ready, 3 * g + 2)
                pool.wait_ge(pool_steps, s.n)
                nc.gpsimd.tensor_tensor(own[:, w], own[:, w], vprev[:], ALU.add).then_inc(own_ready, 1)

            prepare(0)
            own_terms(0)
            for g in range(NG):
                if g % 2 == 0 and g // 2 + 1 < NU:
                    prepare(g // 2 + 1)
                if g + 1 < NG:
                    own_terms(g + 1)

        @block.scalar
        def _(act):
            def round_q(n):
                act.wait_ge(taps_done, n + 1)
                if n:
                    act.wait_ge(qhi_out, 16 * n)
                nc.scalar.copy(qhi[:], qf[:]).then_inc(qhi_ready, 1)

            def exps(g, i, pair):
                n = g * NI + i
                qb, kt = ITEMS[i]
                off = max(0, kt * P - qb * QB)
                act.wait_ge(s_full, 2 * n + pair + 1)
                if n >= 2:
                    act.wait_ge(pv_done, n - 1)
                nc.scalar.activation(Pt[:, n % 2, 2 * pair:2 * pair + 2, off:QB], spair[pair][:, :, off:QB],
                                     ACT.Exp).then_inc(p_ready, 1)

            def turn_out(g, qb):
                act.wait_ge(pv_done, g * NI + (QB // P if qb == 0 else NI))
                if g >= 1:
                    act.wait_ge(ring_full, ring_index[("out", g - 1, qb)] + 1)
                nc.scalar.copy(oT[:, qb, :], pv[qb][:]).then_inc(o_ready, 1)

            def own_exps(g):
                act.wait_ge(dless_ready, g + 1)
                nc.scalar.activation(e01[:, g % 2], e01[:, g % 2], ACT.Exp).then_inc(e01_ready, 1)

            round_q(0)
            round_q(1)
            own_exps(0)
            for g in range(NG):
                for i in range(NI):
                    for pair in range(2):
                        exps(g, i, pair)
                    if i == 1 and g >= 1:
                        turn_out(g - 1, 1)
                    if i == 5:
                        turn_out(g, 0)
                    if g % 2 == 0 and g // 2 + 1 < NU and i in (HALF_SLOTS - 2, 2 * HALF_SLOTS - 2):
                        round_q(2 * (g // 2 + 1) + i // HALF_SLOTS)
                if g + 1 < NG:
                    own_exps(g + 1)
            turn_out(NG - 1, 1)

        @block.tensor
        def _(pe):
            def ring_take(it):
                n = ring_index[it]
                bank = ringb[n % 2]
                if n >= 2:
                    pe.wait_ge(ring_free, n - 1)
                if it[0] == "diag":
                    u = it[1]
                    pe.wait_ge(dprod_ready, 4 * (u + 1))
                    for kind in range(2):
                        for k in range(TB):
                            col = (kind * TB + k) * UH
                            last = nc.tensor.matmul(bank[:, col:col + UH], dprod[:, kind, k * P:(k + 1) * P],
                                                    sumsel[:], start=True, stop=True)
                elif it[0] == "max":
                    _, g, (h, qt, c) = it
                    slot = GH * (g % 2) + h
                    if (qt, c) == (0, 0):
                        pe.wait_ge(kq1_in[slot], 64 * (g // 2) + 32)
                    lo, hi = c * QB, min((c + 1) * QB, (qt + 1) * P)
                    ma, mb = max(qt * P - 2, lo), hi
                    masked = mb > ma
                    last = nc.tensor.matmul(bank[:, 0:hi - lo], Q1[0:MROW, slot, qt * P:(qt + 1) * P],
                                            K[0:MROW, slot, lo:hi], start=True, stop=not masked)
                    if masked:
                        o = ma - (qt * P - 2)
                        last = nc.tensor.matmul(bank[:, ma - lo:mb - lo], identb[:], mask_q[:, o:o + mb - ma],
                                                start=False, stop=True)
                elif it[0] == "turn_m":
                    g = it[1]
                    pe.wait_ge(nm_ready, g + 1)
                    last = nc.tensor.transpose(bank[0:GH * TB, 0:P], nm[:].rearrange("p h t -> p (h t)"), ident[:])
                else:
                    _, g, qb = it
                    pe.wait_ge(o_ready, 2 * g + qb + 1)
                    for k in range(4):
                        last = nc.tensor.transpose(bank[:, k * P:(k + 1) * P], oT[:, qb, k * P:(k + 1) * P], ident[:])
                last.then_inc(ring_full, 1)

            def scores(g, i, pair, ring_between):
                n = g * NI + i
                qb, kt = ITEMS[i]
                q0, q1 = max(kt * P, qb * QB), (qb + 1) * QB
                if n >= 1:
                    pe.wait_ge(p_ready, 2 * (n - 1) + pair + 1)
                if i == 0:
                    pe.wait_ge(mrow_in, 16 * (g + 1))
                if kt == 0:
                    pe.wait_ge(q2_in[qb], 128 * (g + 1))
                ma, mb = max(kt * P, q0), min(kt * P + P + 2, q1)
                masked = mb > ma
                for j in range(2):
                    h = 2 * pair + j
                    if j:
                        ring_between(2 * pair)
                    slot = GH * (g % 2) + h
                    bank = spair[pair][:, j, :]
                    o = q0 - qb * QB
                    keys = slice(kt * P, (kt + 1) * P)
                    nc.tensor.matmul(bank[:, o:QB], K[:, slot, keys], Q1[:, slot, q0:q1], start=True, stop=False)
                    last = nc.tensor.matmul(bank[:, o:QB], K[0:MROW, slot, keys], Q2[:, qb, h, o:QB],
                                            start=False, stop=not masked)
                    if masked:
                        a, b_ = ma - qb * QB, mb - qb * QB
                        last = nc.tensor.matmul(bank[:, a:b_], identb[:], mask_k[:, ma - kt * P:mb - kt * P],
                                                start=False, stop=True)
                last.then_inc(s_full, 1)

            def weigh(g, i):
                n = g * NI + i
                qb, kt = ITEMS[i]
                off = max(0, kt * P - qb * QB)
                pe.wait_ge(p_ready, 2 * (n + 1))
                if kt == 0 and g >= 1:
                    pe.wait_ge(o_ready, 2 * (g - 1) + qb + 1)
                t = (g // 4) * TB + kt
                for h in range(GH):
                    c0 = (t * H + GH * (g % 4) + h) * VW
                    last = nc.tensor.matmul(pv[qb][32 * h:32 * h + 32, off:QB], vaug[:, c0:c0 + 32],
                                            Pt[:, n % 2, h, off:QB], start=(kt == 0),
                                            stop=(kt == (qb + 1) * QB // P - 1))
                last.then_inc(pv_done, 1)

            for s_ in range(NI + 1):
                for it in stage_items(-1, s_):
                    ring_take(it)
            for g in range(NG):
                for i in range(NI):
                    items = [it for it in stage_items(g, i) if it[0] != "turn_m"]
                    late = stage_items(g, i)[len(items):]

                    def ring_between(m):
                        for it in items[m:m + 1]:
                            ring_take(it)

                    for pair in range(2):
                        scores(g, i, pair, ring_between)
                        ring_between(2 * pair + 1)
                    if i:
                        weigh(g, i - 1)
                    for it in items[4:] + late:
                        ring_take(it)
                weigh(g, NI - 1)
            for it in stage_items(NG, 0):
                ring_take(it)

        @block.vector
        def _(dve):
            s = Steps(dve, dve_steps)

            def taps(n, steps):
                u, half = divmod(n, 2)
                t0 = half * QB
                if n and 0 in steps:
                    dve.wait_ge(qhi_ready, n)
                    dve.wait_ge(dprod_ready, 2 * n)
                    dve.wait_ge(qlo_ready, n)
                q = [ucol(qT, u, t0, i - 1) for i in range(3)]
                k = [[kerP[:, u, 3 * i + j:3 * i + j + 1] for j in range(3)] for i in range(3)]
                mid = {0: (qf[:, 0, :], qf[:, 0, :]), 1: (q1a[:], q1a[:]), 2: (q2a[:], q2b[:])}
                for step in steps:
                    i, j = 2 - step // 3, step % 3
                    if i == 2:
                        s.mark(nc.vector.tensor_scalar(mid[j][0], q[2], k[2][j], None, ALU.mult))
                    else:
                        src = mid[j][0] if i == 1 else mid[j][1]
                        dst = mid[j][1] if i == 1 else qf[:, j, :]
                        if j == 0:
                            dve.wait_ge(dve_steps, s.n)
                        ins = nc.vector.scalar_tensor_tensor(dst, q[i], k[i][j], src, ALU.mult, ALU.add)
                        if (i, j) == (0, 2):
                            ins.then_inc(taps_done, 1)
                        else:
                            s.mark(ins)

            def low_parts(n):
                dve.wait_ge(qhi_ready, n + 1)
                if n:
                    dve.wait_ge(qlo_out, 16 * n)
                nc.vector.tensor_tensor(qlo[:], qf[:], qhi[:].bitcast(F32), ALU.subtract).then_inc(qlo_ready, 1)

            def ring_give(it):
                n = ring_index[it]
                bank = ringb[n % 2]
                dve.wait_ge(ring_full, n + 1)
                if it[0] == "diag":
                    ins = nc.vector.tensor_copy(d01[:].rearrange("p c t h -> p (c t h)"), bank[:, 0:2 * TB * UH])
                    ins.then_inc(ring_free, 1)
                    dve.wait_ge(ring_free, n + 1)
                    s.mark(nc.vector.tensor_scalar(d01[:, 1, 0, :], d01[:, 1, 0, :], first_neg[:, 0:1], None, ALU.add))
                elif it[0] == "max":
                    _, g, (h, qt, c) = it
                    width = min((c + 1) * QB, (qt + 1) * P) - c * QB
                    col = chunk_column(qt, c)
                    nc.vector.tensor_reduce(mx[:, h, col:col + 1], bank[:, 0:width], X, ALU.max).then_inc(ring_free, 1)
                elif it[0] == "turn_m":
                    g = it[1]
                    if g:
                        dve.wait_ge(mrow_in, 16 * g)
                    nc.vector.tensor_copy(mrow[:], bank[0:GH * TB, 0:P]).then_inc(ring_free, 1)
                else:
                    _, g, qb = it
                    w, rows = g % 2, slice(4 * qb, 4 * qb + 4)
                    o = bank[:].rearrange("p (k h e) -> p k h e", k=4, h=GH)
                    m = 2 * g + qb
                    dve.wait_ge(own_ready, 3 * (g + 1))
                    if m:
                        dve.wait_ge(ao_ready, m)
                    if m >= 2:
                        dve.wait_ge(ao_out[m % 2], 16 * (m // 2))
                    s.mark(nc.vector.tensor_tensor(rl[:], o[:, :, :, HD], esum[:, w, rows, :], ALU.add))
                    ins = nc.vector.tensor_tensor(num[:], o[:, :, :, 0:HD], own[:, w, rows, :, :], ALU.add)
                    ins.then_inc(ring_free, 1)
                    dve.wait_ge(ring_free, n + 1)
                    s.link(nc.vector.reciprocal(rl[:], rl[:]))
                    nc.vector.tensor_tensor(ao[:, m % 2], num[:], rl[:].unsqueeze(3).to_broadcast([P, 4, GH, HD]),
                                            ALU.mult).then_inc(ao_ready, 1)

            def finish_max(g):
                hh = GH * (g % 2)
                dv = [d01[:, k, :, hh:hh + GH] for k in range(2)]
                last = max(ring_index[("max", g, CHUNKS[-1])], ring_index[("diag", g // 2)])
                dve.wait_ge(ring_free, last + 1)
                dve.wait_ge(dve_steps, s.n)
                hi = (T - QB) // P
                s.link(nc.vector.tensor_tensor(mx[:, :, TB - hi:TB], mx[:, :, TB - hi:TB], mx[:, :, TB:TB + hi], ALU.max))
                for k in range(2):
                    s.link(nc.vector.tensor_tensor(mx[:, :, 0:TB], mx[:, :, 0:TB],
                                                   dv[k].rearrange("p t h -> p h t"), ALU.max))
                if g:
                    dve.wait_ge(ring_full, ring_index[("turn_m", g - 1)] + 1)
                nc.vector.tensor_scalar(nm[:].bitcast(F32R), mx[:, :, 0:TB], -1.0, None, ALU.mult).then_inc(nm_ready, 1)
                dve.wait_ge(nm_ready, g + 1)
                if g >= 2:
                    dve.wait_ge(own_ready, 3 * (g - 1))
                for k in range(2):
                    ins = nc.vector.tensor_tensor(e01[:, g % 2, k], dv[k], nm[:].rearrange("p h t -> p t h"), ALU.add)
                    s.mark(ins) if k == 0 else ins.then_inc(dless_ready, 1)

            for half in range(2):
                taps(half, range(9))
                low_parts(half)
            for it in stage_items(-1, 0):
                ring_give(it)
            finish_max(0)
            for it in stage_items(-1, NI):
                ring_give(it)
            for g in range(NG):
                more = g % 2 == 0 and g // 2 + 1 < NU
                n0 = 2 * (g // 2 + 1)
                for i in range(NI):
                    items = stage_items(g, i)
                    half, third = divmod(i, HALF_SLOTS)
                    if i == LAST_MAX + 1 and g + 1 < NG:
                        finish_max(g + 1)
                    for m in range(max(len(items), 3)):
                        for it in items[m:m + 1]:
                            ring_give(it)
                        if more and half < 2 and third < 3 and m < 3:
                            taps(n0 + half, [3 * third + m])
                    if more and half < 2 and third == HALF_SLOTS - 1:
                        low_parts(n0 + half)
            for it in stage_items(NG, 0):
                ring_give(it)

def general_attention(nc, sem, ident, qT, kT, vaug_t, mask, kern_d, qk_d, v_d, oh_d, ao_d):
    HEADS = B * H
    NP2 = NQB * TB
    with ExitStack() as ctx:
        def sb(name, shape, dt=F32):
            return ctx.enter_context(nc.sbuf_tensor(name, shape, dt))

        mask_words = sb("g_mask", [P, TB, T // 4], mybir.dt.int32)
        keep = sb("g_keep", [P, TB, T], BF16)
        drop = sb("g_drop", [P, TB, T], BF16)
        shift = sb("g_shift", [P, 3, P])
        corner = sb("g_corner", [P, 2, P])
        qh, kh = sb("g_q", [HD, T]), sb("g_k", [HD, T])
        vh = sb("g_v", [P, TB, HD])
        taps = sb("g_taps", [P, TAPS])
        band = sb("g_band", [P, 3, P])
        part = sb("g_part", [P, 3, P])
        edge = sb("g_edge", [P, 2, 3, P])
        s0 = sb("g_s0", [P, TB, T + 2])
        sc = sb("g_sc", [P, T])
        pr = sb("g_p", [P, T])
        prT = sb("g_pT", [P, TB, P])
        nmax, total = sb("g_nmax", [P, 1]), sb("g_total", [P, 1])
        oh = sb("g_oh", [P, TB, HD])
        spare = sb("g_spare", [P, 1])
        sbank, cbank, tbank = ([ctx.enter_context(nc.psum_tensor(f"g_{n}bank{i}", [P, QB], F32)) for i in range(2)]
                               for n in ("s", "c", "t"))
        obank = ctx.enter_context(nc.psum_tensor("g_o", [P, QB], F32))

        mask_in, dumped, head_in, head_out = (sem(n) for n in ("g_mask_in", "g_dumped", "g_head_in", "g_head_out"))
        masks_ready, shifts_ready, steps, psteps = (sem(n) for n in ("g_masks", "g_shifts", "g_steps", "g_psteps"))
        bands_ready, s_full, s_free, c_full, c_free = (sem(n) for n in (
            "g_bands", "g_s_full", "g_s_free", "g_c_full", "g_c_free"))
        max_ready, p_ready, t_full, t_free, o_full, o_free = (sem(n) for n in (
            "g_max", "g_p_ready", "g_t_full", "g_t_free", "g_o_full", "g_o_free"))
        written, spare_ready = sem("g_written"), sem("g_spare")

        block = ctx.enter_context(nc.Block())

        @block.sync
        def _(sp):
            sp.dma_start(mask_words[:], mask.rearrange("(t p) k -> p t k", p=P)).then_inc(mask_in, 16)
            for n, t in enumerate((qT, kT)):
                sp.dma_start(qk_d[n].rearrange("(u p) t -> p u t", p=P), t[:]).then_inc(dumped, 16)
            for b in range(B):
                for h in range(H):
                    sp.dma_start(v_d[b * H + h], vaug_t[:, b * TB:(b + 1) * TB, h, 0:HD]).then_inc(dumped, 16)
            sp.wait_ge(dumped, 16 * (2 + HEADS))
            sp.dma_start(oh_d[0], v_d[0]).then_inc(head_out, 16)
            sp.wait_ge(head_out, 16)
            with sp.Fori(0, HEADS) as i:
                row0 = sp.snap(i * HD)
                sp.wait_ge(o_free, i * TB + 1)
                for n, t in enumerate((qh, kh)):
                    sp.dma_start(t[:], qk_d[n, bass.ds(row0, HD), LPAD:LPAD + T]).then_inc(head_in, 16)
                sp.dma_start(vh[:], v_d[bass.ds(i, 1)].rearrange("o p t d -> (o p) t d")).then_inc(head_in, 16)
                row = kern_d.rearrange("b (h t) -> (b h) t", t=TAPS)[bass.ds(i, 1), :]
                sp.dma_start(taps[:], row.partition_broadcast(P).rearrange("p o t -> p (o t)")).then_inc(head_in, 16)
                sp.wait_ge(o_free, i * TB + TB + 1)
                sp.dma_start(oh_d[bass.ds(i, 1)].rearrange("o p t d -> (o p) t d"), oh[:]).then_inc(head_out, 16)
            sp.wait_ge(head_out, 16 * (HEADS + 1))
            for b in range(B):
                for h in range(H):
                    dst = ao_d[b * T:(b + 1) * T, h * HD:(h + 1) * HD].rearrange("(t p) d -> p t d", p=P)
                    sp.dma_start(dst, oh_d[b * H + h]).then_inc(written, 16)
            sp.wait_ge(written, 16 * HEADS)

        @block.gpsimd
        def _(pool):
            s = Steps(pool, psteps)
            s.mark(nc.gpsimd.memset(shift[:], 0.0))
            s.link(nc.gpsimd.memset(corner[:], 0.0))
            for i in range(3):
                s.link(nc.gpsimd.affine_select(out=shift[:, i, :], in_=shift[:, i, :], compare_op=ALU.not_equal,
                                               fill=1.0, base=1 - i, pattern=[[-1, P]], channel_multiplier=1))
            for n, base in enumerate((1 - P, P - 1)):
                s.link(nc.gpsimd.affine_select(out=corner[:, n, :], in_=corner[:, n, :], compare_op=ALU.not_equal,
                                               fill=1.0, base=base, pattern=[[-1, P]], channel_multiplier=1))
            nc.gpsimd.memset(spare[:], 0.0).then_inc(shifts_ready, 1)

        @block.tensor
        def _(pe):
            with pe.Fori(0, HEADS) as i:
                pe.wait_ge(head_in, i * 64 + 64)
                for n in range(NP2):
                    qt, c = divmod(n, NQB)
                    pe.wait_ge(s_free, i * NP2 + n + 1)
                    nc.tensor.matmul(sbank[n % 2][:], qh[:, qt * P:(qt + 1) * P], kh[:, c * QB:(c + 1) * QB],
                                     start=True, stop=True).then_inc(s_full, 1)
                pe.wait_ge(bands_ready, i + 1)
                pe.wait_ge(s_free, i * NP2 + NP2 + 2)
                for qt in range(TB):
                    for c in range(NQB):
                        n = NQB * qt + c
                        pe.wait_ge(c_free, i * NP2 + n + 1)
                        around = [(band, qt)] + [(edge[:, m], t) for m, t in ((0, qt - 1), (1, qt + 1)) if 0 <= t < TB]
                        taken = [(w, t, j) for w, t in around for j in range(3)]
                        for m, (w, t, j) in enumerate(taken):
                            last = nc.tensor.matmul(cbank[n % 2][:], w[:, j, :], s0[:, t, c * QB + j:c * QB + j + QB],
                                                    start=(m == 0), stop=(m == len(taken) - 1))
                        last.then_inc(c_full, 1)
                    pe.wait_ge(p_ready, i * TB + qt + 1)
                    for c in range(NQB):
                        pe.wait_ge(t_free, i * NP2 + NQB * qt + c + 1)
                        for k in range(QB // P):
                            last = nc.tensor.transpose(tbank[c][:, k * P:(k + 1) * P],
                                                       pr[:, (4 * c + k) * P:(4 * c + k + 1) * P], ident[:])
                        last.then_inc(t_full, 1)
                    pe.wait_ge(t_free, i * NP2 + NQB * (qt + 1) + 2)
                    pe.wait_ge(o_free, i * TB + qt + 1)
                    for k in range(TB):
                        last = nc.tensor.matmul(obank[:, 0:HD], prT[:, k, :], vh[:, k, :], start=(k == 0), stop=(k == TB - 1))
                    last.then_inc(o_full, 1)

        @block.scalar
        def _(act):
            act.sem_inc(t_free, 2)
            with act.Fori(0, HEADS) as i:
                for qt in range(TB):
                    act.wait_ge(max_ready, i * TB + qt + 1)
                    nc.scalar.activation(pr[:], sc[:], ACT.Exp, bias=nmax[:, 0:1], accum_out=total[:]).then_inc(p_ready, 1)
                    for c in range(NQB):
                        act.wait_ge(t_full, i * NP2 + NQB * qt + c + 1)
                        nc.scalar.copy(prT[:, 4 * c:4 * c + 4, :].rearrange("p k q -> p (k q)"), tbank[c][:]).then_inc(t_free, 1)

        @block.vector
        def _(dve):
            dve.sem_inc(s_free, 2)
            dve.sem_inc(c_free, 2)
            dve.sem_inc(o_free, 1)
            dve.wait_ge(mask_in, 16)
            dve.wait_ge(shifts_ready, 1)
            nc.vector.tensor_scalar(keep[:], mask_words[:].bitcast(mybir.dt.uint8), -1.0, 1.0, ALU.mult, ALU.add).then_inc(masks_ready, 1)
            nc.vector.tensor_scalar(drop[:], mask_words[:].bitcast(mybir.dt.uint8), -BIG, None, ALU.mult).then_inc(masks_ready, 1)
            nc.vector.memset(s0[:], 0.0).then_inc(masks_ready, 1)
            dve.wait_ge(masks_ready, 3)
            NS = 6
            with dve.Fori(0, HEADS) as i:
                dve.wait_ge(head_in, i * 64 + 64)
                tap = [taps[:, 3 * r:3 * r + 3].unsqueeze(2).to_broadcast([P, 3, P]) for r in range(3)]
                wide = lambda a: a.unsqueeze(1).to_broadcast([P, 3, P])
                nc.vector.tensor_tensor(band[:], wide(shift[:, 0, :]), tap[0], ALU.mult).then_inc(steps, 1)
                nc.vector.tensor_tensor(part[:], wide(shift[:, 1, :]), tap[1], ALU.mult).then_inc(steps, 1)
                dve.wait_ge(steps, i * NS + 2)
                nc.vector.tensor_tensor(band[:], band[:], part[:], ALU.add).then_inc(steps, 1)
                dve.wait_ge(steps, i * NS + 3)
                nc.vector.tensor_tensor(part[:], wide(shift[:, 2, :]), tap[2], ALU.mult).then_inc(steps, 1)
                dve.wait_ge(steps, i * NS + 4)
                nc.vector.tensor_tensor(band[:], band[:], part[:], ALU.add).then_inc(steps, 1)
                nc.vector.tensor_tensor(edge[:, 0], wide(corner[:, 0, :]), tap[0], ALU.mult).then_inc(steps, 1)
                nc.vector.tensor_tensor(edge[:, 1], wide(corner[:, 1, :]), tap[2], ALU.mult).then_inc(bands_ready, 1)
                for n in range(NP2):
                    qt, c = divmod(n, NQB)
                    dve.wait_ge(s_full, i * NP2 + n + 1)
                    nc.vector.tensor_tensor(s0[:, qt, 1 + c * QB:1 + (c + 1) * QB], sbank[n % 2][:],
                                            keep[:, qt, c * QB:(c + 1) * QB], ALU.mult).then_inc(s_free, 1)
                for qt in range(TB):
                    dve.wait_ge(o_free, i * TB + qt + 1)
                    for c in range(NQB):
                        n = NQB * qt + c
                        dve.wait_ge(c_full, i * NP2 + n + 1)
                        nc.vector.tensor_tensor(sc[:, c * QB:(c + 1) * QB], cbank[n % 2][:],
                                                drop[:, qt, c * QB:(c + 1) * QB], ALU.add).then_inc(c_free, 1)
                    dve.wait_ge(c_free, i * NP2 + NQB * (qt + 1) + 2)
                    nc.vector.tensor_reduce(nmax[:], sc[:], X, ALU.max, negate=True).then_inc(max_ready, 1)
                    dve.wait_ge(p_ready, i * TB + qt + 1)
                    dve.wait_ge(o_full, i * TB + qt + 1)
                    if qt == 0:
                        dve.wait_ge(head_out, i * 16 + 16)
                    nc.vector.reciprocal(spare[:], total[:]).then_inc(spare_ready, 1)
                    dve.wait_ge(spare_ready, i * TB + qt + 1)
                    nc.vector.tensor_scalar(oh[:, qt, :], obank[:, 0:HD], spare[:, 0:1], None, ALU.mult).then_inc(o_free, 1)

def block3(nc, sem, ident, vkeep, x, ao_d, x1_d, proj_W, wrT, w1T, w2T, out):
    KS = E * FC
    NR = LOOPS * NB
    BT = QB // P
    NE12 = GROUPS + E
    LR = 32 + NE12
    CR = 32 + E
    HB, SB = 3, 5
    with ExitStack() as ctx:
        def sb(name, shape, dt=F32):
            return ctx.enter_context(nc.sbuf_tensor(name, shape, dt))

        w1 = [sb(f"w1{n}", [P, DC, E, F], F32R) for n in ("hi", "lo")]
        w2 = [sb(f"w2{n}", [P, FC, E, D], F32R) for n in ("hi", "lo")]
        wr = sb("wr", [P, DC, P], F32R)
        wr_f = sb("wr_f", [P, DC, NE12])
        proj_w = sb("proj_w", [P, DC, D])
        z = sb("z", [P, NT, D])
        xT = [[sb(f"xT{n}{b}", [P, DC, QB], F32R) for n in ("hi", "lo")] for b in range(2)]
        hs = sb("hs", [P, HB, QB])
        hh, hl = (sb(n, [P, SB, QB], F32R) for n in ("hh", "hl"))
        yT = sb("yT", [P, DC, QB])
        xn = yT[:].rearrange("p c q -> p (c q)").rearrange("p (t d) -> p t d", d=D)
        both = sb("both", [P, DC, QB])
        rows = both[:].rearrange("p c q -> p (c q)").rearrange("p (t d) -> p t d", d=D)
        stage = sb("stage", [P, 2, QB])
        cs = sb("cs", [CR, QB], F32R)
        esel = sb("esel", [CR, E], F32R)
        esel_f = sb("esel_f", [CR, E])
        minus_low = sb("minus_low", [CR, 1])
        rank0 = sb("rank0", [P, BT, GROUPS])
        st6 = sb("st6", [P, 6])
        mv = sb("mv3", [P, BT, 2])
        sd = sb("sd", [P, 2, BT])
        lg = sb("lg", [P, BT, NE12])
        mm = sb("mm", [P, BT, 1 + GROUPS])
        rk = sb("rk", [P, BT, GROUPS])
        ge = sb("ge", [P, BT, GROUPS])
        wg = sb("wg", [P, BT, GROUPS])
        c40 = sb("c40", [P, BT, CR])

        hb = [ctx.enter_context(nc.psum_tensor(f"hb{i}", [P, QB], F32)) for i in range(HB)]
        cb = ctx.enter_context(nc.psum_tensor("cb", [P, QB], F32))
        acc = [ctx.enter_context(nc.psum_tensor(f"acc{i}", [P, QB], F32)) for i in range(DC)]
        misc = [ctx.enter_context(nc.psum_tensor(f"misc{i}", [P, QB], F32)) for i in range(2)]

        dve_steps, pool_steps = sem("dve_steps3"), sem("pool_steps3")
        proj_in, router_in = sem("proj_in"), sem("router_in")
        xz_in = [sem(f"xz_in{n}") for n in range(NB)]
        stage_in = [sem(f"stage_in{i}") for i in range(2)]
        whi_done, wlo_done = sem("whi_done"), sem("wlo_done")
        consts = sem("consts3")
        router_ready = sem("router_ready")
        rows_in, x1_out, x1_ready, out_ready, out_done = (sem(n) for n in (
            "rows_in", "x1_out", "x1_ready", "out_ready", "out_done"))
        misc_full, misc_free = sem("misc_full"), sem("misc_free")
        ln_var, ln_std, rms_var, rms_std = (sem(n) for n in ("ln_var", "ln_std", "rms_var", "rms_std"))
        xn_ready, xhi_done = sem("xn3_ready"), sem("xhi_done")
        logits_exp, c_ready, chi_done = (sem(n) for n in ("logits_exp", "c_ready", "chi_done"))
        h_full, silu_done, hc_done, hi_done, lo_done = (sem(n) for n in (
            "h_full", "silu_done", "hc_done", "hi_done", "lo_done"))
        cb_full, l2_done, yT_ready, z_ready = (sem(n) for n in ("cb_full", "l2_done", "yT_ready", "z_ready"))

        def items_at(r, k):
            out_ = []
            if k == 1 and r + 1 < NB:
                out_ += [("aoT", r + 1, c) for c in range(DC)]
            if k == 2 and r + 1 < NB:
                out_ += [("proj", r + 1, half) for half in range(2)]
            if k == 6 and r >= 1:
                out_ += [("z", r - 1, half) for half in range(2)]
            if r + 1 < NR:
                out_ += {11: [("x", r + 1, c) for c in range(DC)], 14: [("logits", r + 1)],
                         16: [("turn_l", r + 1)], 27: [("turn_c", r + 1)]}.get(k, [])
            return out_

        order = [it for r in range(-1, NR + 1) for k in range(KS) for it in items_at(r, k)]
        index = {it: n for n, it in enumerate(order)}
        pieces = [(w, e, c) for e in range(E) for w in (1, 2) for c in range(2)]

        def piece_of(w, e, c):
            if w == 1:
                return (lambda t: t[:, c, e, :]), (lambda st: st)
            return (lambda t: t[:, 2 * c:2 * c + 2, e, :]), (lambda st: st.rearrange("p (a d) -> p a d", a=2))

        block = ctx.enter_context(nc.Block())

        @block.sync
        def _(sp):
            for n in range(NB):
                sp.dma_start(z[:, BT * n:BT * n + BT, :],
                             x[n * QB:(n + 1) * QB, :].rearrange("(t p) d -> p t d", p=P)).then_inc(xz_in[n], 16)
                if n == 0:
                    sp.dma_start(rows, ao_d[0:QB, :].rearrange("(t p) d -> p t d", p=P)).then_inc(rows_in, 16)
                    sp.dma_start(proj_w[:], proj_W.rearrange("(c p) n -> p c n", p=P)).then_inc(proj_in, 16)
                    sp.dma_start(wr_f[:], wrT.rearrange("(c p) n -> p c n", p=P)).then_inc(router_in, 16)

            def write_x1(n):
                sp.wait_ge(x1_ready, n + 1)
                sp.dma_start(x1_d[n * QB:(n + 1) * QB, :].rearrange("(t p) d -> p t d", p=P),
                             z[:, BT * n:BT * n + BT, :]).then_inc(x1_out, 16)

            def write_out(n):
                sp.wait_ge(out_ready, n + 1)
                sp.dma_start(out[n * QB:(n + 1) * QB, :].rearrange("(t p) d -> p t d", p=P),
                             z[:, BT * n:BT * n + BT, :]).then_inc(out_done, 16)

            write_x1(0)
            for r in range(NR):
                sp.wait_ge(misc_free, index[("turn_c", r)] + 1)
                if r + 1 < NB:
                    n = r + 1
                    sp.dma_start(rows, ao_d[n * QB:(n + 1) * QB, :].rearrange("(t p) d -> p t d", p=P)).then_inc(rows_in, 16)
                    write_x1(n)
                if r >= NB + 1:
                    n = r - 1 - NB
                    sp.dma_start(rows, x1_d[n * QB:(n + 1) * QB, :].rearrange("(t p) d -> p t d", p=P)).then_inc(rows_in, 16)
                    write_out(n)
            n = NB - 1
            sp.wait_ge(out_ready, n)
            sp.dma_start(rows, x1_d[n * QB:(n + 1) * QB, :].rearrange("(t p) d -> p t d", p=P)).then_inc(rows_in, 16)
            write_out(n)
            sp.wait_ge(out_done, 16 * NB)

        @block.gpsimd
        def _(pool):
            s = Steps(pool, pool_steps)
            for t, v in ((esel_f, 0.0), (minus_low, -1.0), (c40, 0.0)):
                s.mark(nc.gpsimd.memset(t[:], v))
            for g in range(GROUPS):
                s.mark(nc.gpsimd.memset(rank0[:, :, g:g + 1], float(GROUPS - 1 - g)))
            pool.wait_ge(pool_steps, s.n)
            s.mark(nc.gpsimd.memset(minus_low[0:32, :], 0.0))
            for base in (0, 32):
                s.link(nc.gpsimd.affine_select(out=esel_f[:], in_=esel_f[:], compare_op=ALU.not_equal, fill=1.0,
                                               base=-base, pattern=[[-1, E]], channel_multiplier=1))
            nc.gpsimd.tensor_copy(esel[:], esel_f[:]).then_inc(consts, 1)
            for i, (w, e, c) in enumerate(pieces):
                if i >= 2:
                    pool.wait_ge(wlo_done, i - 1)
                if i < 2:
                    load_piece(nc, pool, stage, w1T, w2T, pieces, i, stage_in)
                pool.wait_ge(whi_done, i + 1)
                to, view = piece_of(w, e, c)
                hi, lo = (w1, w2)[w - 1]
                nc.gpsimd.tensor_tensor(to(lo), view(stage[:, i % 2, :]), to(hi).bitcast(F32),
                                        ALU.subtract).then_inc(wlo_done, 1)
                if i + 2 < len(pieces):
                    pool.wait_ge(wlo_done, i + 1)
                    load_piece(nc, pool, stage, w1T, w2T, pieces, i + 2, stage_in)

        @block.tensor
        def _(pe):
            def take(it):
                i = index[it]
                bank = misc[i % 2]
                if i >= 2:
                    pe.wait_ge(misc_free, i - 1)
                kind = it[0]
                if kind == "aoT":
                    _, n, c = it
                    pe.wait_ge(rows_in, 16 * (n + 1))
                    for t in range(BT):
                        last = nc.tensor.transpose(bank[:, t * P:(t + 1) * P], rows[:, t, c * P:(c + 1) * P], ident[:])
                elif kind == "proj":
                    _, n, half = it
                    pe.wait_ge(misc_free, index[("aoT", n, DC - 1)] + 1)
                    if n == 0 and half == 0:
                        pe.wait_ge(proj_in, 16)
                    for j in range(2):
                        t = 2 * half + j
                        for c in range(DC):
                            last = nc.tensor.matmul(bank[:, j * D:(j + 1) * D], yT[:, c, t * P:(t + 1) * P],
                                                    proj_w[:, c, :], start=(c == 0), stop=(c == DC - 1))
                elif kind == "z":
                    _, r, half = it
                    pe.wait_ge(yT_ready, r + 1)
                    for j in range(2):
                        t = 2 * half + j
                        for c in range(DC):
                            o = j * D + c * P
                            last = nc.tensor.transpose(bank[:, o:o + P], yT[:, c, t * P:(t + 1) * P], ident[:])
                elif kind == "x":
                    _, r, c = it
                    pe.wait_ge(xn_ready, r + 1)
                    for t in range(BT):
                        last = nc.tensor.transpose(bank[:, t * P:(t + 1) * P], xn[:, t, c * P:(c + 1) * P], ident[:])
                elif kind == "logits":
                    r = it[1]
                    pe.wait_ge(misc_free, index[("x", r, DC - 1)] + 1)
                    pe.wait_ge(router_ready, 1)
                    for c in range(DC):
                        for b_ in range(2):
                            last = nc.tensor.matmul(bank[:], wr[:, c, :], xT[r % 2][b_][:, c, :],
                                                    start=(c + b_ == 0), stop=(c + b_ == DC))
                elif kind == "turn_l":
                    r = it[1]
                    pe.wait_ge(misc_free, index[("logits", r)] + 1)
                    for t in range(BT):
                        last = nc.tensor.transpose(bank[:, t * LR:(t + 1) * LR], both[0:LR, 0, t * P:(t + 1) * P],
                                                   ident[0:LR, 0:LR])
                else:
                    r = it[1]
                    pe.wait_ge(c_ready, r + 1)
                    for t in range(BT):
                        last = nc.tensor.transpose(bank[0:CR, t * P:(t + 1) * P], c40[:, t, :], ident[:])
                last.then_inc(misc_full, 1)

            def spread(g):
                e = g % E
                if g:
                    pe.wait_ge(hc_done, FC * g)
                if e == 0:
                    pe.wait_ge(misc_free, index[("turn_c", g // E)] + 1)
                nc.tensor.matmul(cb[:], esel[:, e:e + 1].to_broadcast([CR, P]), cs[:],
                                 start=True, stop=True).then_inc(cb_full, 1)

            def hidden(kk):
                r, k = divmod(kk, KS)
                e, f = divmod(k, FC)
                if kk >= HB:
                    pe.wait_ge(silu_done, kk - HB + 1)
                if r == 0 and f == 0:
                    pe.wait_ge(wlo_done, 4 * e + 2)
                if k == 0:
                    pe.wait_ge(misc_free, index[("x", r, DC - 1)] + 1)
                n = 0
                for c in range(DC):
                    for a, b_ in ((0, 0), (0, 1), (1, 0)):
                        last = nc.tensor.matmul(hb[kk % HB][:], w1[a][:, c, e, f * P:(f + 1) * P], xT[r % 2][b_][:, c, :],
                                                start=(n == 0), stop=(n == 3 * DC - 1))
                        n += 1
                last.then_inc(h_full, 1)

            def outward(kk):
                r, k = divmod(kk, KS)
                e, f = divmod(k, FC)
                pe.wait_ge(lo_done, kk + 1)
                if r == 0 and f == 0:
                    pe.wait_ge(wlo_done, 4 * e + 4)
                if k == 0 and r:
                    pe.wait_ge(yT_ready, r)
                for c in range(DC):
                    for n, (a, part) in enumerate(((0, hh), (0, hl), (1, hh))):
                        last = nc.tensor.matmul(acc[c][:], w2[a][:, f, e, c * P:(c + 1) * P], part[:, kk % SB, :],
                                                start=(k == 0 and n == 0), stop=(k == KS - 1 and n == 2))
                last.then_inc(l2_done, 1)

            pe.wait_ge(consts, 1)
            for k in range(KS):
                for it in items_at(-1, k):
                    take(it)
            for kk in range(NR * KS + FC):
                r, k = divmod(kk, KS)
                if k % FC == 2 and kk < NR * KS:
                    spread(kk // FC)
                for it in items_at(r, k):
                    take(it)
                if kk < NR * KS:
                    hidden(kk)
                if kk >= FC:
                    outward(kk - FC)
            for it in items_at(NR, 6):
                take(it)

        @block.scalar
        def _(act):
            def weight_hi(i):
                w, e, c = pieces[i]
                to, view = piece_of(w, e, c)
                act.wait_ge(stage_in[i % 2], 16 * (i // 2 + 1))
                nc.scalar.copy(to((w1, w2)[w - 1][0]), view(stage[:, i % 2, :])).then_inc(whi_done, 1)

            def steps_at(r, k):
                n = r + 1
                if k == 4 and n < NB:
                    act.wait_ge(ln_var, n + 1)
                    nc.scalar.activation(sd[:, 0, :], sd[:, 0, :], ACT.Sqrt).then_inc(ln_std, 1)
                if k == 4 and r >= 1:
                    act.wait_ge(l2_done, KS * r)
                    if n < NB:
                        act.wait_ge(misc_full, index[("proj", n, 1)] + 1)
                    for c in range(DC):
                        last = nc.scalar.copy(yT[:, c, :], acc[c][:])
                        if c == DC - 1:
                            last.then_inc(yT_ready, 1)
                if n >= NR:
                    return
                if k == 9:
                    act.wait_ge(rms_var, n + 1)
                    nc.scalar.activation(sd[:, 1, :], sd[:, 1, :], ACT.Sqrt).then_inc(rms_std, 1)
                if k == 12:
                    for c in range(DC):
                        act.wait_ge(misc_full, index[("x", n, c)] + 1)
                        nc.scalar.copy(xT[n % 2][0][:, c, :], misc[index[("x", n, c)] % 2][:]).then_inc(xhi_done, 1)
                if k == 18:
                    act.wait_ge(misc_free, index[("turn_l", n)] + 1)
                    nc.scalar.activation(lg[:], lg[:], ACT.Exp).then_inc(logits_exp, 1)
                if k == 28:
                    i = index[("turn_c", n)]
                    act.wait_ge(misc_full, i + 1)
                    nc.scalar.copy(both[0:CR, 1, :].bitcast(F32R), misc[i % 2][0:CR, :]).then_inc(chi_done, 1)

            def silu(kk):
                act.wait_ge(h_full, kk + 1)
                if kk >= HB:
                    act.wait_ge(lo_done, kk - HB + 1)
                nc.scalar.activation(hs[:, kk % HB, :], hb[kk % HB][:], ACT.Silu).then_inc(silu_done, 1)

            def high(kk):
                act.wait_ge(hc_done, kk + 1)
                if kk >= SB:
                    act.wait_ge(l2_done, kk - SB + 1)
                nc.scalar.copy(hh[:, kk % SB, :], hs[:, kk % HB, :]).then_inc(hi_done, 1)

            for i in range(4):
                weight_hi(i)
            for k in range(KS):
                steps_at(-1, k)
            for kk in range(NR * KS + 1):
                r, k = divmod(kk, KS)
                if r == 0 and k % FC == 0 and 4 * (kk // FC + 1) < len(pieces):
                    for i in range(4 * (kk // FC + 1), 4 * (kk // FC + 1) + 4):
                        weight_hi(i)
                if kk < NR * KS:
                    steps_at(r, k)
                    silu(kk)
                if kk:
                    high(kk - 1)
            steps_at(NR, 4)

        @block.vector
        def _(dve):
            s = Steps(dve, dve_steps)
            eng = nc.vector
            proj_b = vkeep[:, VEC["proj_b"][0]:VEC["proj_b"][1]]
            norm_w = vkeep[:, VEC["norm_w"][0]:VEC["norm_w"][1]]

            def root(which, ready, eps_in):
                v = mv[:, :, 1]
                s.link(eng.tensor_scalar(v, v, *eps_in, ALU.mult, ALU.add))
                eng.tensor_copy(sd[:, which, :], v).then_inc(ready, 1)

            def root_end(which, done, count):
                dve.wait_ge(done, count)
                r_ = sd[:, which, :]
                s.link(eng.reciprocal(r_, r_))
                t = mm[:, :, 0]
                s.link(eng.tensor_tensor(t, r_, r_, ALU.mult))
                s.link(eng.tensor_tensor(t, t, mv[:, :, 1], ALU.mult))
                s.link(eng.tensor_scalar(t, t, -0.5, 1.5, ALU.mult, ALU.add))
                s.link(eng.tensor_tensor(r_, r_, t, ALU.mult))

            def give(it):
                i = index[it]
                bank = misc[i % 2]
                dve.wait_ge(misc_full, i + 1)
                kind = it[0]
                if kind == "aoT":
                    _, n, c = it
                    eng.tensor_copy(yT[:, c, :], bank[:]).then_inc(misc_free, 1)
                elif kind == "proj":
                    _, n, half = it
                    if half == 0:
                        dve.wait_ge(xz_in[n], 16)
                    for j in range(2):
                        t = BT * n + 2 * half + j
                        o = eng.tensor_tensor(z[:, t, :], z[:, t, :], bank[:, j * D:(j + 1) * D], ALU.add)
                        s.mark(o) if j == 0 else o.then_inc(misc_free, 1)
                    dve.wait_ge(misc_free, i + 1)
                    for j in range(2):
                        t = BT * n + 2 * half + j
                        o = eng.tensor_tensor(z[:, t, :], z[:, t, :], proj_b, ALU.add)
                        s.mark(o) if half == 0 or j == 0 else o.then_inc(x1_ready, 1)
                elif kind == "z":
                    _, r, half = it
                    n = r % NB
                    zt = z[:, BT * n + 2 * half:BT * n + 2 * half + 2, :].rearrange("p t d -> p (t d)")
                    eng.tensor_tensor(zt, zt, bank[:], ALU.add).then_inc(misc_free, 1)
                    if half == 1 and r >= NB:
                        dve.wait_ge(rows_in, 16 * (NB + n + 1))
                        dve.wait_ge(misc_free, i + 1)
                        zz = z[:, BT * n:BT * n + BT, :]
                        eng.tensor_tensor(zz, zz, rows, ALU.add).then_inc(out_ready, 1)
                elif kind == "x":
                    _, r, c = it
                    dve.wait_ge(xhi_done, DC * r + c + 1)
                    xlo = xT[r % 2][1][:, c, :]
                    eng.tensor_tensor(xlo, bank[:], xT[r % 2][0][:, c, :].bitcast(F32), ALU.subtract).then_inc(misc_free, 1)
                    dve.wait_ge(misc_free, i + 1)
                elif kind == "logits":
                    eng.tensor_copy(both[0:LR, 0, :], bank[0:LR, :]).then_inc(misc_free, 1)
                elif kind == "turn_l":
                    r = it[1]
                    l3 = bank[:, 0:BT * LR].rearrange("p (t n) -> p t n", t=BT)
                    s.link(eng.tensor_copy(lg[:], l3[:, :, 32:LR]))
                    s.link(eng.tensor_tensor(lg[:], lg[:], l3[:, :, 0:NE12], ALU.add))
                    pairs = lg[:, :, GROUPS:NE12].rearrange("p t (g m) -> p t g m", m=2)
                    s.link(eng.tensor_reduce(mm[:, :, 0:1], lg[:, :, 0:GROUPS], X, ALU.max))
                    s.link(eng.tensor_reduce(mm[:, :, 1:1 + GROUPS], pairs, X, ALU.max))
                    s.mark(eng.tensor_tensor(lg[:, :, 0:GROUPS], lg[:, :, 0:GROUPS],
                                             mm[:, :, 0:1].to_broadcast([P, BT, GROUPS]), ALU.subtract))
                    eng.tensor_tensor(pairs, pairs, mm[:, :, 1:1 + GROUPS].unsqueeze(3).to_broadcast([P, BT, GROUPS, 2]),
                                      ALU.subtract).then_inc(misc_free, 1)
                else:
                    r = it[1]
                    dve.wait_ge(chi_done, r + 1)
                    dve.wait_ge(cb_full, E * r)
                    eng.scalar_tensor_tensor(cs[:], both[0:CR, 1, :], minus_low[:, 0:1], bank[0:CR, :],
                                             ALU.mult, ALU.add).then_inc(misc_free, 1)

            def combine(r):
                dve.wait_ge(logits_exp, r + 1)
                G = GROUPS
                p = lg[:, :, 0:G]
                pairs = lg[:, :, G:NE12].rearrange("p t (g m) -> p t g m", m=2)
                s.link(eng.tensor_reduce(mm[:, :, 0:1], p, X, ALU.add))
                s.link(eng.tensor_reduce(mm[:, :, 1:1 + G], pairs, X, ALU.add))
                s.link(eng.reciprocal(mm[:], mm[:]))
                s.mark(eng.tensor_tensor(p, p, mm[:, :, 0:1].to_broadcast([P, BT, G]), ALU.mult))
                s.link(eng.tensor_tensor(pairs, pairs, mm[:, :, 1:1 + G].unsqueeze(3).to_broadcast([P, BT, G, 2]),
                                         ALU.mult))
                s.link(eng.tensor_copy(rk[:], rank0[:]))
                for d in range(1, G):
                    s.link(eng.tensor_tensor(ge[:, :, 0:G - d], p[:, :, 0:G - d], p[:, :, d:G], ALU.is_ge))
                    s.link(eng.tensor_tensor(rk[:, :, d:G], rk[:, :, d:G], ge[:, :, 0:G - d], ALU.add))
                    s.link(eng.tensor_tensor(rk[:, :, 0:G - d], rk[:, :, 0:G - d], ge[:, :, 0:G - d], ALU.subtract))
                s.link(eng.tensor_scalar(rk[:], rk[:], 2.0, None, ALU.is_lt))
                s.link(eng.tensor_tensor(wg[:], rk[:], p, ALU.mult))
                s.link(eng.tensor_reduce(mm[:, :, 0:1], wg[:], X, ALU.add))
                s.link(eng.tensor_reduce(mm[:, :, 1:1 + G], pairs, X, ALU.max))
                s.link(eng.tensor_tensor(ge[:], pairs[:, :, :, 0], pairs[:, :, :, 1], ALU.is_ge))
                s.link(eng.tensor_copy(rk[:], mm[:, :, 1:1 + G]))
                s.link(eng.tensor_scalar(mm[:], mm[:], TOP_EPS, None, ALU.add))
                s.link(eng.reciprocal(mm[:], mm[:]))
                s.link(eng.tensor_tensor(rk[:], rk[:], mm[:, :, 1:1 + G], ALU.mult))
                s.link(eng.tensor_tensor(wg[:], wg[:], mm[:, :, 0:1].to_broadcast([P, BT, G]), ALU.mult))
                s.link(eng.tensor_tensor(wg[:], wg[:], rk[:], ALU.mult))
                if r:
                    dve.wait_ge(misc_full, index[("turn_c", r - 1)] + 1)
                c4 = [c40[:, :, o:o + E].rearrange("p t (g m) -> p t g m", m=2) for o in (0, 32)]
                s.link(eng.tensor_tensor(c4[0][:, :, :, 0], wg[:], ge[:], ALU.mult))
                s.link(eng.tensor_tensor(c4[0][:, :, :, 1], wg[:], c4[0][:, :, :, 0], ALU.subtract))
                eng.tensor_copy(c40[:, :, 32:32 + E], c40[:, :, 0:E]).then_inc(c_ready, 1)

            def steps_at(r, k):
                n = r + 1
                blk = n % NB
                for it in items_at(r, k):
                    if it[0] not in ("x", "logits", "turn_l", "turn_c"):
                        give(it)
                if k == 3 and n < NB:
                    dve.wait_ge(x1_ready, n + 1)
                    for t in range(BT):
                        s.link(eng.bn_stats(st6[:], z[:, BT * n + t, :]))
                        s.link(eng.bn_aggr(mv[:, t, :], st6[:]))
                    root(0, ln_var, (1.0, LN_EPS))
                if k == 7 and n < NB:
                    root_end(0, ln_std, n + 1)
                    dve.wait_ge(x1_out, 16 * (n + 1))
                    for t in range(BT):
                        zt = z[:, BT * n + t, :]
                        s.mark(eng.tensor_scalar(zt, zt, mv[:, t, 0:1], sd[:, 0, t:t + 1], ALU.subtract, ALU.mult))
                    dve.wait_ge(dve_steps, s.n)
                if n >= NR:
                    return
                if k == 8:
                    if r >= 1:
                        dve.wait_ge(misc_full, index[("z", r - 1, 1)] + 1)
                        dve.wait_ge(misc_free, index[("z", r - 1, 1)] + 1)
                    if n < NB:
                        dve.wait_ge(misc_full, index[("proj", n, 1)] + 1)
                    for t in range(BT):
                        zt = z[:, BT * blk + t, :]
                        s.link(eng.tensor_tensor(xn[:, t, :], zt, zt, ALU.mult))
                    s.link(eng.tensor_reduce(mv[:, :, 1], xn, X, ALU.add))
                    root(1, rms_var, (1.0 / D, RMS_EPS))
                if k == 10:
                    root_end(1, rms_std, n + 1)
                    for t in range(BT):
                        o = eng.scalar_tensor_tensor(xn[:, t, :], z[:, BT * blk + t, :], sd[:, 1, t:t + 1], norm_w,
                                                     ALU.mult, ALU.mult)
                        s.mark(o) if t < BT - 1 else o.then_inc(xn_ready, 1)
                if k == 13:
                    for c in range(DC):
                        give(("x", n, c))
                if k == 15:
                    give(("logits", n))
                if k == 17:
                    give(("turn_l", n))
                if k == 19:
                    combine(n)
                if k == 30:
                    give(("turn_c", n))

            def combined(kk):
                dve.wait_ge(silu_done, kk + 1)
                dve.wait_ge(cb_full, kk // FC + 1)
                h = hs[:, kk % HB, :]
                eng.tensor_tensor(h, h, cb[:], ALU.mult).then_inc(hc_done, 1)

            def low(kk):
                dve.wait_ge(hi_done, kk + 1)
                eng.tensor_tensor(hl[:, kk % SB, :], hs[:, kk % HB, :], hh[:, kk % SB, :].bitcast(F32),
                                  ALU.subtract).then_inc(lo_done, 1)

            dve.wait_ge(router_in, 16)
            s.link(eng.memset(wr[:].bitcast(F32), 0.0))
            s.link(eng.tensor_copy(wr[:, :, 0:NE12], wr_f[:]))
            eng.tensor_tensor(wr[:, :, 32:LR], wr_f[:], wr[:, :, 0:NE12].bitcast(F32),
                              ALU.subtract).then_inc(router_ready, 1)
            dve.wait_ge(consts, 1)
            for k in range(KS):
                steps_at(-1, k)
            for kk in range(NR * KS + 1):
                r, k = divmod(kk, KS)
                if kk < NR * KS:
                    steps_at(r, k)
                    combined(kk)
                if kk:
                    low(kk - 1)
            for it in items_at(NR, 6):
                give(it)


def load_piece(nc, engine, stage, w1T, w2T, pieces, i, stage_in):
    w, e, c = pieces[i]
    if w == 1:
        src = w1T[c * P:(c + 1) * P, e, :]
        dst = stage[:, i % 2, :]
    else:
        src = w2T[2 * c * P:(2 * c + 2) * P, e, :].rearrange("(a p) d -> p a d", p=P)
        dst = stage[:, i % 2, :].rearrange("p (a d) -> p a d", a=2)
    engine.dma_start(dst, src).then_inc(stage_in[i % 2], 16)

def kernel(**inputs):
    import numpy as _np
    import concourse.bacc as _bacc
    from concourse import mybir as _mybir
    from concourse.bass_utils import run_bass_kernel_spmd as _run

    arrays = laid_out(_np, inputs)
    nc = _bacc.Bacc("TRN2", target_bir_lowering=False, num_devices=1)
    args = {name: nc.dram_tensor(f"in_{name}", a.shape, _mybir.dt.from_np(a.dtype), kind="ExternalInput").ap()
            for name, a in arrays.items()}
    out = nc.dram_tensor("out_x", (B * T, D), F32, kind="ExternalOutput").ap()
    build(nc, out=out, **args)
    r = _run(nc, [{f"in_{name}": a for name, a in arrays.items()}], core_ids=[0])
    return r.results[0]["out_x"].reshape(B, T, D)


def laid_out(np, inputs):
    i = {name: np.asarray(a) for name, a in inputs.items()}
    c = np.ascontiguousarray
    rows = [i[n].reshape(-1) for n in (
        "L0_xattn_proj_b", "L0_ffn_norm_w", "L0_xattn_hist_b", "L0_xattn_hist_ln_g", "L0_xattn_hist_ln_b",
        "L0_xattn_ctx_b1", "L0_xattn_ctx_W2", "L0_xattn_ctx_b2", "L0_xattn_kg_b1", "L0_xattn_kg_ln_g",
        "L0_xattn_kg_ln_b", "L0_xattn_kg_b2")]
    router = np.concatenate([i["L0_ffn_w_macro"], i["L0_ffn_w_micro"].reshape(E, D)], axis=0)
    return {
        "x": c(i["x"].reshape(B * T, D)),
        "ctxT": c(i["ctx_1024"].reshape(NCT * S2, D).T),
        "hist_W": c(i["L0_xattn_hist_W"]), "ctx_W1": c(i["L0_xattn_ctx_W1"]),
        "kg_W1": c(i["L0_xattn_kg_W1"]), "kg_W2": c(i["L0_xattn_kg_W2"]),
        "Wq": c(i["L0_xattn_Wq"]), "Wk": c(i["L0_xattn_Wk"]), "Wv": c(i["L0_xattn_Wv"]),
        "proj_W": c(i["L0_xattn_proj_W"]),
        "vecs": c(np.concatenate(rows).reshape(1, NVEC)),
        "wrT": c(router.T),
        "mask": c(i["mask_SxS_bc0"]).view(np.int32),
        "w1T": c(i["L0_ffn_w1"].transpose(2, 0, 1)),
        "w2T": c(i["L0_ffn_w2"].transpose(2, 0, 1)),
    }
```

```python
from contextlib import ExitStack

import concourse.bass as bass
from concourse import mybir

ALU = mybir.AluOpType
ACT = mybir.ActivationFunctionType
F32 = mybir.dt.float32
F32R = mybir.dt.float32r
BF16 = mybir.dt.bfloat16
X = mybir.AxisListType.X

P = 128
B, T, D = 2, 1024, 256
H, HD = 16, 16
DC = D // P
NT = B * T // P
TB = T // P
LPAD, RPAD = 3, 1
W = LPAD + T + RPAD
TAPS = 9
S2, CW = 77, 512
NCT = 4
UH = 8
NU = 2 * B
GH = 4
NG = NU * UH // GH
QB = 512
NQB = T // QB
VW = HD + 1
KROWS = 3 * HD
MROW = 2 * KROWS
BIG = 1.0e30
E, F, GROUPS = 8, 512, 4
FC = F // P
LOOPS = 2
NTILE = (2 * T + E * (P - 1)) // P
LN_AT, GATHER_AT, RMS_AT, X_AT = 4, 4, 8, 9
LN_EPS, RMS_EPS, TOP_EPS = 1e-5, 1e-6, 1e-9

VEC = {}
_at = 0
for _name, _n in (("proj_b", D), ("norm_w", D), ("hist_b", CW), ("hist_g", CW), ("hist_beta", CW),
                  ("ctx_b1", CW // 4), ("ctx_W2", CW // 4), ("ctx_b2", 1), ("kg_b1", D), ("kg_g", D),
                  ("kg_beta", D), ("kg_b2", H * TAPS)):
    VEC[_name] = (_at, _at + _n)
    _at += _n
NVEC = _at
NKEEP = VEC["norm_w"][1]


class Steps:

    def __init__(self, engine, sem):
        self.engine, self.sem, self.n = engine, sem, 0

    def mark(self, ins):
        ins.then_inc(self.sem, 1)
        self.n += 1
        return self.n

    def link(self, ins):
        self.mark(ins)
        self.engine.wait_ge(self.sem, self.n)


def qblock_items():
    return [(qb, kt) for qb in range(NQB) for kt in range((qb + 1) * QB // P)]


ITEMS = qblock_items()
NI = len(ITEMS)
HALF_SLOTS = 6
DIAG_AT = 1
FIRST_MAX, LAST_MAX = 2, NI - 3
CHUNKS = [(h, qt, c) for h in range(GH) for qt in range(TB) for c in range((qt * P) // QB + 1)]


def chunk_column(qt, c):
    return qt if c == 0 else TB + qt - QB // P


def load_keys(sp, K, ks_d, u, h, slot, loaded):
    r = HD * h
    for part in range(2):
        base = ks_d[part, u, r:r + HD, LPAD - 1:LPAD - 1 + T]
        src = bass.AP(base.tensor, base.offset, [[W, HD], [1, 3], [1, T]])
        sp.dma_start(K[part * KROWS:(part + 1) * KROWS, slot, :].bitcast(F32), src).then_inc(loaded, 16)


def build(nc, x, ctxT, hist_W, ctx_W1, kg_W1, kg_W2, Wq, Wk, Wv, proj_W, vecs, wrT, w1T, w2T, mask, out):
    kern_d = nc.dram_tensor("kern_scratch", (B, H * TAPS), F32, kind="Internal").ap()
    qs_d = nc.dram_tensor("q_parts_scratch", (2, NU, P, 3, T), F32, kind="Internal").ap()
    ks_d = nc.dram_tensor("k_parts_scratch", (2, NU, P, W), F32, kind="Internal").ap()
    ao_d = nc.dram_tensor("attn_scratch", (B * T, D), F32, kind="Internal").ap()
    qk_d = nc.dram_tensor("general_qk_scratch", (2, NU * P, W), F32, kind="Internal").ap()
    v_d = nc.dram_tensor("general_v_scratch", (B * H, P, TB, HD), F32, kind="Internal").ap()
    oh_d = nc.dram_tensor("general_out_scratch", (B * H, P, TB, HD), F32, kind="Internal").ap()
    x1_d = nc.dram_tensor("residual_scratch", (B * T, D), F32, kind="Internal").ap()
    xdisp_d, ydisp_d = ([nc.dram_tensor(f"{n}_sorted{b}", (NTILE * P, D), F32, kind="Internal").ap() for b in range(B)]
                        for n in ("x", "y"))

    with ExitStack() as whole:
        def sem(name):
            return whole.enter_context(nc.semaphore(name))

        def keep(name, shape, dt=F32):
            return whole.enter_context(nc.sbuf_tensor(name, shape, dt))

        ident = keep("ident", [P, P])
        vkeep = keep("vkeep", [P, NKEEP])
        ones = keep("ones", [P, 1])
        const_ready = sem("const_ready")
        vkeep_in = sem("vkeep_in")

        with ExitStack() as two:
            def sb2(name, shape, dt=F32):
                return two.enter_context(nc.sbuf_tensor(name, shape, dt))

            qT = sb2("qT", [P, NU, W])
            kT = sb2("kT", [P, NU, W])
            vaug = sb2("vaug", [P, NT * H * VW + 32])
            vaug_t = vaug[:, 0:NT * H * VW].rearrange("p (t h e) -> p t h e", t=NT, h=H)
            mask_flag = sb2("mask_flag", [1, 1], mybir.dt.int32)
            kerP = sb2("kerP", [P, NU, TAPS])
            identb = sb2("identb", [P, P], BF16)
            mask_q = sb2("mask_q", [P, P + 2], BF16)
            mask_k = sb2("mask_k", [P, P + 2], BF16)
            first_neg = sb2("first_neg", [P, 1])
            sumsel = sb2("sumsel", [P, UH])
            khi, klo = (sb2(n, [P, W], F32R) for n in ("khi", "klo"))
            K = sb2("K", [MROW + 1, 2 * GH, T], F32R)
            consts = (identb, mask_q, mask_k, first_neg, sumsel)
            block1(nc, sem, ident, ones, vkeep, const_ready, vkeep_in, qT, kT, vaug, vaug_t, kerP,
                   consts, khi, klo, K, xdisp_d, ks_d, kern_d, x, ctxT, hist_W, ctx_W1, kg_W1, kg_W2, Wq, Wk, Wv, vecs, mask, mask_flag)
            other_mask = nc.values_load(mask_flag[0:1, 0:1], min_val=0, max_val=P)
            with nc.If(other_mask > 0):
                general_attention(nc, sem, ident, qT, kT, vaug_t, mask, kern_d, qk_d, v_d, oh_d, ao_d)
            with nc.Else():
                block2(nc, sem, ident, qT, kT, vaug, vaug_t, kerP, consts, khi, klo, K, qs_d, ks_d, ao_d)
        block3(nc, sem, ident, vkeep, x, ao_d, x1_d, xdisp_d, ydisp_d, proj_W, wrT, w1T, w2T, out)

def block1(nc, sem, ident, ones, vkeep, const_ready, vkeep_in, qT, kT, vaug, vaug_t, kerP,
           consts, khi, klo, K, xdisp_d, ks_d, kern_d, x, ctxT, hist_W, ctx_W1, kg_W1, kg_W2, Wq, Wk, Wv, vecs, mask, mask_flag):
    identb, mask_q, mask_k, first_neg, sumsel = consts
    with ExitStack() as ctx:
        def sb(name, shape, dt=F32):
            return ctx.enter_context(nc.sbuf_tensor(name, shape, dt))

        x_sb = sb("x_sb", [P, NT, D])
        xnT = sb("xnT", [P, DC, NT * P])
        ctx_sb = sb("ctx_sb", [P, DC, NCT * S2])
        hist_w = sb("hist_w", [P, DC, CW])
        ctx_w1 = sb("ctx_w1", [P, CW // P, CW // 4])
        kg_w1 = sb("kg_w1", [P, CW // P, D])
        kg_w2 = sb("kg_w2", [P, DC, H * TAPS])
        wq, wk, wv = (sb(n, [P, DC, D]) for n in ("wq", "wk", "wv"))
        vrow = sb("vrow", [P, NVEC])
        stats = sb("stats", [P, 6])
        mv = sb("mv", [P, NT, 2])
        rstd = sb("rstd", [P, NT])
        tmpn = sb("tmpn", [P, NT])
        eh = sb("eh", [S2, NCT, CW])
        estats = sb("estats", [S2, 6])
        emv = sb("emv", [S2, NCT, 2])
        erstd = sb("erstd", [S2, NCT])
        ehT = sb("ehT", [P, NCT, CW // P, S2])
        ag = sb("ag", [S2, NCT, CW // 4])
        awc = sb("awc", [S2, NCT])
        awr = sb("awr", [1, B, 2 * S2])
        aws = sb("aws", [1, 4 * B])
        ccT = sb("ccT", [P, CW // P, B])
        kg = sb("kg", [B, D])
        kstats = sb("kstats", [B, 8])
        kgT = sb("kgT", [P, DC, B])
        kp = sb("kp", [B, H, TAPS])
        ks = sb("ks", [B, 2 * H])
        mask_words = sb("mask_words", [P, TB, T // 4], mybir.dt.int32)
        causal = sb("causal", [P, 2 * T], BF16)
        differs = sb("differs", [P, T], BF16)
        diff_max = sb("diff_max", [P, TB + 1])
        zeros = sb("zeros", [P, D])
        banks = [ctx.enter_context(nc.psum_tensor(f"work{i}", [P, 512], F32)) for i in range(4)]
        cbank = [ctx.enter_context(nc.psum_tensor(f"ctxb{i}", [P, 512], F32)) for i in range(4)]

        dve_steps, pool_steps = sem("dve_steps"), sem("pool_steps")
        x_in = [sem(f"x_in{i}") for i in range(4)]
        hist_in, cw_in, qkv_in, vrow_in = sem("hist_in"), sem("cw_in"), sem("qkv_in"), sem("vrow_in")
        pads_ready = sem("pads_ready")
        mask_in, causal_ready, diff_ready, flag_ready = (sem(n) for n in (
            "mask_in", "causal_ready", "diff_ready", "flag_ready"))
        xvar_ready, xstd_ready, xn_ready = sem("xvar_ready"), sem("xstd_ready"), sem("xn_ready")
        work_full, work_free = sem("work_full"), sem("work_free")
        ctx_pe, ctx_dve, ctx_act = sem("ctx_pe"), sem("ctx_dve"), sem("ctx_act")
        kern_out, kern_in = sem("kern_out"), sem("kern_in")
        zeros_ready, cleared = sem("zeros_ready"), sem("cleared")
        khilo_ready, k_out, k0_in = sem("khilo_ready1"), sem("k_out1"), sem("k0_in")

        ring = [("xT", c, n) for n in range(4) for c in range(DC)]
        ring += [("qk", which, u, blk) for u in range(NU) for which in range(2) for blk in range(2)]
        ring += [("v", t) for t in range(NT)]
        before_keys = ring.index(("qk", 1, 0, 1)) + 1
        before = [0, 12, 16, 22, 25, 27, 29, 31]

        block = ctx.enter_context(nc.Block())

        def vec(name, rows):
            a, b = VEC[name]
            return vrow[0:rows, a:b]

        @block.sync
        def _(sp):
            sp.dma_start(ctx_sb[:], ctxT.rearrange("(c p) s -> p c s", p=P)).then_inc(hist_in, 16)
            sp.dma_start(hist_w[:], hist_W.rearrange("(c p) n -> p c n", p=P)).then_inc(hist_in, 16)
            for n in range(4):
                src = x[n * 512:(n + 1) * 512, :].rearrange("(t p) d -> p t d", p=P)
                sp.dma_start(x_sb[:, 4 * n:4 * n + 4, :], src).then_inc(x_in[n], 16)
            sp.dma_start(vrow[:], vecs.partition_broadcast(P)).then_inc(vrow_in, 16)
            for w, dram in ((wq, Wq), (wk, Wk), (wv, Wv)):
                sp.dma_start(w[:], dram.rearrange("(c p) n -> p c n", p=P)).then_inc(qkv_in, 16)
            for w, dram in ((ctx_w1, ctx_W1), (kg_w1, kg_W1), (kg_w2, kg_W2)):
                sp.dma_start(w[:], dram.rearrange("(c p) n -> p c n", p=P)).then_inc(cw_in, 16)
            sp.dma_start(mask_words[:], mask.rearrange("(t p) k -> p t k", p=P)).then_inc(mask_in, 16)
            sp.wait_ge(zeros_ready, 1)
            for b in range(B):
                sp.dma_start(xdisp_d[b].rearrange("(i p) d -> p i d", p=P),
                             zeros[:].unsqueeze(1).to_broadcast([P, NTILE, D])).then_inc(cleared, 16)
            sp.wait_ge(khilo_ready, 2)
            for part, t in enumerate((khi, klo)):
                sp.dma_start(ks_d[part, 0], t[:].bitcast(F32)).then_inc(k_out, 16)
            sp.wait_ge(k_out, 32)
            for h in range(UH):
                load_keys(sp, K, ks_d, 0, h, h, k0_in)
            sp.wait_ge(ctx_dve, 12)
            sp.dma_start(kern_d, kp[:].rearrange("b h t -> b (h t)")).then_inc(kern_out, 16)
            sp.wait_ge(kern_out, 16)
            for u in range(NU):
                b, half = divmod(u, 2)
                row = kern_d[b:b + 1, half * UH * TAPS:(half + 1) * UH * TAPS]
                src = bass.AP(row.tensor, row.offset, [[TAPS, UH], [0, HD], [1, TAPS]])
                sp.dma_start(kerP[:, u, :], src).then_inc(kern_in, 16)
            sp.wait_ge(kern_in, 16 * NU)
            sp.wait_ge(k0_in, 16 * 2 * UH)
            sp.wait_ge(cleared, 16 * B)

        @block.gpsimd
        def _(pool):
            nc.gpsimd.memset(ident[:], 0.0).then_inc(pool_steps, 1)
            pool.wait_ge(pool_steps, 1)
            nc.gpsimd.affine_select(out=ident[:], in_=ident[:], compare_op=ALU.not_equal, fill=1.0, base=0,
                                    pattern=[[-1, P]], channel_multiplier=1).then_inc(const_ready, 1)
            nc.gpsimd.memset(ones[:], 1.0).then_inc(const_ready, 1)
            nc.gpsimd.memset(zeros[:], 0.0).then_inc(zeros_ready, 1)
            nc.gpsimd.memset(vaug[:], 1.0).then_inc(pads_ready, 1)
            for t in (qT, kT):
                nc.gpsimd.memset(t[:, :, 0:LPAD], 0.0).then_inc(pads_ready, 1)
                nc.gpsimd.memset(t[:, :, LPAD + T:W], 0.0).then_inc(pads_ready, 1)
            nc.gpsimd.memset(causal[:], 0.0).then_inc(pool_steps, 1)
            pool.wait_ge(pool_steps, 2)
            nc.gpsimd.affine_select(out=causal[:], in_=causal[:], compare_op=ALU.is_ge, fill=1.0, base=T,
                                    pattern=[[-1, 2 * T]], channel_multiplier=1).then_inc(causal_ready, 1)
            s = Steps(pool, pool_steps)
            s.n = 2
            pool.wait_ge(const_ready, 1)
            nc.gpsimd.tensor_copy(identb[:], ident[:])
            for m in (mask_q, mask_k, first_neg, sumsel):
                s.mark(nc.gpsimd.memset(m[:], 1.0 if m is sumsel else 0.0))
            pool.wait_ge(pool_steps, s.n)
            nc.gpsimd.affine_select(out=mask_q[:], in_=mask_q[:], compare_op=ALU.is_ge, fill=-BIG, base=0,
                                    pattern=[[-1, P + 2]], channel_multiplier=1)
            nc.gpsimd.affine_select(out=mask_k[:], in_=mask_k[:], compare_op=ALU.is_ge, fill=-BIG, base=-2,
                                    pattern=[[1, P + 2]], channel_multiplier=-1)
            nc.gpsimd.affine_select(out=first_neg[:], in_=first_neg[:], compare_op=ALU.is_ge, fill=-BIG, base=-1,
                                    pattern=[[0, 1]], channel_multiplier=1)
            s.link(nc.gpsimd.affine_select(out=sumsel[:], in_=sumsel[:], compare_op=ALU.is_ge, fill=0.0, base=0,
                                           pattern=[[-HD, UH]], channel_multiplier=1))
            s.link(nc.gpsimd.affine_select(out=sumsel[:], in_=sumsel[:], compare_op=ALU.is_ge, fill=0.0, base=HD - 1,
                                    pattern=[[HD, UH]], channel_multiplier=-1))
            for h in range(0, 2 * GH, GH):
                s.link(nc.gpsimd.memset(K[MROW:MROW + 1, h:h + GH, :].bitcast(F32), 1.0))
            pool.wait_ge(work_free, before_keys)
            pool.wait_ge(pads_ready, 5)
            nc.gpsimd.tensor_copy(khi[:], kT[:, 0, :]).then_inc(khilo_ready, 1)
            pool.wait_ge(khilo_ready, 1)
            nc.gpsimd.tensor_tensor(klo[:], kT[:, 0, :], khi[:].bitcast(F32), ALU.subtract).then_inc(khilo_ready, 1)

        @block.tensor
        def _(pe):
            pe.wait_ge(const_ready, 2)
            done = [0]

            def take():
                i = done[0]
                done[0] += 1
                bank = banks[i % 4]
                item = ring[i]
                if i >= 4:
                    pe.wait_ge(work_free, i - 3)
                if item[0] == "xT":
                    _, c, n = item
                    pe.wait_ge(xn_ready, 4 * n + 4)
                    for k in range(4):
                        last = nc.tensor.transpose(bank[:, k * P:(k + 1) * P],
                                                   x_sb[:, 4 * n + k, c * P:(c + 1) * P], ident[:])
                elif item[0] == "qk":
                    _, which, u, blk = item
                    b, half = divmod(u, 2)
                    if i == 8:
                        pe.wait_ge(qkv_in, 48)
                        pe.wait_ge(work_free, 8)
                    t0 = b * T + blk * QB
                    for c in range(DC):
                        last = nc.tensor.matmul(bank[:], (wq, wk)[which][:, c, half * P:(half + 1) * P],
                                                xnT[:, c, t0:t0 + QB], start=(c == 0), stop=(c == DC - 1))
                else:
                    t = item[1]
                    for c in range(DC):
                        last = nc.tensor.matmul(bank[:, 0:D], xnT[:, c, t * P:(t + 1) * P], wv[:, c, :],
                                                start=(c == 0), stop=(c == DC - 1))
                last.then_inc(work_full, 1)

            def ring_to(n):
                while done[0] < n:
                    take()

            pe.wait_ge(hist_in, 32)
            for t in range(NCT):
                for c in range(DC):
                    last = nc.tensor.matmul(cbank[t][0:S2, :], ctx_sb[:, c, t * S2:(t + 1) * S2],
                                            hist_w[:, c, :], start=(c == 0), stop=(c == DC - 1))
            last.then_inc(ctx_pe, 1)
            ring_to(before[1])
            pe.wait_ge(ctx_act, 2)
            for t in range(NCT):
                for c in range(CW // P):
                    last = nc.tensor.transpose(cbank[t][:, c * S2:(c + 1) * S2], eh[:, t, c * P:(c + 1) * P],
                                               ident[0:S2, 0:S2])
            last.then_inc(ctx_pe, 1)
            ring_to(before[2])
            pe.wait_ge(ctx_dve, 3)
            pe.wait_ge(cw_in, 48)
            for t in range(NCT):
                for c in range(CW // P):
                    last = nc.tensor.matmul(cbank[0][0:S2, t * P:(t + 1) * P], ehT[:, t, c, :],
                                            ctx_w1[:, c, :], start=(c == 0), stop=(c == CW // P - 1))
            last.then_inc(ctx_pe, 1)
            ring_to(before[3])
            pe.wait_ge(ctx_dve, 5)
            for t in range(NCT):
                last = nc.tensor.matmul(cbank[1][0:1, t * S2:(t + 1) * S2], awc[:, t:t + 1],
                                        ident[0:S2, 0:S2], start=True, stop=True)
            last.then_inc(ctx_pe, 1)
            ring_to(before[4])
            pe.wait_ge(diff_ready, 1)
            nc.tensor.matmul(cbank[0][0:1, 0:1], diff_max[:, TB:TB + 1], ones[:], start=True,
                             stop=True).then_inc(flag_ready, 1)
            pe.wait_ge(ctx_dve, 7)
            for t in range(NCT):
                b, part = divmod(t, 2)
                last = nc.tensor.matmul(cbank[2][0:S2, t:t + 1], awr[0:1, b, part * S2:(part + 1) * S2],
                                        ones[0:1, 0:1], start=True, stop=True)
            last.then_inc(ctx_pe, 1)
            pe.wait_ge(ctx_dve, 8)
            for c in range(CW // P):
                for t in range(NCT):
                    b, part = divmod(t, 2)
                    last = nc.tensor.matmul(cbank[3][:, c * B + b:c * B + b + 1], eh[:, t, c * P:(c + 1) * P],
                                            awc[:, t:t + 1], start=(part == 0), stop=(part == 1))
            last.then_inc(ctx_pe, 1)
            ring_to(before[5])
            pe.wait_ge(flag_ready, 2)
            pe.wait_ge(ctx_act, 5)
            for c in range(CW // P):
                last = nc.tensor.matmul(cbank[0][0:B, 0:D], ccT[:, c, :], kg_w1[:, c, :],
                                        start=(c == 0), stop=(c == CW // P - 1))
            last.then_inc(ctx_pe, 1)
            ring_to(before[6])
            pe.wait_ge(ctx_act, 7)
            for c in range(DC):
                last = nc.tensor.transpose(cbank[1][:, c * B:(c + 1) * B], kg[:, c * P:(c + 1) * P],
                                           ident[0:B, 0:B])
            last.then_inc(ctx_pe, 1)
            pe.wait_ge(ctx_act, 8)
            for c in range(DC):
                last = nc.tensor.matmul(cbank[2][0:B, 0:H * TAPS], kgT[:, c, :], kg_w2[:, c, :],
                                        start=(c == 0), stop=(c == DC - 1))
            last.then_inc(ctx_pe, 1)
            ring_to(len(ring))

        @block.scalar
        def _(act):
            done = [0]

            def take():
                i = done[0]
                done[0] += 1
                bank, item = banks[i % 4], ring[i]
                act.wait_ge(work_full, i + 1)
                if item[0] == "xT":
                    _, c, n = item
                    ins = nc.scalar.copy(xnT[:, c, n * 512:(n + 1) * 512], bank[:])
                elif item[0] == "qk":
                    _, which, u, blk = item
                    if i == 8:
                        act.wait_ge(pads_ready, 5)
                    dst = (qT, kT)[which][:, u, LPAD + blk * QB:LPAD + (blk + 1) * QB]
                    ins = nc.scalar.mul(dst, bank[:], HD ** -0.5 if which == 0 else 1.0)
                else:
                    t = item[1]
                    ins = nc.scalar.copy(vaug_t[:, t, :, 0:HD], bank[:, 0:D].rearrange("p (h d) -> p h d", d=HD))
                ins.then_inc(work_free, 1)

            def ring_to(n):
                while done[0] < n:
                    take()

            act.wait_ge(xvar_ready, 1)
            nc.scalar.activation(rstd[:], tmpn[:], ACT.Sqrt).then_inc(xstd_ready, 1)
            act.wait_ge(ctx_dve, 1)
            nc.scalar.activation(erstd[:], erstd[:], ACT.Sqrt).then_inc(ctx_act, 1)
            ring_to(8)
            act.wait_ge(ctx_dve, 2)
            nc.scalar.activation(eh[:], eh[:], ACT.Gelu).then_inc(ctx_act, 1)
            ring_to(before[2] + 2)
            act.wait_ge(ctx_dve, 4)
            nc.scalar.activation(ag[:], ag[:], ACT.Gelu).then_inc(ctx_act, 1)
            ring_to(before[3] + 2)
            act.wait_ge(ctx_dve, 6)
            nc.scalar.activation(awr[:], awr[:], ACT.Exp).then_inc(ctx_act, 1)
            ring_to(before[4])
            act.wait_ge(ctx_pe, 6)
            nc.scalar.copy(ccT[:], cbank[3][:, 0:CW // P * B].rearrange("p (c b) -> p c b", b=B)).then_inc(ctx_act, 1)
            ring_to(before[5])
            act.wait_ge(ctx_dve, 9)
            nc.scalar.activation(kstats[:, 7:8], kstats[:, 7:8], ACT.Sqrt).then_inc(ctx_act, 1)
            act.wait_ge(ctx_dve, 10)
            nc.scalar.activation(kg[:], kg[:], ACT.Gelu).then_inc(ctx_act, 1)
            ring_to(before[6])
            act.wait_ge(ctx_pe, 8)
            nc.scalar.copy(kgT[:], cbank[1][:, 0:DC * B].rearrange("p (c b) -> p c b", b=B)).then_inc(ctx_act, 1)
            act.wait_ge(ctx_dve, 11)
            nc.scalar.activation(kp[:], kp[:], ACT.Exp).then_inc(ctx_act, 1)
            ring_to(len(ring))

        @block.vector
        def _(dve):
            s = Steps(dve, dve_steps)

            def compare_mask(a, b_):
                for t in range(a, b_):
                    if t == 0:
                        dve.wait_ge(mask_in, 16)
                        dve.wait_ge(causal_ready, 1)
                    rows = mask_words[:, t, :].bitcast(mybir.dt.uint8)
                    s.link(nc.vector.tensor_tensor(differs[:], rows, causal[:, T - t * P:2 * T - t * P],
                                                   ALU.not_equal))
                    s.link(nc.vector.tensor_reduce(diff_max[:, t:t + 1], differs[:], X, ALU.max))

            for t in range(NT):
                if t % 4 == 0:
                    dve.wait_ge(x_in[t // 4], 16)
                s.link(nc.vector.bn_stats(stats[:], x_sb[:, t, :]))
                s.link(nc.vector.bn_aggr(mv[:, t, :], stats[:]))
            nc.vector.tensor_scalar(tmpn[:], mv[:, :, 1], LN_EPS, None, ALU.add).then_inc(xvar_ready, 1)
            dve.wait_ge(xstd_ready, 1)
            s.link(nc.vector.reciprocal(rstd[:], rstd[:]))
            newton(nc, s, rstd[:], tmpn[:])
            for t in range(NT):
                nc.vector.tensor_scalar(x_sb[:, t, :], x_sb[:, t, :], mv[:, t, 0:1], rstd[:, t:t + 1],
                                        ALU.subtract, ALU.mult).then_inc(xn_ready, 1)
            dve.wait_ge(ctx_pe, 1)
            dve.wait_ge(vrow_in, 16)
            for t in range(NCT):
                s.mark(nc.vector.tensor_tensor(eh[:, t, :], cbank[t][0:S2, :], vec("hist_b", S2), ALU.add))
            for t in range(NCT):
                dve.wait_ge(dve_steps, s.n)
                s.link(nc.vector.bn_stats(estats[:], eh[:, t, :]))
                s.link(nc.vector.bn_aggr(emv[:, t, :], estats[:]))
            s.link(nc.vector.tensor_scalar(emv[:, :, 1], emv[:, :, 1], LN_EPS, None, ALU.add))
            nc.vector.tensor_copy(erstd[:], emv[:, :, 1]).then_inc(ctx_dve, 1)
            dve.wait_ge(ctx_act, 1)
            s.link(nc.vector.reciprocal(erstd[:], erstd[:]))
            newton(nc, s, erstd[:], emv[:, :, 1])
            for t in range(NCT):
                s.mark(nc.vector.tensor_scalar(eh[:, t, :], eh[:, t, :], emv[:, t, 0:1], erstd[:, t:t + 1],
                                               ALU.subtract, ALU.mult))
            dve.wait_ge(dve_steps, s.n)
            for t in range(NCT):
                s.mark(nc.vector.tensor_tensor(eh[:, t, :], eh[:, t, :], vec("hist_g", S2), ALU.mult))
            dve.wait_ge(dve_steps, s.n)
            for t in range(NCT):
                last = nc.vector.tensor_tensor(eh[:, t, :], eh[:, t, :], vec("hist_beta", S2), ALU.add)
                s.mark(last) if t < NCT - 1 else last.then_inc(ctx_dve, 1)
            compare_mask(0, 4)
            dve.wait_ge(ctx_pe, 2)
            for t in range(NCT):
                last = nc.vector.tensor_copy(ehT[:, t, :, :].rearrange("p c s -> p (c s)"), cbank[t][:, 0:CW // P * S2])
                s.mark(last) if t < NCT - 1 else last.then_inc(ctx_dve, 1)
            dve.wait_ge(ctx_pe, 3)
            b1 = vec("ctx_b1", S2).unsqueeze(1).to_broadcast([S2, NCT, CW // 4])
            nc.vector.tensor_tensor(ag[:], cbank[0][0:S2, :].rearrange("p (t n) -> p t n", t=NCT), b1,
                                    ALU.add).then_inc(ctx_dve, 1)
            compare_mask(4, TB)
            nc.vector.tensor_reduce(diff_max[:, TB:TB + 1], diff_max[:, 0:TB], X, ALU.max).then_inc(diff_ready, 1)
            dve.wait_ge(ctx_act, 3)
            w2 = vec("ctx_W2", S2).unsqueeze(1).to_broadcast([S2, NCT, CW // 4])
            s.link(nc.vector.tensor_tensor(ag[:], ag[:], w2, ALU.mult))
            s.link(nc.vector.tensor_reduce(awc[:], ag[:], X, ALU.add))
            nc.vector.tensor_scalar(awc[:], awc[:], vec("ctx_b2", S2), None, ALU.add).then_inc(ctx_dve, 1)
            dve.wait_ge(ctx_pe, 4)
            scores = cbank[1][0:1, 0:NCT * S2].rearrange("p (b s) -> p b s", b=B)
            s.link(nc.vector.tensor_reduce(aws[:, 0:B], scores, X, ALU.max))
            nc.vector.tensor_tensor(awr[:], scores, aws[:, 0:B].unsqueeze(2).to_broadcast([1, B, 2 * S2]),
                                    ALU.subtract).then_inc(ctx_dve, 1)
            dve.wait_ge(flag_ready, 1)
            nc.vector.tensor_copy(mask_flag[:], cbank[0][0:1, 0:1]).then_inc(flag_ready, 1)
            dve.wait_ge(ctx_act, 4)
            s.link(nc.vector.tensor_reduce(aws[:, B:2 * B], awr[:], X, ALU.add))
            s.link(nc.vector.reciprocal(aws[:, 2 * B:3 * B], aws[:, B:2 * B]))
            nc.vector.tensor_tensor(awr[:], awr[:], aws[:, 2 * B:3 * B].unsqueeze(2).to_broadcast([1, B, 2 * S2]),
                                    ALU.mult).then_inc(ctx_dve, 1)
            dve.wait_ge(ctx_pe, 5)
            nc.vector.tensor_copy(awc[:], cbank[2][0:S2, 0:NCT]).then_inc(ctx_dve, 1)
            dve.wait_ge(ctx_pe, 7)
            s.link(nc.vector.tensor_tensor(kg[:], cbank[0][0:B, 0:D], vec("kg_b1", B), ALU.add))
            s.link(nc.vector.bn_stats(kstats[:, 0:6], kg[:]))
            s.link(nc.vector.bn_aggr(ks[:, 0:2], kstats[:, 0:6]))
            s.link(nc.vector.tensor_scalar(ks[:, 1:2], ks[:, 1:2], LN_EPS, None, ALU.add))
            nc.vector.tensor_copy(kstats[:, 7:8], ks[:, 1:2]).then_inc(ctx_dve, 1)
            dve.wait_ge(ctx_act, 6)
            s.link(nc.vector.reciprocal(kstats[:, 7:8], kstats[:, 7:8]))
            newton(nc, s, kstats[:, 7:8], ks[:, 1:2])
            s.link(nc.vector.tensor_scalar(kg[:], kg[:], ks[:, 0:1], kstats[:, 7:8], ALU.subtract, ALU.mult))
            s.link(nc.vector.tensor_tensor(kg[:], kg[:], vec("kg_g", B), ALU.mult))
            nc.vector.tensor_tensor(kg[:], kg[:], vec("kg_beta", B), ALU.add).then_inc(ctx_dve, 1)
            dve.wait_ge(ctx_pe, 9)
            kpf = kp[:].rearrange("b h t -> b (h t)")
            s.link(nc.vector.tensor_tensor(kpf, cbank[2][0:B, 0:H * TAPS], vec("kg_b2", B), ALU.add))
            s.link(nc.vector.tensor_reduce(ks[:, 0:H], kp[:], X, ALU.max))
            nc.vector.tensor_tensor(kp[:], kp[:], ks[:, 0:H].unsqueeze(2).to_broadcast([B, H, TAPS]),
                                    ALU.subtract).then_inc(ctx_dve, 1)
            dve.wait_ge(ctx_act, 9)
            s.link(nc.vector.tensor_reduce(ks[:, 0:H], kp[:], X, ALU.add))
            s.link(nc.vector.reciprocal(ks[:, H:2 * H], ks[:, 0:H]))
            nc.vector.tensor_tensor(kp[:], kp[:], ks[:, H:2 * H].unsqueeze(2).to_broadcast([B, H, TAPS]),
                                    ALU.mult).then_inc(ctx_dve, 1)
            dve.wait_ge(vrow_in, 16)
            nc.vector.tensor_copy(vkeep[:], vrow[:, 0:NKEEP]).then_inc(vkeep_in, 1)


def newton(nc, s, r, v):
    with ExitStack() as c:
        t = c.enter_context(nc.sbuf_tensor(f"newton{s.n}", [r.shape[0], r.shape[1]], F32))
        s.link(nc.vector.tensor_tensor(t[:], r, r, ALU.mult))
        s.link(nc.vector.tensor_tensor(t[:], t[:], v, ALU.mult))
        s.link(nc.vector.tensor_scalar(t[:], t[:], -0.5, 1.5, ALU.mult, ALU.add))
        s.link(nc.vector.tensor_tensor(r, r, t[:], ALU.mult))

def block2(nc, sem, ident, qT, kT, vaug, vaug_t, kerP, consts, khi, klo, K, qs_d, ks_d, ao_d):
    identb, mask_q, mask_k, first_neg, sumsel = consts
    RB = 3
    with ExitStack() as ctx:
        def sb(name, shape, dt=F32):
            return ctx.enter_context(nc.sbuf_tensor(name, shape, dt))

        Q1 = sb("Q1", [MROW + 1, 2 * GH, T], F32R)
        Q2 = sb("Q2", [MROW, 2, GH, QB], F32R)
        qf = sb("qf", [P, 3, QB])
        q1a, q2a, q2b = (sb(n, [P, QB]) for n in ("q1a", "q2a", "q2b"))
        qhi, qlo = (sb(n, [P, 3, QB], F32R) for n in ("qhi", "qlo"))
        pa = sb("pa", [P, QB])
        dprod = sb("dprod", [P, 2, T])
        d01 = sb("d01", [P, 2, TB, UH])
        mx = sb("mx", [P, GH, TB + (T - QB) // P])
        nm = sb("nm", [P, GH, TB])
        mrow = sb("mrow", [GH * TB, P])
        e01 = sb("e01", [P, 2, 2, TB, GH])
        esum = sb("esum", [P, 2, TB, GH])
        vprev = sb("vprev", [P, TB, GH, HD])
        own = sb("own", [P, 2, TB, GH, HD])
        Pt = sb("Pt", [P, 2, GH, QB])
        oT = sb("oT", [P, 2, QB])
        rl = sb("rl", [P, 4, GH])
        num = sb("num", [P, 4, GH, HD])
        ao = sb("ao", [P, 2, 4, GH, HD])


        def tap_buffers(n):
            if n != 1:
                return qf[:], q1a[:], q2a[:], q2b[:]
            spare = Pt[:].rearrange("p a h q -> p (a h) q")
            return spare[:, 0:3, :], spare[:, 3, :], spare[:, 4, :], spare[:, 5, :]

        spair = [ctx.enter_context(nc.psum_tensor(f"spair{i}", [P, 2, QB], F32)) for i in range(2)]
        ringb = [ctx.enter_context(nc.psum_tensor(f"ring{i}", [P, QB], F32)) for i in range(RB)]
        pv = ctx.enter_context(nc.psum_tensor("pv", [P, QB], F32))

        dve_steps, pool_steps = sem("dve_steps2"), sem("pool_steps2")
        taps_done = sem("taps_done")
        qhi_ready, qlo_ready = sem("qhi_ready"), sem("qlo_ready")
        khilo_ready = sem("khilo_ready")
        dprod_ready = sem("dprod_ready")
        qhi_out, qlo_out, k_out = sem("qhi_out"), sem("qlo_out"), sem("k_out")
        kq1_in = [sem(f"kq1_in{i}") for i in range(2 * GH)]
        q2_in = [sem(f"q2_in{i}") for i in range(2)]
        ring_full, ring_free = sem("ring_full"), sem("ring_free")
        nm_ready, mrow_in = sem("nm_ready"), sem("mrow_in")
        dless_ready, e01_ready = sem("dless_ready"), sem("e01_ready")
        vprev_in, own_ready = sem("vprev_in"), sem("own_ready")
        s_full, p_ready, pv_done = sem("s_full"), sem("p_ready"), sem("pv_done")
        o_ready = sem("o_ready")
        ao_ready, ao_out = sem("ao_ready"), [sem(f"ao_out{i}") for i in range(2)]

        def ucol(t, u, t0, shift):
            return t[:, u, LPAD + t0 + shift:LPAD + t0 + shift + QB]

        def stage_ring(g):
            out = []
            nxt = g + 1
            if nxt < NG:
                if nxt % 2 == 0 and g >= 0:
                    out.append((DIAG_AT, ("diag", nxt // 2)))
                first = FIRST_MAX if g >= 0 else 0
                per = -(-len(CHUNKS) // (LAST_MAX + 1 - FIRST_MAX)) if g >= 0 else len(CHUNKS)
                for n, c in enumerate(CHUNKS):
                    if g < 0 and c == (GH - 1, 0, 0):
                        out.append((0, ("diag", nxt // 2)))
                    out.append((first + n // per, ("max", nxt, c)))
                out.append((NI if g < 0 else LAST_MAX + 1, ("turn_m", nxt)))
            if g >= 0:
                out.append((7, ("out", g, 0)))
            if g >= 1:
                out.append((3, ("out", g - 1, 1)))
            return sorted(out, key=lambda a: a[0])

        rings = {g: stage_ring(g) for g in range(-1, NG + 1)}
        rings[NG] = [(0, ("out", NG - 1, 1))]

        def stage_items(g, slot):
            return [it for s_, it in rings[g] if s_ == slot]

        flat = [it for g in range(-1, NG + 1) for s_ in range(NI + 1) for it in stage_items(g, s_)]
        ring_index = {it: n for n, it in enumerate(flat)}
        first_banks = ringb + [spair[a][:, b_, :] for a in range(2) for b_ in range(2)]
        PRO, FB = len(stage_items(-1, 0)), len(first_banks)

        def ring_bank(n):
            return first_banks[n % FB] if n < PRO else ringb[n % RB]

        block = ctx.enter_context(nc.Block())

        @block.sync
        def _(sp):
            def write_high(n):
                u, half = divmod(n, 2)
                sp.wait_ge(qhi_ready, n + 1)
                sp.dma_start(qs_d[0, u, :, :, half * QB:(half + 1) * QB], qhi[:].bitcast(F32)).then_inc(qhi_out, 16)

            def write_low(n):
                u, half = divmod(n, 2)
                sp.wait_ge(qlo_ready, n + 1)
                sp.dma_start(qs_d[1, u, :, :, half * QB:(half + 1) * QB], qlo[:].bitcast(F32)).then_inc(qlo_out, 16)
                if half == 0 and u:
                    sp.wait_ge(khilo_ready, 2 * u)
                    sp.dma_start(ks_d[0, u], khi[:].bitcast(F32)).then_inc(k_out, 16)
                    sp.dma_start(ks_d[1, u], klo[:].bitcast(F32)).then_inc(k_out, 16)

            def load_kq1(g):
                u, h0 = g // 2, GH * (g % 2)
                if g >= 2:
                    sp.wait_ge(pv_done, NI * (g - 1))
                    sp.wait_ge(s_full, 2 * NI * (g - 1))
                if u:
                    sp.wait_ge(k_out, 32 * u)
                sp.wait_ge(qhi_out, 32 * (u + 1))
                for h in range(GH):
                    slot, r = GH * (g % 2) + h, HD * (h0 + h)
                    if u:
                        load_keys(sp, K, ks_d, u, h0 + h, slot, kq1_in[slot])
                    for part in range(2):
                        sp.dma_start(Q1[part * KROWS:(part + 1) * KROWS, slot, :].bitcast(F32),
                                     qs_d[0, u, r:r + HD]).then_inc(kq1_in[slot], 16)

            def load_q2(g, qb):
                u, h0 = g // 2, GH * (g % 2)
                if g >= 1:
                    sp.wait_ge(s_full, 2 * (NI * (g - 1) + (QB // P if qb == 0 else NI)))
                sp.wait_ge(qlo_out, 32 * (u + 1))
                for h in range(GH):
                    r = HD * (h0 + h)
                    for part in range(2):
                        sp.dma_start(Q2[part * KROWS:(part + 1) * KROWS, qb, h, :].bitcast(F32),
                                     qs_d[1, u, r:r + HD, :, qb * QB:(qb + 1) * QB]).then_inc(q2_in[qb], 16)

            def load_vprev(g):
                b, h0 = g // 4, GH * (g % 4)
                if g >= 1:
                    sp.wait_ge(own_ready, 3 * g)
                for k in range(TB):
                    sp.dma_start(vprev[1:P, k, :, :],
                                 vaug_t[0:P - 1, b * TB + k, h0:h0 + GH, 0:HD]).then_inc(vprev_in, 16)
                    sp.dma_start(vprev[0:1, k, :, :],
                                 vaug_t[P - 1:P, b * TB + max(k - 1, 0), h0:h0 + GH, 0:HD]).then_inc(vprev_in, 16)

            def place_max(g):
                sp.wait_ge(ring_free, ring_index[("turn_m", g)] + 1)
                s0 = GH * (g % 2)
                sp.dma_start(Q1[MROW:MROW + 1, s0:s0 + GH, :].bitcast(F32), mrow[:]).then_inc(mrow_in, 16)

            def write_ao(g, qb):
                n = 2 * g + qb
                sp.wait_ge(ao_ready, n + 1)
                b, h0 = g // 4, GH * (g % 4)
                r0 = b * T + qb * QB
                dst = ao_d[r0:r0 + QB, h0 * HD:(h0 + GH) * HD].rearrange("(k p) d -> p k d", p=P)
                sp.dma_start(dst, ao[:, n % 2, :, :, :].rearrange("p k h d -> p k (h d)")).then_inc(ao_out[n % 2], 16)

            write_high(0)
            write_low(0)
            write_high(1)
            load_kq1(0)
            write_low(1)
            load_kq1(1)
            load_q2(0, 0)
            load_q2(0, 1)
            load_vprev(0)
            place_max(0)
            for g in range(NG):
                if g + 1 < NG and g >= 1:
                    load_kq1(g + 1)
                if g >= 1:
                    write_ao(g - 1, 1)
                if g + 1 < NG:
                    load_vprev(g + 1)
                more = g % 2 == 0 and g // 2 + 1 < NU
                if more:
                    write_high(g + 2)
                    write_low(g + 2)
                if g + 1 < NG:
                    load_q2(g + 1, 0)
                write_ao(g, 0)
                if g + 1 < NG:
                    place_max(g + 1)
                if more:
                    write_high(g + 3)
                    write_low(g + 3)
                if g + 1 < NG:
                    load_q2(g + 1, 1)
            write_ao(NG - 1, 1)
            for done in ao_out:
                sp.wait_ge(done, 16 * NG)

        @block.gpsimd
        def _(pool):
            s = Steps(pool, pool_steps)
            def prepare(u):
                if u:
                    if u > 1:
                        pool.wait_ge(k_out, 32 * (u - 1))
                    nc.gpsimd.tensor_copy(khi[:], kT[:, u, :]).then_inc(khilo_ready, 1)
                    pool.wait_ge(khilo_ready, 2 * u - 1)
                    nc.gpsimd.tensor_tensor(klo[:], kT[:, u, :], khi[:].bitcast(F32),
                                            ALU.subtract).then_inc(khilo_ready, 1)
                if u:
                    pool.wait_ge(ring_full, ring_index[("diag", u - 1)] + 1)
                for half in range(2):
                    t0 = half * QB
                    pool.wait_ge(taps_done, 2 * u + half + 1)
                    q_, a1, a2, b2 = tap_buffers(2 * u + half)
                    for kind, terms in enumerate((((q_[:, 0, :], -1), (a1, 0), (a2, 1)),
                                                  ((q_[:, 0, :], -2), (q_[:, 1, :], -1), (b2, 0)))):
                        dp = dprod[:, kind, t0:t0 + QB]
                        s.mark(nc.gpsimd.tensor_tensor(dp, terms[0][0], ucol(kT, u, t0, terms[0][1]), ALU.mult))
                        s.link(nc.gpsimd.tensor_tensor(pa[:], terms[1][0], ucol(kT, u, t0, terms[1][1]), ALU.mult))
                        s.link(nc.gpsimd.tensor_tensor(dp, dp, pa[:], ALU.add))
                        s.link(nc.gpsimd.tensor_tensor(pa[:], terms[2][0], ucol(kT, u, t0, terms[2][1]), ALU.mult))
                        nc.gpsimd.tensor_tensor(dp, dp, pa[:], ALU.add).then_inc(dprod_ready, 1)
                        pool.wait_ge(dprod_ready, 2 * (2 * u + half) + kind + 1)

            def own_terms(g):
                b, h0, w = g // 4, GH * (g % 4), g % 2
                pool.wait_ge(e01_ready, g + 1)
                if g >= 2:
                    pool.wait_ge(ao_ready, 2 * (g - 1))
                e = [e01[:, w, k, :, :].unsqueeze(3).to_broadcast([P, TB, GH, HD]) for k in range(2)]
                nc.gpsimd.tensor_tensor(esum[:, w], e01[:, w, 0], e01[:, w, 1], ALU.add).then_inc(own_ready, 1)
                s.mark(nc.gpsimd.tensor_tensor(own[:, w], vaug_t[:, b * TB:(b + 1) * TB, h0:h0 + GH, 0:HD], e[0],
                                               ALU.mult))
                pool.wait_ge(vprev_in, 16 * 2 * TB * (g + 1))
                nc.gpsimd.tensor_tensor(vprev[:], vprev[:], e[1], ALU.mult).then_inc(own_ready, 1)
                pool.wait_ge(own_ready, 3 * g + 2)
                pool.wait_ge(pool_steps, s.n)
                nc.gpsimd.tensor_tensor(own[:, w], own[:, w], vprev[:], ALU.add).then_inc(own_ready, 1)

            prepare(0)
            own_terms(0)
            for g in range(NG):
                if g % 2 == 0 and g // 2 + 1 < NU:
                    prepare(g // 2 + 1)
                if g + 1 < NG:
                    own_terms(g + 1)

        @block.scalar
        def _(act):
            def round_q(n):
                act.wait_ge(taps_done, n + 1)
                if n:
                    act.wait_ge(qlo_ready, n)
                    act.wait_ge(qhi_out, 16 * n)
                nc.scalar.copy(qhi[:], tap_buffers(n)[0]).then_inc(qhi_ready, 1)

            def exps(g, i, pair):
                n = g * NI + i
                qb, kt = ITEMS[i]
                off = max(0, kt * P - qb * QB)
                act.wait_ge(s_full, 2 * n + pair + 1)
                if n >= 2:
                    act.wait_ge(pv_done, n - 1)
                nc.scalar.activation(Pt[:, n % 2, 2 * pair:2 * pair + 2, off:QB], spair[pair][:, :, off:QB],
                                     ACT.Exp).then_inc(p_ready, 1)

            def turn_out(g, qb):
                act.wait_ge(pv_done, g * NI + (QB // P if qb == 0 else NI))
                if g >= 1:
                    act.wait_ge(ring_full, ring_index[("out", g - 1, qb)] + 1)
                nc.scalar.copy(oT[:, qb, :], pv[:]).then_inc(o_ready, 1)

            def own_exps(g):
                act.wait_ge(dless_ready, g + 1)
                nc.scalar.activation(e01[:, g % 2], e01[:, g % 2], ACT.Exp).then_inc(e01_ready, 1)

            round_q(0)
            round_q(1)
            own_exps(0)
            for g in range(NG):
                for i in range(NI):
                    for pair in range(2):
                        exps(g, i, pair)
                    if i == 0 and g >= 1:
                        turn_out(g - 1, 1)
                    if i == QB // P:
                        turn_out(g, 0)
                    if g % 2 == 0 and g // 2 + 1 < NU and i in (HALF_SLOTS - 2, 2 * HALF_SLOTS - 2):
                        round_q(2 * (g // 2 + 1) + i // HALF_SLOTS)
                if g + 1 < NG:
                    own_exps(g + 1)
            turn_out(NG - 1, 1)

        @block.tensor
        def _(pe):
            def ring_take(it):
                n = ring_index[it]
                bank = ring_bank(n)
                if FB <= n < PRO:
                    pe.wait_ge(ring_free, n - FB + 1)
                elif n >= PRO:
                    pe.wait_ge(ring_free, max(n - RB + 1, PRO))
                if it[0] == "diag":
                    u = it[1]
                    pe.wait_ge(dprod_ready, 4 * (u + 1))
                    for kind in range(2):
                        for k in range(TB):
                            col = (kind * TB + k) * UH
                            last = nc.tensor.matmul(bank[:, col:col + UH], dprod[:, kind, k * P:(k + 1) * P],
                                                    sumsel[:], start=True, stop=True)
                elif it[0] == "max":
                    _, g, (h, qt, c) = it
                    slot = GH * (g % 2) + h
                    if (qt, c) == (0, 0):
                        pe.wait_ge(kq1_in[slot], 64 * (g // 2) + 32)
                    lo, hi = c * QB, min((c + 1) * QB, (qt + 1) * P)
                    ma, mb = max(qt * P - 2, lo), hi
                    masked = mb > ma
                    last = nc.tensor.matmul(bank[:, 0:hi - lo], Q1[0:MROW, slot, qt * P:(qt + 1) * P],
                                            K[0:MROW, slot, lo:hi], start=True, stop=not masked)
                    if masked:
                        o = ma - (qt * P - 2)
                        last = nc.tensor.matmul(bank[:, ma - lo:mb - lo], identb[:], mask_q[:, o:o + mb - ma],
                                                start=False, stop=True)
                elif it[0] == "turn_m":
                    g = it[1]
                    pe.wait_ge(nm_ready, g + 1)
                    last = nc.tensor.transpose(bank[0:GH * TB, 0:P], nm[:].rearrange("p h t -> p (h t)"), ident[:])
                else:
                    _, g, qb = it
                    pe.wait_ge(o_ready, 2 * g + qb + 1)
                    for k in range(4):
                        last = nc.tensor.transpose(bank[:, k * P:(k + 1) * P], oT[:, qb, k * P:(k + 1) * P], ident[:])
                last.then_inc(ring_full, 1)

            def scores(g, i, pair, ring_between):
                n = g * NI + i
                qb, kt = ITEMS[i]
                q0, q1 = max(kt * P, qb * QB), (qb + 1) * QB
                if n >= 1:
                    pe.wait_ge(p_ready, 2 * (n - 1) + pair + 1)
                if i == 0:
                    pe.wait_ge(mrow_in, 16 * (g + 1))
                if kt == 0:
                    pe.wait_ge(q2_in[qb], 128 * (g + 1))
                ma, mb = max(kt * P, q0), min(kt * P + P + 2, q1)
                masked = mb > ma
                for j in range(2):
                    h = 2 * pair + j
                    if j:
                        ring_between(2 * pair)
                    slot = GH * (g % 2) + h
                    bank = spair[pair][:, j, :]
                    o = q0 - qb * QB
                    keys = slice(kt * P, (kt + 1) * P)
                    nc.tensor.matmul(bank[:, o:QB], K[:, slot, keys], Q1[:, slot, q0:q1], start=True, stop=False)
                    last = nc.tensor.matmul(bank[:, o:QB], K[0:MROW, slot, keys], Q2[:, qb, h, o:QB],
                                            start=False, stop=not masked)
                    if masked:
                        a, b_ = ma - qb * QB, mb - qb * QB
                        last = nc.tensor.matmul(bank[:, a:b_], identb[:], mask_k[:, ma - kt * P:mb - kt * P],
                                                start=False, stop=True)
                last.then_inc(s_full, 1)

            def weigh(g, i):
                n = g * NI + i
                qb, kt = ITEMS[i]
                off = max(0, kt * P - qb * QB)
                pe.wait_ge(p_ready, 2 * (n + 1))
                if kt == 0 and g + qb:
                    pe.wait_ge(o_ready, 2 * g + qb)
                t = (g // 4) * TB + kt
                for h in range(GH):
                    c0 = (t * H + GH * (g % 4) + h) * VW
                    last = nc.tensor.matmul(pv[32 * h:32 * h + 32, off:QB], vaug[:, c0:c0 + 32],
                                            Pt[:, n % 2, h, off:QB], start=(kt == 0),
                                            stop=(kt == (qb + 1) * QB // P - 1))
                last.then_inc(pv_done, 1)

            for s_ in range(NI + 1):
                for it in stage_items(-1, s_):
                    ring_take(it)
            for g in range(NG):
                for i in range(NI):
                    items = [it for it in stage_items(g, i) if it[0] != "turn_m"]
                    late = stage_items(g, i)[len(items):]

                    def ring_between(m):
                        for it in items[m:m + 1]:
                            ring_take(it)

                    for pair in range(2):
                        scores(g, i, pair, ring_between)
                        ring_between(2 * pair + 1)
                    if i:
                        weigh(g, i - 1)
                    for it in items[4:] + late:
                        ring_take(it)
                weigh(g, NI - 1)
            for it in stage_items(NG, 0):
                ring_take(it)

        @block.vector
        def _(dve):
            s = Steps(dve, dve_steps)

            def taps(n, steps):
                u, half = divmod(n, 2)
                t0 = half * QB
                if n > 1 and 0 in steps:
                    dve.wait_ge(qhi_ready, n)
                    dve.wait_ge(dprod_ready, 2 * n)
                    dve.wait_ge(qlo_ready, n)
                q = [ucol(qT, u, t0, i - 1) for i in range(3)]
                k = [[kerP[:, u, 3 * i + j:3 * i + j + 1] for j in range(3)] for i in range(3)]
                q_, a1, a2, b2 = tap_buffers(n)
                mid = {0: (q_[:, 0, :], q_[:, 0, :]), 1: (a1, a1), 2: (a2, b2)}
                for step in steps:
                    i, j = 2 - step // 3, step % 3
                    if i == 2:
                        s.mark(nc.vector.tensor_scalar(mid[j][0], q[2], k[2][j], None, ALU.mult))
                    else:
                        src = mid[j][0] if i == 1 else mid[j][1]
                        dst = mid[j][1] if i == 1 else q_[:, j, :]
                        if j == 0:
                            dve.wait_ge(dve_steps, s.n)
                        ins = nc.vector.scalar_tensor_tensor(dst, q[i], k[i][j], src, ALU.mult, ALU.add)
                        if (i, j) == (0, 2):
                            ins.then_inc(taps_done, 1)
                        else:
                            s.mark(ins)

            def low_parts(n):
                dve.wait_ge(qhi_ready, n + 1)
                if n:
                    dve.wait_ge(qlo_out, 16 * n)
                nc.vector.tensor_tensor(qlo[:], tap_buffers(n)[0], qhi[:].bitcast(F32), ALU.subtract).then_inc(qlo_ready, 1)

            def ring_give(it):
                n = ring_index[it]
                bank = ring_bank(n)
                dve.wait_ge(ring_full, n + 1)
                if it[0] == "diag":
                    ins = nc.vector.tensor_copy(d01[:].rearrange("p c t h -> p (c t h)"), bank[:, 0:2 * TB * UH])
                    ins.then_inc(ring_free, 1)
                    dve.wait_ge(ring_free, n + 1)
                    s.mark(nc.vector.tensor_scalar(d01[:, 1, 0, :], d01[:, 1, 0, :], first_neg[:, 0:1], None, ALU.add))
                elif it[0] == "max":
                    _, g, (h, qt, c) = it
                    width = min((c + 1) * QB, (qt + 1) * P) - c * QB
                    col = chunk_column(qt, c)
                    nc.vector.tensor_reduce(mx[:, h, col:col + 1], bank[:, 0:width], X, ALU.max).then_inc(ring_free, 1)
                elif it[0] == "turn_m":
                    g = it[1]
                    if g:
                        dve.wait_ge(mrow_in, 16 * g)
                    nc.vector.tensor_copy(mrow[:], bank[0:GH * TB, 0:P]).then_inc(ring_free, 1)
                else:
                    _, g, qb = it
                    w, rows = g % 2, slice(4 * qb, 4 * qb + 4)
                    o = bank[:].rearrange("p (k h e) -> p k h e", k=4, h=GH)
                    m = 2 * g + qb
                    dve.wait_ge(own_ready, 3 * (g + 1))
                    if m:
                        dve.wait_ge(ao_ready, m)
                    if m >= 2:
                        dve.wait_ge(ao_out[m % 2], 16 * (m // 2))
                    s.mark(nc.vector.tensor_tensor(rl[:], o[:, :, :, HD], esum[:, w, rows, :], ALU.add))
                    ins = nc.vector.tensor_tensor(num[:], o[:, :, :, 0:HD], own[:, w, rows, :, :], ALU.add)
                    ins.then_inc(ring_free, 1)
                    dve.wait_ge(ring_free, n + 1)
                    s.link(nc.vector.reciprocal(rl[:], rl[:]))
                    nc.vector.tensor_tensor(ao[:, m % 2], num[:], rl[:].unsqueeze(3).to_broadcast([P, 4, GH, HD]),
                                            ALU.mult).then_inc(ao_ready, 1)

            def finish_max(g):
                hh = GH * (g % 2)
                dv = [d01[:, k, :, hh:hh + GH] for k in range(2)]
                last = max(ring_index[("max", g, CHUNKS[-1])], ring_index[("diag", g // 2)])
                dve.wait_ge(ring_free, last + 1)
                dve.wait_ge(dve_steps, s.n)
                hi = (T - QB) // P
                s.link(nc.vector.tensor_tensor(mx[:, :, TB - hi:TB], mx[:, :, TB - hi:TB], mx[:, :, TB:TB + hi], ALU.max))
                for k in range(2):
                    s.link(nc.vector.tensor_tensor(mx[:, :, 0:TB], mx[:, :, 0:TB],
                                                   dv[k].rearrange("p t h -> p h t"), ALU.max))
                if g:
                    dve.wait_ge(ring_full, ring_index[("turn_m", g - 1)] + 1)
                nc.vector.tensor_scalar(nm[:].bitcast(F32R), mx[:, :, 0:TB], -1.0, None, ALU.mult).then_inc(nm_ready, 1)
                dve.wait_ge(nm_ready, g + 1)
                if g >= 2:
                    dve.wait_ge(own_ready, 3 * (g - 1))
                for k in range(2):
                    ins = nc.vector.tensor_tensor(e01[:, g % 2, k], dv[k], nm[:].rearrange("p h t -> p t h"), ALU.add)
                    s.mark(ins) if k == 0 else ins.then_inc(dless_ready, 1)

            taps(0, range(9))
            taps(1, range(3))
            low_parts(0)
            taps(1, range(3, 9))
            low_parts(1)
            for it in stage_items(-1, 0):
                ring_give(it)
            finish_max(0)
            for it in stage_items(-1, NI):
                ring_give(it)
            for g in range(NG):
                more = g % 2 == 0 and g // 2 + 1 < NU
                n0 = 2 * (g // 2 + 1)
                for i in range(NI):
                    items = stage_items(g, i)
                    half, third = divmod(i, HALF_SLOTS)
                    if i == LAST_MAX + 1 and g + 1 < NG:
                        finish_max(g + 1)
                    for m in range(max(len(items), 3)):
                        for it in items[m:m + 1]:
                            ring_give(it)
                        if more and half < 2 and third < 3 and m < 3:
                            taps(n0 + half, [3 * third + m])
                    if more and half < 2 and third == HALF_SLOTS - 1:
                        low_parts(n0 + half)
            for it in stage_items(NG, 0):
                ring_give(it)

def general_attention(nc, sem, ident, qT, kT, vaug_t, mask, kern_d, qk_d, v_d, oh_d, ao_d):
    HEADS = B * H
    NP2 = NQB * TB
    with ExitStack() as ctx:
        def sb(name, shape, dt=F32):
            return ctx.enter_context(nc.sbuf_tensor(name, shape, dt))

        mask_words = sb("g_mask", [P, TB, T // 4], mybir.dt.int32)
        keep = sb("g_keep", [P, TB, T], BF16)
        drop = sb("g_drop", [P, TB, T], BF16)
        shift = sb("g_shift", [P, 3, P])
        corner = sb("g_corner", [P, 2, P])
        qh, kh = sb("g_q", [HD, T]), sb("g_k", [HD, T])
        vh = sb("g_v", [P, TB, HD])
        taps = sb("g_taps", [P, TAPS])
        band = sb("g_band", [P, 3, P])
        part = sb("g_part", [P, 3, P])
        edge = sb("g_edge", [P, 2, 3, P])
        s0 = sb("g_s0", [P, TB, T + 2])
        sc = sb("g_sc", [P, T])
        pr = sb("g_p", [P, T])
        prT = sb("g_pT", [P, TB, P])
        nmax, total = sb("g_nmax", [P, 1]), sb("g_total", [P, 1])
        oh = sb("g_oh", [P, TB, HD])
        spare = sb("g_spare", [P, 1])
        sbank, cbank, tbank = ([ctx.enter_context(nc.psum_tensor(f"g_{n}bank{i}", [P, QB], F32)) for i in range(2)]
                               for n in ("s", "c", "t"))
        obank = ctx.enter_context(nc.psum_tensor("g_o", [P, QB], F32))

        mask_in, dumped, head_in, head_out = (sem(n) for n in ("g_mask_in", "g_dumped", "g_head_in", "g_head_out"))
        masks_ready, shifts_ready, steps, psteps = (sem(n) for n in ("g_masks", "g_shifts", "g_steps", "g_psteps"))
        bands_ready, s_full, s_free, c_full, c_free = (sem(n) for n in (
            "g_bands", "g_s_full", "g_s_free", "g_c_full", "g_c_free"))
        max_ready, p_ready, t_full, t_free, o_full, o_free = (sem(n) for n in (
            "g_max", "g_p_ready", "g_t_full", "g_t_free", "g_o_full", "g_o_free"))
        written, spare_ready = sem("g_written"), sem("g_spare")

        block = ctx.enter_context(nc.Block())

        @block.sync
        def _(sp):
            sp.dma_start(mask_words[:], mask.rearrange("(t p) k -> p t k", p=P)).then_inc(mask_in, 16)
            for n, t in enumerate((qT, kT)):
                sp.dma_start(qk_d[n].rearrange("(u p) t -> p u t", p=P), t[:]).then_inc(dumped, 16)
            for b in range(B):
                for h in range(H):
                    sp.dma_start(v_d[b * H + h], vaug_t[:, b * TB:(b + 1) * TB, h, 0:HD]).then_inc(dumped, 16)
            sp.wait_ge(dumped, 16 * (2 + HEADS))
            sp.dma_start(oh_d[0], v_d[0]).then_inc(head_out, 16)
            sp.wait_ge(head_out, 16)
            with sp.Fori(0, HEADS) as i:
                row0 = sp.snap(i * HD)
                sp.wait_ge(o_free, i * TB + 1)
                for n, t in enumerate((qh, kh)):
                    sp.dma_start(t[:], qk_d[n, bass.ds(row0, HD), LPAD:LPAD + T]).then_inc(head_in, 16)
                sp.dma_start(vh[:], v_d[bass.ds(i, 1)].rearrange("o p t d -> (o p) t d")).then_inc(head_in, 16)
                row = kern_d.rearrange("b (h t) -> (b h) t", t=TAPS)[bass.ds(i, 1), :]
                sp.dma_start(taps[:], row.partition_broadcast(P).rearrange("p o t -> p (o t)")).then_inc(head_in, 16)
                sp.wait_ge(o_free, i * TB + TB + 1)
                sp.dma_start(oh_d[bass.ds(i, 1)].rearrange("o p t d -> (o p) t d"), oh[:]).then_inc(head_out, 16)
            sp.wait_ge(head_out, 16 * (HEADS + 1))
            for b in range(B):
                for h in range(H):
                    dst = ao_d[b * T:(b + 1) * T, h * HD:(h + 1) * HD].rearrange("(t p) d -> p t d", p=P)
                    sp.dma_start(dst, oh_d[b * H + h]).then_inc(written, 16)
            sp.wait_ge(written, 16 * HEADS)

        @block.gpsimd
        def _(pool):
            s = Steps(pool, psteps)
            s.mark(nc.gpsimd.memset(shift[:], 0.0))
            s.link(nc.gpsimd.memset(corner[:], 0.0))
            for i in range(3):
                s.link(nc.gpsimd.affine_select(out=shift[:, i, :], in_=shift[:, i, :], compare_op=ALU.not_equal,
                                               fill=1.0, base=1 - i, pattern=[[-1, P]], channel_multiplier=1))
            for n, base in enumerate((1 - P, P - 1)):
                s.link(nc.gpsimd.affine_select(out=corner[:, n, :], in_=corner[:, n, :], compare_op=ALU.not_equal,
                                               fill=1.0, base=base, pattern=[[-1, P]], channel_multiplier=1))
            nc.gpsimd.memset(spare[:], 0.0).then_inc(shifts_ready, 1)

        @block.tensor
        def _(pe):
            with pe.Fori(0, HEADS) as i:
                pe.wait_ge(head_in, i * 64 + 64)
                for n in range(NP2):
                    qt, c = divmod(n, NQB)
                    pe.wait_ge(s_free, i * NP2 + n + 1)
                    nc.tensor.matmul(sbank[n % 2][:], qh[:, qt * P:(qt + 1) * P], kh[:, c * QB:(c + 1) * QB],
                                     start=True, stop=True).then_inc(s_full, 1)
                pe.wait_ge(bands_ready, i + 1)
                pe.wait_ge(s_free, i * NP2 + NP2 + 2)
                for qt in range(TB):
                    for c in range(NQB):
                        n = NQB * qt + c
                        pe.wait_ge(c_free, i * NP2 + n + 1)
                        around = [(band, qt)] + [(edge[:, m], t) for m, t in ((0, qt - 1), (1, qt + 1)) if 0 <= t < TB]
                        taken = [(w, t, j) for w, t in around for j in range(3)]
                        for m, (w, t, j) in enumerate(taken):
                            last = nc.tensor.matmul(cbank[n % 2][:], w[:, j, :], s0[:, t, c * QB + j:c * QB + j + QB],
                                                    start=(m == 0), stop=(m == len(taken) - 1))
                        last.then_inc(c_full, 1)
                    pe.wait_ge(p_ready, i * TB + qt + 1)
                    for c in range(NQB):
                        pe.wait_ge(t_free, i * NP2 + NQB * qt + c + 1)
                        for k in range(QB // P):
                            last = nc.tensor.transpose(tbank[c][:, k * P:(k + 1) * P],
                                                       pr[:, (4 * c + k) * P:(4 * c + k + 1) * P], ident[:])
                        last.then_inc(t_full, 1)
                    pe.wait_ge(t_free, i * NP2 + NQB * (qt + 1) + 2)
                    pe.wait_ge(o_free, i * TB + qt + 1)
                    for k in range(TB):
                        last = nc.tensor.matmul(obank[:, 0:HD], prT[:, k, :], vh[:, k, :], start=(k == 0), stop=(k == TB - 1))
                    last.then_inc(o_full, 1)

        @block.scalar
        def _(act):
            act.sem_inc(t_free, 2)
            with act.Fori(0, HEADS) as i:
                for qt in range(TB):
                    act.wait_ge(max_ready, i * TB + qt + 1)
                    nc.scalar.activation(pr[:], sc[:], ACT.Exp, bias=nmax[:, 0:1], accum_out=total[:]).then_inc(p_ready, 1)
                    for c in range(NQB):
                        act.wait_ge(t_full, i * NP2 + NQB * qt + c + 1)
                        nc.scalar.copy(prT[:, 4 * c:4 * c + 4, :].rearrange("p k q -> p (k q)"), tbank[c][:]).then_inc(t_free, 1)

        @block.vector
        def _(dve):
            dve.sem_inc(s_free, 2)
            dve.sem_inc(c_free, 2)
            dve.sem_inc(o_free, 1)
            dve.wait_ge(mask_in, 16)
            dve.wait_ge(shifts_ready, 1)
            nc.vector.tensor_scalar(keep[:], mask_words[:].bitcast(mybir.dt.uint8), -1.0, 1.0, ALU.mult, ALU.add).then_inc(masks_ready, 1)
            nc.vector.tensor_scalar(drop[:], mask_words[:].bitcast(mybir.dt.uint8), -BIG, None, ALU.mult).then_inc(masks_ready, 1)
            nc.vector.memset(s0[:], 0.0).then_inc(masks_ready, 1)
            dve.wait_ge(masks_ready, 3)
            NS = 6
            with dve.Fori(0, HEADS) as i:
                dve.wait_ge(head_in, i * 64 + 64)
                tap = [taps[:, 3 * r:3 * r + 3].unsqueeze(2).to_broadcast([P, 3, P]) for r in range(3)]
                wide = lambda a: a.unsqueeze(1).to_broadcast([P, 3, P])
                nc.vector.tensor_tensor(band[:], wide(shift[:, 0, :]), tap[0], ALU.mult).then_inc(steps, 1)
                nc.vector.tensor_tensor(part[:], wide(shift[:, 1, :]), tap[1], ALU.mult).then_inc(steps, 1)
                dve.wait_ge(steps, i * NS + 2)
                nc.vector.tensor_tensor(band[:], band[:], part[:], ALU.add).then_inc(steps, 1)
                dve.wait_ge(steps, i * NS + 3)
                nc.vector.tensor_tensor(part[:], wide(shift[:, 2, :]), tap[2], ALU.mult).then_inc(steps, 1)
                dve.wait_ge(steps, i * NS + 4)
                nc.vector.tensor_tensor(band[:], band[:], part[:], ALU.add).then_inc(steps, 1)
                nc.vector.tensor_tensor(edge[:, 0], wide(corner[:, 0, :]), tap[0], ALU.mult).then_inc(steps, 1)
                nc.vector.tensor_tensor(edge[:, 1], wide(corner[:, 1, :]), tap[2], ALU.mult).then_inc(bands_ready, 1)
                for n in range(NP2):
                    qt, c = divmod(n, NQB)
                    dve.wait_ge(s_full, i * NP2 + n + 1)
                    nc.vector.tensor_tensor(s0[:, qt, 1 + c * QB:1 + (c + 1) * QB], sbank[n % 2][:],
                                            keep[:, qt, c * QB:(c + 1) * QB], ALU.mult).then_inc(s_free, 1)
                for qt in range(TB):
                    dve.wait_ge(o_free, i * TB + qt + 1)
                    for c in range(NQB):
                        n = NQB * qt + c
                        dve.wait_ge(c_full, i * NP2 + n + 1)
                        nc.vector.tensor_tensor(sc[:, c * QB:(c + 1) * QB], cbank[n % 2][:],
                                                drop[:, qt, c * QB:(c + 1) * QB], ALU.add).then_inc(c_free, 1)
                    dve.wait_ge(c_free, i * NP2 + NQB * (qt + 1) + 2)
                    nc.vector.tensor_reduce(nmax[:], sc[:], X, ALU.max, negate=True).then_inc(max_ready, 1)
                    dve.wait_ge(p_ready, i * TB + qt + 1)
                    dve.wait_ge(o_full, i * TB + qt + 1)
                    if qt == 0:
                        dve.wait_ge(head_out, i * 16 + 16)
                    nc.vector.reciprocal(spare[:], total[:]).then_inc(spare_ready, 1)
                    dve.wait_ge(spare_ready, i * TB + qt + 1)
                    nc.vector.tensor_scalar(oh[:, qt, :], obank[:, 0:HD], spare[:, 0:1], None, ALU.mult).then_inc(o_free, 1)

def block3(nc, sem, ident, vkeep, x, ao_d, x1_d, xdisp_d, ydisp_d, proj_W, wrT, w1T, w2T, out):
    HT = TB
    PH = LOOPS * B
    ALL = PH * NTILE
    G = GROUPS
    NE12 = G + E
    WC = 1024
    POOL_PIECES = 10
    HI_AT = {1: (0,), 3: (1, 2), 4: (3, 4), 7: (5, 6, 7, 8), 10: (9, 10, 11), 12: (12, 13, 14, 15)}
    DVE_SCALES = 7
    YB, SL = 4, 3
    with ExitStack() as ctx:
        def sb(name, shape, dt=F32):
            return ctx.enter_context(nc.sbuf_tensor(name, shape, dt))

        w1 = [sb(f"w1{n}", [P, DC, E * F], F32R) for n in ("hi", "lo")]
        w2 = [sb(f"w2{n}", [P, FC, E * D], F32R) for n in ("hi", "lo")]
        wr = sb("wr", [P, DC, NE12])
        proj_w = sb("proj_w", [P, DC, D])
        z = sb("z", [P, NT, D])
        xn = sb("xn", [P, HT, D])
        xnT = sb("xnT3", [P, DC, T])
        yg = sb("yg", [P, YB, D])
        xd = sb("xd", [P, SL, D])
        xT = [sb(f"xT{n}", [P, 2, DC * P], F32R) for n in ("hi", "lo")]
        h = sb("h", [P, 2, F])
        hT = [sb(f"hT{n}", [P, 2, FC * P], F32R) for n in ("hi", "lo")]
        yo = sb("yo", [P, SL, D])
        mv = sb("mv3", [P, HT, 2])
        st6 = sb("st6", [P, HT, 6])
        sd = sb("sd", [P, 2, HT])
        lg = sb("lg", [P, HT, NE12])
        mm = sb("mm", [P, HT, 1 + G])
        rk, ge, wg, sel = (sb(n, [P, HT, G]) for n in ("rk", "ge", "wg", "sel"))
        chosen = sb("chosen", [P, HT, E])
        chosen_b = sb("chosen_b", [P, HT, E], BF16)
        cw = sb("cw", [P, HT, E])
        place = sb("place", [P, HT, E])
        tops = sb("tops", [P, 2, HT, G, G])
        ahead = sb("ahead", [P, G, G])
        fits = sb("fits", [P, E, HT])
        thr = sb("thr", [P, E, HT])
        tiles_e, ends, base = (sb(n, [P, E]) for n in ("tiles_e", "ends", "base"))
        last_one, scratch = (sb(n, [P, HT, E]) for n in ("last_one", "scratch"))
        pq = sb("pq", [P, 2, HT])
        wt = sb("wt", [P, B, 2, HT])
        idx = sb("idx", [P, B, 2, HT], mybir.dt.int32)
        tix = sb("tix", [1, NTILE, E])
        tcmp = sb("tcmp", [1, NTILE, E])
        tef = sb("tef", [1, NTILE])
        table = sb("table", [1, B, NTILE], mybir.dt.int32)
        tri = sb("tri", [P, P], BF16)
        onesb = sb("onesb", [P, P], BF16)

        hb = [ctx.enter_context(nc.psum_tensor(f"hb{i}", [P, F], F32)) for i in range(2)]
        tb = [ctx.enter_context(nc.psum_tensor(f"tb{i}", [P, FC * P], F32)) for i in range(2)]
        yb = ctx.enter_context(nc.psum_tensor("yb", [P, D], F32))
        xb = ctx.enter_context(nc.psum_tensor("xb", [P, DC * P], F32))
        misc = [ctx.enter_context(nc.psum_tensor(f"misc{i}", [P, 512], F32)) for i in range(2)]

        dve_steps, pool_steps = sem("dve_steps3"), sem("pool_steps3")
        small_in, rows_in, consts = (sem(n) for n in ("small_in", "rows_in", "consts3"))
        xz_in = [sem(f"xz_in{b}") for b in range(B)]
        wlo_done = [sem(f"wlo_done{i}") for i in range(2)]
        whi_done = sem("whi_done")
        x1_ready, out_ready, out_done = (sem(n) for n in ("x1_ready", "out_ready", "out_done"))
        x1_out = [sem(f"x1_out{b}") for b in range(B)]
        misc_full, misc_free = sem("misc_full"), [sem(f"misc_free{i}") for i in range(2)]
        ln_var, ln_std, rms_var, rms_std = (sem(n) for n in ("ln_var", "ln_std", "rms_var", "rms_std"))
        first_rows = sem("first_rows")
        root_ready, pool_scaled = sem("root_ready"), sem("pool_scaled")
        xn_ready, logits_exp, logits_less, chosen_ready = (sem(n) for n in (
            "xn3_ready", "logits_exp", "logits_less", "chosen_ready"))
        sorted_, table_ready, scattered = sem("sorted"), sem("table_ready"), sem("scattered")
        y_in = [sem(f"y_in{i}") for i in range(YB)]
        gathered = sem("gathered")
        xd_in, y_out = ([sem(f"{n}{i}") for i in range(SL)] for n in ("xd_in", "y_out"))
        x_turned, xhi_done, xlo_done, h_full, silu_done = (sem(n) for n in (
            "x_turned", "xhi_done3", "xlo_done", "h_full", "silu_done"))
        t_full, hhi_done, hlo_done, y_full, y_ready = (sem(n) for n in (
            "t_full3", "hhi_done", "hlo_done", "y_full", "y_ready"))

        def items_at(ph, i):
            n = ph + 1
            if n < B and i < 2:
                return [("aoT", n, i, q) for q in range(2)]
            if n < B and i < 4:
                return [("proj", n, 2 * i - 4 + q) for q in range(2)]
            if n < PH:
                return {X_AT: [("x", n, 0, q) for q in range(2)], X_AT + 1: [("x", n, 1, q) for q in range(2)],
                        X_AT + 2: [("logits", n)], X_AT + 6: [("counts", n)]}.get(i, [])
            return []

        order = [it for ph in range(-1, PH) for i in range(NTILE) for it in items_at(ph, i)]
        index = {it: n for n, it in enumerate(order)}
        pieces = [(w1, w1T, c, j) for c in range(DC) for j in range(E * F // WC)]
        pieces += [(w2, w2T, c, j) for c in range(FC) for j in range(E * D // WC)]
        piece_in = [sem(f"piece_in{i}") for i in range(len(pieces))]

        def low_part(eng, i):
            w, _, c, j = pieces[i]
            hi, lo = (t[:, c, j * WC:(j + 1) * WC] for t in w)
            return eng.tensor_tensor(lo, lo.bitcast(F32), hi.bitcast(F32), ALU.subtract)

        norm_w = vkeep[:, VEC["norm_w"][0]:VEC["norm_w"][1]]

        def wait_drained(engine, it):
            i = index[it]
            engine.wait_ge(misc_free[i % 2], i // 2 + 1)

        def drained(ins, it):
            ins.then_inc(misc_free[index[it] % 2], 1)

        def tile_rows(t, i):
            return t[i * P:(i + 1) * P, :]

        def half_rows(t, b):
            return t[b * T:(b + 1) * T, :].rearrange("(t p) d -> p t d", p=P)

        block = ctx.enter_context(nc.Block())

        @block.sync
        def _(sp):
            sp.dma_start(xn[:, 0:HT // 2, :], half_rows(ao_d, 0)[:, 0:HT // 2, :]).then_inc(first_rows, 16)
            sp.dma_start(xn[:, HT // 2:HT, :], half_rows(ao_d, 0)[:, HT // 2:HT, :]).then_inc(rows_in, 16)
            sp.dma_start(proj_w[:], proj_W.rearrange("(c p) n -> p c n", p=P)).then_inc(small_in, 16)
            sp.dma_start(wr[:], wrT.rearrange("(c p) n -> p c n", p=P)).then_inc(small_in, 16)
            sp.dma_start(z[:, 0:HT, :], half_rows(x, 0)).then_inc(xz_in[0], 16)
            for i, (w, dram, c, j) in enumerate(pieces):
                if i == 7:
                    sp.wait_ge(x1_ready, 1)
                    sp.dma_start(half_rows(x1_d, 0), xn[:]).then_inc(x1_out[0], 16)
                src = dram.rearrange("d e n -> d (e n)")[c * P:(c + 1) * P, j * WC:(j + 1) * WC]
                sp.dma_start(w[1][:, c, j * WC:(j + 1) * WC].bitcast(F32), src).then_inc(piece_in[i], 16)
            sp.dma_start(z[:, HT:NT, :], half_rows(x, 1)).then_inc(xz_in[1], 16)
            for n in range(ALL):
                ph, i = divmod(n, NTILE)
                if i == 0:
                    sp.wait_ge(scattered, 16 * 2 * HT * (ph + 1))
                    if ph == 0:
                        sp.dma_start(xn[:], half_rows(ao_d, 1)).then_inc(rows_in, 16)
                    if ph == PH - 1:
                        sp.dma_start(xn[:], half_rows(x1_d, 0)).then_inc(rows_in, 16)
                if n >= SL:
                    sp.wait_ge(x_turned, n - SL + 1)
                sp.dma_start(xd[:, n % SL, :], tile_rows(xdisp_d[ph % B], i)).then_inc(xd_in[n % SL], 16)
            sp.wait_ge(out_ready, 1)
            sp.dma_start(xn[:], half_rows(x1_d, 1)).then_inc(rows_in, 16)
            for b in range(B):
                sp.wait_ge(out_ready, b + 1)
                sp.dma_start(half_rows(out, b), z[:, b * HT:(b + 1) * HT, :]).then_inc(out_done, 16)
            sp.wait_ge(out_done, 16 * B)

        @block.gpsimd
        def _(pool):
            s = Steps(pool, pool_steps)
            for t, v in ((tri, 0.0), (onesb, 1.0)):
                s.mark(nc.gpsimd.memset(t[:], v))
            s.mark(nc.gpsimd.memset(ahead[:], 0.0))
            pool.wait_ge(pool_steps, s.n)
            for g in range(1, G):
                s.mark(nc.gpsimd.memset(ahead[:, g, 0:g], 1.0))
            for j in range(HT):
                s.mark(nc.gpsimd.memset(thr[:, :, j:j + 1], float(P * j)))
            for i in range(NTILE):
                s.mark(nc.gpsimd.memset(tix[:, i, :], float(i)))
            pool.wait_ge(pool_steps, s.n)
            nc.gpsimd.affine_select(out=tri[:], in_=tri[:], compare_op=ALU.is_ge, fill=1.0, base=0,
                                    pattern=[[-1, P]], channel_multiplier=1).then_inc(consts, 1)

            def write_x1(b):
                pool.wait_ge(x1_ready, b + 1)
                pool.dma_start(half_rows(x1_d, b), xn[:]).then_inc(x1_out[b], 16)

            def gather(ph):
                b = ph % B
                for i in range(SL):
                    pool.wait_ge(y_out[i], 16 * len(range(i, (ph + 1) * NTILE, SL)))
                for m in range(2 * HT):
                    k = 2 * HT * ph + m
                    if k >= YB:
                        pool.wait_ge(gathered, k - YB + 1)
                    t, w = divmod(m, 2)
                    at = bass.IndirectOffsetOnAxis(ap=idx[:, b, w, t:t + 1], axis=0)
                    pool.indirect_dma_start(yg[:, k % YB, :], None, ydisp_d[b], at,
                                            bounds_check=NTILE * P - 1).then_inc(y_in[k % YB], 16)

            def scale_rest(ph):
                pool.wait_ge(root_ready, 2 * min(ph + 1, B) + max(ph + 1 - B, 0))
                for t in range(DVE_SCALES, HT):
                    s.link(nc.gpsimd.tensor_scalar(xn[:, t, :], z[:, (ph % B) * HT + t, :], sd[:, 1, t:t + 1], None,
                                                   ALU.mult))
                    nc.gpsimd.tensor_tensor(xn[:, t, :], xn[:, t, :], norm_w, ALU.mult).then_inc(pool_scaled, 1)

            def scatter(ph):
                b = ph % B
                pool.wait_ge(sorted_, ph + 1)
                if ph >= B:
                    pool.wait_ge(x_turned, (ph - 1) * NTILE)
                for t in range(HT):
                    for w in range(2):
                        at = bass.IndirectOffsetOnAxis(ap=idx[:, b, w, t:t + 1], axis=0)
                        pool.indirect_dma_start(xdisp_d[b], at, xn[:, t, :], None,
                                                bounds_check=NTILE * P - 1).then_inc(scattered, 16)

            for i in range(POOL_PIECES):
                pool.wait_ge(whi_done, i + 1)
                low_part(nc.gpsimd, i).then_inc(wlo_done[0], 1)
            for ph in range(PH):
                if ph == 1:
                    write_x1(1)
                if ph >= B:
                    gather(ph - B)
                if ph:
                    if ph < B:
                        pool.wait_ge(x1_out[ph], 16)
                    else:
                        pool.wait_ge(scattered, 16 * 2 * HT * ph)
                    scale_rest(ph)
                scatter(ph)
            for ph in range(PH - B, PH):
                gather(ph)

        @block.tensor
        def _(pe):
            def take(it):
                i = index[it]
                bank = misc[i % 2]
                if i >= 2:
                    pe.wait_ge(misc_free[i % 2], i // 2)
                kind, n = it[0:2]
                if kind in ("aoT", "x"):
                    _, _, c, q = it
                    if kind == "aoT" and n == 0:
                        pe.wait_ge(first_rows if q == 0 else rows_in, 16)
                    elif kind == "aoT":
                        pe.wait_ge(rows_in, 16 * (n + 1))
                    else:
                        pe.wait_ge(xn_ready, HT + DVE_SCALES * n)
                        if n:
                            pe.wait_ge(pool_scaled, (HT - DVE_SCALES) * n)
                    for j in range(4):
                        last = nc.tensor.transpose(bank[:, j * P:(j + 1) * P], xn[:, 4 * q + j, c * P:(c + 1) * P],
                                                   ident[:])
                elif kind == "proj":
                    if it[2] == 0:
                        pe.wait_ge(small_in, 32)
                        for q in range(2):
                            wait_drained(pe, ("aoT", n, 1, q))
                    for j in range(2):
                        t = 2 * it[2] + j
                        for c in range(DC):
                            last = nc.tensor.matmul(bank[:, j * D:(j + 1) * D], xnT[:, c, t * P:(t + 1) * P],
                                                    proj_w[:, c, :], start=(c == 0), stop=(c == DC - 1))
                elif kind == "logits":
                    for q in range(2):
                        wait_drained(pe, ("x", n, 1, q))
                    for t in range(HT):
                        for c in range(DC):
                            last = nc.tensor.matmul(bank[:, t * NE12:(t + 1) * NE12], xnT[:, c, t * P:(t + 1) * P],
                                                    wr[:, c, :], start=(c == 0), stop=(c == DC - 1))
                else:
                    pe.wait_ge(chosen_ready, n + 1)
                    flags = chosen_b[:].rearrange("p t e -> p (t e)")
                    NF = HT * E
                    nc.tensor.matmul(bank[:, 0:NF], tri[:], flags, start=True, stop=False)
                    for t in range(1, HT):
                        nc.tensor.matmul(bank[:, t * E:NF], onesb[:], flags[:, 0:NF - t * E], start=False,
                                         stop=(t == HT - 1))
                    for t in range(HT):
                        last = nc.tensor.matmul(bank[:, NF:NF + E], onesb[:], flags[:, t * E:(t + 1) * E],
                                                start=(t == 0), stop=(t == HT - 1))
                last.then_inc(misc_full, 1)

            def turn_x(n):
                pe.wait_ge(xd_in[n % SL], 16 * (n // SL + 1))
                if n:
                    pe.wait_ge(xlo_done, n)
                for c in range(DC):
                    last = nc.tensor.transpose(xb[:, c * P:(c + 1) * P], xd[:, n % SL, c * P:(c + 1) * P], ident[:])
                last.then_inc(x_turned, 1)

            def hidden(n, e):
                if n == 0:
                    pe.wait_ge(wlo_done[0], POOL_PIECES)
                    pe.wait_ge(wlo_done[1], len(pieces) - POOL_PIECES)
                if n >= 2:
                    pe.wait_ge(silu_done, n - 1)
                pe.wait_ge(xlo_done, n + 1)
                at = pe.snap(e * F)
                m = 0
                for a, b_ in ((0, 0), (1, 0), (0, 1)):
                    for c in range(DC):
                        last = nc.tensor.matmul(hb[n % 2][:], xT[a][:, n % 2, c * P:(c + 1) * P],
                                                w1[b_][:, c, bass.ds(at, F)], start=(m == 0), stop=(m == 3 * DC - 1))
                        m += 1
                last.then_inc(h_full, 1)

            def turn_h(n):
                pe.wait_ge(silu_done, n + 1)
                if n >= 2:
                    pe.wait_ge(hlo_done, n - 1)
                for f in range(FC):
                    cols = slice(f * P, (f + 1) * P)
                    last = nc.tensor.transpose(tb[n % 2][:, cols], h[:, n % 2, cols], ident[:])
                last.then_inc(t_full, 1)

            def outward(n, e):
                pe.wait_ge(hlo_done, n + 1)
                if n:
                    pe.wait_ge(y_ready, n)
                at = pe.snap(e * D)
                m = 0
                for a, b_ in ((0, 0), (1, 0), (0, 1)):
                    for f in range(FC):
                        last = nc.tensor.matmul(yb[:], hT[a][:, n % 2, f * P:(f + 1) * P],
                                                w2[b_][:, f, bass.ds(at, D)], start=(m == 0), stop=(m == 3 * FC - 1))
                        m += 1
                last.then_inc(y_full, 1)

            def expert_of(n):
                ph, i = divmod(n, NTILE)
                if i == 0:
                    pe.wait_ge(table_ready, ph + 1)
                return pe.value_load(table[0:1, ph % B, i:i + 1], min_val=0, max_val=E - 1)

            pe.wait_ge(consts, 1)
            for i in range(NTILE):
                for it in items_at(-1, i):
                    take(it)
            turn_x(0)
            for n in range(ALL + 2):
                if n < ALL:
                    hidden(n, expert_of(n))
                first_next = (n + 1) % NTILE == 0
                if n + 1 < ALL and not first_next:
                    turn_x(n + 1)
                if 1 <= n <= ALL:
                    turn_h(n - 1)
                if n < ALL:
                    for it in items_at(*divmod(n, NTILE)):
                        take(it)
                if n >= 2:
                    outward(n - 2, expert_of(n - 2))
                if n + 1 < ALL and first_next:
                    turn_x(n + 1)

        @block.scalar
        def _(act):
            def weight_hi(i):
                w, _, c, j = pieces[i]
                act.wait_ge(piece_in[i], 16)
                hi, lo = (t[:, c, j * WC:(j + 1) * WC] for t in w)
                nc.scalar.copy(hi, lo.bitcast(F32)).then_inc(whi_done, 1)

            def side(ph, i):
                n = ph + 1
                for it in items_at(ph, i):
                    if it[0] in ("aoT", "x"):
                        _, _, c, q = it
                        k = index[it]
                        first_use = (c, q) == (0, 0)
                        if first_use and it[0] == "x" and n < B:
                            act.wait_ge(misc_full, index[("proj", n, 3)] + 1)
                        if first_use and n and (it[0] == "aoT" or n >= B):
                            act.wait_ge(misc_full, index[("logits", n - 1)] + 1)
                        if it[0] == "x":
                            act.wait_ge(rms_var, n + 1)
                        act.wait_ge(misc_full, k + 1)
                        drained(nc.scalar.copy(xnT[:, c, q * 512:(q + 1) * 512], misc[k % 2][:]), it)

            def functions(ph, i):
                n = ph + 1
                if n < B and i == LN_AT + 1:
                    act.wait_ge(ln_var, n + 1)
                    nc.scalar.activation(sd[:, 0, :], sd[:, 0, :], ACT.Sqrt).then_inc(ln_std, 1)
                if n < PH and i == RMS_AT:
                    act.wait_ge(rms_var, n + 1)
                    nc.scalar.activation(sd[:, 1, :], sd[:, 1, :], ACT.Sqrt).then_inc(rms_std, 1)
                if n < PH and i == X_AT + 3:
                    act.wait_ge(logits_less, n + 1)
                    nc.scalar.activation(lg[:], lg[:], ACT.Exp).then_inc(logits_exp, 1)

            def silu(n):
                act.wait_ge(h_full, n + 1)
                if n >= 2:
                    act.wait_ge(t_full, n - 1)
                nc.scalar.activation(h[:, n % 2, :], hb[n % 2][:], ACT.Silu).then_inc(silu_done, 1)

            def high_h(n):
                act.wait_ge(t_full, n + 1)
                if n >= 2:
                    act.wait_ge(y_full, n - 1)
                nc.scalar.copy(hT[0][:, n % 2, :], tb[n % 2][:]).then_inc(hhi_done, 1)

            def high_x(n):
                act.wait_ge(x_turned, n + 1)
                if n >= 2:
                    act.wait_ge(h_full, n - 1)
                nc.scalar.copy(xT[0][:, n % 2, :], xb[:]).then_inc(xhi_done, 1)

            def write_y(n):
                ph, i = divmod(n, NTILE)
                act.wait_ge(y_ready, n + 1)
                act.dma_start(tile_rows(ydisp_d[ph % B], i), yo[:, n % SL, :]).then_inc(y_out[n % SL], 16)

            for i in range(NTILE):
                functions(-1, i)
                side(-1, i)
                for k in HI_AT.get(i, ()):
                    weight_hi(k)
            high_x(0)
            for n in range(ALL + 4):
                if n < ALL:
                    silu(n)
                    functions(*divmod(n, NTILE))
                first_next = (n + 1) % NTILE == 0
                if n + 1 < ALL and not first_next:
                    high_x(n + 1)
                if 1 <= n <= ALL:
                    high_h(n - 1)
                if n + 1 < ALL and first_next:
                    high_x(n + 1)
                if n < ALL:
                    side(*divmod(n, NTILE))
                if 3 <= n < ALL + 3:
                    write_y(n - 3)

        @block.vector
        def _(dve):
            s = Steps(dve, dve_steps)
            eng = nc.vector
            proj_b = vkeep[:, VEC["proj_b"][0]:VEC["proj_b"][1]]

            def wide(a, k):
                return a.unsqueeze(2).to_broadcast([P, HT, k])

            def root(which, ready, eps_in):
                v = mv[:, :, 1]
                s.link(eng.tensor_scalar(v, v, *eps_in, ALU.mult, ALU.add))
                eng.tensor_copy(sd[:, which, :], v).then_inc(ready, 1)

            roots = [0]

            def root_end(which, done, count):
                dve.wait_ge(done, count)
                r_ = sd[:, which, :]
                s.link(eng.reciprocal(r_, r_))
                t = mm[:, :, 0]
                s.link(eng.tensor_tensor(t, r_, r_, ALU.mult))
                s.link(eng.tensor_tensor(t, t, mv[:, :, 1], ALU.mult))
                s.link(eng.tensor_scalar(t, t, -0.5, 1.5, ALU.mult, ALU.add))
                eng.tensor_tensor(r_, r_, t, ALU.mult).then_inc(root_ready, 1)
                roots[0] += 1
                dve.wait_ge(root_ready, roots[0])

            def residual(it):
                _, b, q = it
                i = index[it]
                dve.wait_ge(misc_full, i + 1)
                if q == 0:
                    dve.wait_ge(xz_in[b], 16)
                dve.wait_ge(misc_full, index[("aoT", b, DC - 1, 1)] + 1)
                zz = z[:, b * HT + 2 * q:b * HT + 2 * q + 2, :]
                x1 = xn[:, 2 * q:2 * q + 2, :]
                ins = eng.tensor_tensor(x1, zz, misc[i % 2][:].rearrange("p (t d) -> p t d", d=D), ALU.add)
                drained(ins, it)
                wait_drained(dve, it)
                ins = eng.tensor_tensor(x1, x1, proj_b.unsqueeze(1).to_broadcast([P, 2, D]), ALU.add)
                s.mark(ins) if q < 3 else ins.then_inc(x1_ready, 1)

            def add_results(ph, t):
                b = ph % B
                for w in range(2):
                    k = 2 * HT * ph + 2 * t + w
                    dve.wait_ge(y_in[k % YB], 16 * (k // YB + 1))
                    if w:
                        dve.wait_ge(gathered, k)
                    zt = z[:, b * HT + t, :]
                    eng.scalar_tensor_tensor(zt, yg[:, k % YB, :], wt[:, b, w, t:t + 1], zt, ALU.mult,
                                             ALU.add).then_inc(gathered, 1)

            def squares(n, t):
                rows = xnT[:].rearrange("p c q -> p (c q)").rearrange("p (t d) -> p t d", d=D)[:, t:t + 2, :]
                zt = z[:, (n % B) * HT + t:(n % B) * HT + t + 2, :]
                s.link(eng.tensor_tensor(rows, zt, zt, ALU.mult))
                s.mark(eng.tensor_reduce(mv[:, t:t + 2, 1], rows, X, ALU.add))

            def less_maximum(n):
                it = ("logits", n)
                i = index[it]
                dve.wait_ge(misc_full, i + 1)
                ins = eng.tensor_copy(lg[:], misc[i % 2][:, 0:HT * NE12].rearrange("p (t n) -> p t n", t=HT))
                drained(ins, it)
                wait_drained(dve, it)
                pairs = lg[:, :, G:NE12].rearrange("p t (g m) -> p t g m", m=2)
                s.mark(eng.tensor_reduce(mm[:, :, 0:1], lg[:, :, 0:G], X, ALU.max))
                s.link(eng.tensor_reduce(mm[:, :, 1:1 + G], pairs, X, ALU.max))
                s.link(eng.tensor_tensor(lg[:, :, 0:G], lg[:, :, 0:G], wide(mm[:, :, 0], G), ALU.subtract))
                eng.tensor_tensor(pairs, pairs, mm[:, :, 1:1 + G].unsqueeze(3).to_broadcast([P, HT, G, 2]),
                                  ALU.subtract).then_inc(logits_less, 1)

            def choose_groups(n):
                dve.wait_ge(logits_exp, n + 1)
                p = lg[:, :, 0:G]
                pairs = lg[:, :, G:NE12].rearrange("p t (g m) -> p t g m", m=2)
                s.mark(eng.tensor_reduce(mm[:, :, 0:1], p, X, ALU.add))
                s.link(eng.tensor_reduce(mm[:, :, 1:1 + G], pairs, X, ALU.add))
                s.link(eng.reciprocal(mm[:], mm[:]))
                s.mark(eng.tensor_tensor(p, p, wide(mm[:, :, 0], G), ALU.mult))
                s.link(eng.tensor_tensor(pairs, pairs, mm[:, :, 1:1 + G].unsqueeze(3).to_broadcast([P, HT, G, 2]),
                                         ALU.mult))
                other = p.unsqueeze(2).to_broadcast([P, HT, G, G])
                own = p.unsqueeze(3).to_broadcast([P, HT, G, G])
                s.mark(eng.tensor_tensor(tops[:, 1], other, own, ALU.is_gt))
                s.link(eng.tensor_tensor(tops[:, 0], other, own, ALU.is_ge))
                s.link(eng.tensor_tensor(tops[:, 0], tops[:, 0], ahead[:].unsqueeze(1).to_broadcast([P, HT, G, G]),
                                         ALU.mult))
                s.link(eng.tensor_tensor(tops[:, 0], tops[:, 0], tops[:, 1], ALU.max))
                s.link(eng.tensor_reduce(rk[:].unsqueeze(3), tops[:, 0], X, ALU.add))

            def choose_experts(n):
                pairs = lg[:, :, G:NE12].rearrange("p t (g m) -> p t g m", m=2)
                s.mark(eng.tensor_scalar(sel[:], rk[:], 2.0, None, ALU.is_lt))
                s.link(eng.tensor_tensor(ge[:], pairs[:, :, :, 0], pairs[:, :, :, 1], ALU.is_ge))
                flags = chosen[:].rearrange("p t (g m) -> p t g m", m=2)
                s.link(eng.tensor_tensor(flags[:, :, :, 0], sel[:], ge[:], ALU.mult))
                s.link(eng.tensor_tensor(flags[:, :, :, 1], sel[:], flags[:, :, :, 0], ALU.subtract))
                eng.tensor_copy(chosen_b[:], chosen[:]).then_inc(chosen_ready, 1)
                s.link(eng.tensor_tensor(wg[:], sel[:], lg[:, :, 0:G], ALU.mult))
                s.link(eng.tensor_reduce(mm[:, :, 0:1], wg[:], X, ALU.add))
                s.link(eng.tensor_reduce(mm[:, :, 1:1 + G], pairs, X, ALU.max))
                s.link(eng.tensor_copy(rk[:], mm[:, :, 1:1 + G]))
                s.link(eng.tensor_scalar(mm[:], mm[:], TOP_EPS, None, ALU.add))
                s.link(eng.reciprocal(mm[:], mm[:]))
                s.mark(eng.tensor_tensor(rk[:], rk[:], mm[:, :, 1:1 + G], ALU.mult))
                s.link(eng.tensor_tensor(wg[:], wg[:], wide(mm[:, :, 0], G), ALU.mult))
                s.link(eng.tensor_tensor(wg[:], wg[:], rk[:], ALU.mult))
                c4 = cw[:].rearrange("p t (g m) -> p t g m", m=2)
                s.link(eng.tensor_tensor(c4[:, :, :, 0], wg[:], ge[:], ALU.mult))
                s.link(eng.tensor_tensor(c4[:, :, :, 1], wg[:], c4[:, :, :, 0], ALU.subtract))

            def count(n):
                it = ("counts", n)
                i = index[it]
                dve.wait_ge(misc_full, i + 1)
                bank = misc[i % 2]
                tokens = bank[:, HT * E:HT * E + E].unsqueeze(2).to_broadcast([P, E, HT])
                s.link(eng.tensor_tensor(fits[:], tokens, thr[:], ALU.is_gt))
                s.link(eng.tensor_reduce(tiles_e[:].unsqueeze(2), fits[:], X, ALU.add))
                s.link(eng.tensor_copy(ends[:], tiles_e[:]))
                for e in range(1, E):
                    s.link(eng.tensor_tensor(ends[:, e:e + 1], ends[:, e:e + 1], ends[:, e - 1:e], ALU.add))
                s.link(eng.tensor_tensor(base[:], ends[:], tiles_e[:], ALU.subtract))
                s.link(eng.tensor_scalar(base[:], base[:], float(P), 1.0, ALU.mult, ALU.add))

            def sort(n):
                b = n % B
                it = ("counts", n)
                rank = misc[index[it] % 2][:, 0:HT * E].rearrange("p (t e) -> p t e", t=HT)
                drained(eng.tensor_tensor(place[:], base[:].unsqueeze(1).to_broadcast([P, HT, E]), rank, ALU.add), it)
                wait_drained(dve, it)
                s.link(eng.tensor_tensor(place[:], place[:], chosen[:], ALU.mult))
                s.link(eng.tensor_reduce(pq[:, 1, :].unsqueeze(2), place[:], X, ALU.max))
                s.link(eng.tensor_tensor(last_one[:], place[:], wide(pq[:, 1, :], E), ALU.is_equal))
                s.link(eng.tensor_tensor(chosen[:], chosen[:], last_one[:], ALU.subtract))
                s.link(eng.tensor_tensor(place[:], place[:], chosen[:], ALU.mult))
                s.link(eng.tensor_reduce(pq[:, 0, :].unsqueeze(2), place[:], X, ALU.add))
                eng.tensor_scalar(idx[:, b], pq[:], -1.0, None, ALU.add).then_inc(sorted_, 1)

            def weights_and_table(n):
                b = n % B
                for w, flags in ((0, chosen), (1, last_one)):
                    s.link(eng.tensor_tensor(scratch[:], cw[:], flags[:], ALU.mult))
                    s.link(eng.tensor_reduce(wt[:, b, w, :].unsqueeze(2), scratch[:], X, ALU.add))
                s.link(eng.tensor_tensor(tcmp[:], tix[:], ends[0:1, :].unsqueeze(1).to_broadcast([1, NTILE, E]),
                                         ALU.is_ge))
                s.link(eng.tensor_reduce(tef[:].unsqueeze(2), tcmp[:], X, ALU.add))
                if n >= B:
                    dve.wait_ge(y_full, (n - 1) * NTILE)
                eng.tensor_scalar(table[:, b, :], tef[:], float(E - 1), None, ALU.min).then_inc(table_ready, 1)

            def side(ph, i):
                n = ph + 1
                b = n % B
                for it in items_at(ph, i):
                    if it[0] == "proj":
                        residual(it)
                if n < B and i == LN_AT:
                    dve.wait_ge(x1_ready, n + 1)
                    dve.wait_ge(dve_steps, s.n)
                    for t in range(HT):
                        s.mark(eng.bn_stats(st6[:, t, :], xn[:, t, :]))
                    dve.wait_ge(dve_steps, s.n)
                    for t in range(HT):
                        s.mark(eng.bn_aggr(mv[:, t, :], st6[:, t, :]))
                    dve.wait_ge(dve_steps, s.n)
                    s.mark(eng.tensor_copy(mm[:, :, 1], mv[:, :, 1]))
                    root(0, ln_var, (1.0, LN_EPS))
                if n < B and i == LN_AT + 1:
                    root_end(0, ln_std, n + 1)
                    s.link(eng.tensor_tensor(mv[:, :, 1], mm[:, :, 1], sd[:, 0, :], ALU.mult))
                    s.mark(eng.tensor_tensor(mv[:, :, 1], mv[:, :, 1], sd[:, 0, :], ALU.mult))
                    for t in range(HT):
                        zt = z[:, b * HT + t, :]
                        s.mark(eng.tensor_scalar(zt, xn[:, t, :], mv[:, t, 0:1], sd[:, 0, t:t + 1], ALU.subtract,
                                                 ALU.mult))
                    dve.wait_ge(dve_steps, s.n)
                if n >= B and 0 <= i - GATHER_AT < 4:
                    for t in range(2 * (i - GATHER_AT), 2 * (i - GATHER_AT) + 2):
                        add_results(n - B, t)
                if B <= n < PH and 0 <= i - GATHER_AT < 4:
                    dve.wait_ge(gathered, 2 * HT * (n - B) + 4 * (i - GATHER_AT + 1))
                    if i == GATHER_AT:
                        dve.wait_ge(misc_full, index[("logits", n - 1)] + 1)
                    squares(n, 2 * (i - GATHER_AT))
                if n < PH and i == RMS_AT - 1:
                    dve.wait_ge(dve_steps, s.n)
                    root(1, rms_var, (1.0 if n < B else 1.0 / D, RMS_EPS))
                if n < PH and i == RMS_AT:
                    root_end(1, rms_std, n + 1)
                    if n < B:
                        dve.wait_ge(x1_out[n], 16)
                    else:
                        dve.wait_ge(scattered, 16 * 2 * HT * n)
                        dve.wait_ge(misc_full, index[("x", n - 1, 1, 1)] + 1)
                    for t in range(DVE_SCALES if n else HT):
                        eng.scalar_tensor_tensor(xn[:, t, :], z[:, b * HT + t, :], sd[:, 1, t:t + 1], norm_w, ALU.mult,
                                                 ALU.mult).then_inc(xn_ready, 1)
                if n < PH and i == X_AT + 2:
                    less_maximum(n)
                if n < PH and i == X_AT + 4:
                    choose_groups(n)
                if n < PH and i == X_AT + 5:
                    choose_experts(n)
                if n < PH and i == X_AT + 6:
                    count(n)
                if n < PH and i == X_AT + 6:
                    sort(n)
                if n < PH and i == X_AT + 7:
                    weights_and_table(n)
                if n >= PH and i == GATHER_AT + 4:
                    dve.wait_ge(rows_in, 16 * (n - PH + B + 1))
                    dve.wait_ge(gathered, 2 * HT * (n - B + 1))
                    zz = z[:, b * HT:(b + 1) * HT, :]
                    eng.tensor_tensor(zz, zz, xn[:], ALU.add).then_inc(out_ready, 1)

            def low_h(n):
                dve.wait_ge(hhi_done, n + 1)
                eng.tensor_tensor(hT[1][:, n % 2, :], tb[n % 2][:], hT[0][:, n % 2, :].bitcast(F32),
                                  ALU.subtract).then_inc(hlo_done, 1)

            def low_x(n):
                dve.wait_ge(xhi_done, n + 1)
                eng.tensor_tensor(xT[1][:, n % 2, :], xb[:], xT[0][:, n % 2, :].bitcast(F32),
                                  ALU.subtract).then_inc(xlo_done, 1)

            def result(n):
                dve.wait_ge(y_full, n + 1)
                if n >= SL:
                    dve.wait_ge(y_out[n % SL], 16 * (n // SL))
                eng.tensor_copy(yo[:, n % SL, :], yb[:]).then_inc(y_ready, 1)

            dve.wait_ge(consts, 1)
            for i in range(NTILE):
                side(-1, i)
            for i in range(POOL_PIECES, len(pieces)):
                dve.wait_ge(whi_done, i + 1)
                low_part(eng, i).then_inc(wlo_done[1], 1)
            low_x(0)
            for n in range(ALL + 2):
                first_next = (n + 1) % NTILE == 0
                if n + 1 < ALL and not first_next:
                    low_x(n + 1)
                if 1 <= n <= ALL:
                    low_h(n - 1)
                if n >= 2:
                    result(n - 2)
                if n + 1 < ALL and first_next:
                    low_x(n + 1)
                if n < ALL:
                    side(*divmod(n, NTILE))
            for i in range(NTILE):
                side(PH, i)

def kernel(**inputs):
    import numpy as _np
    import concourse.bacc as _bacc
    from concourse import mybir as _mybir
    from concourse.bass_utils import run_bass_kernel_spmd as _run

    arrays = laid_out(_np, inputs)
    nc = _bacc.Bacc("TRN2", target_bir_lowering=False, num_devices=1)
    args = {name: nc.dram_tensor(f"in_{name}", a.shape, _mybir.dt.from_np(a.dtype), kind="ExternalInput").ap()
            for name, a in arrays.items()}
    out = nc.dram_tensor("out_x", (B * T, D), F32, kind="ExternalOutput").ap()
    build(nc, out=out, **args)
    r = _run(nc, [{f"in_{name}": a for name, a in arrays.items()}], core_ids=[0])
    return r.results[0]["out_x"].reshape(B, T, D)


def laid_out(np, inputs):
    i = {name: np.asarray(a) for name, a in inputs.items()}
    c = np.ascontiguousarray
    rows = [i[n].reshape(-1) for n in (
        "L0_xattn_proj_b", "L0_ffn_norm_w", "L0_xattn_hist_b", "L0_xattn_hist_ln_g", "L0_xattn_hist_ln_b",
        "L0_xattn_ctx_b1", "L0_xattn_ctx_W2", "L0_xattn_ctx_b2", "L0_xattn_kg_b1", "L0_xattn_kg_ln_g",
        "L0_xattn_kg_ln_b", "L0_xattn_kg_b2")]
    router = np.concatenate([i["L0_ffn_w_macro"], i["L0_ffn_w_micro"].reshape(E, D)], axis=0)
    return {
        "x": c(i["x"].reshape(B * T, D)),
        "ctxT": c(i["ctx_1024"].reshape(NCT * S2, D).T),
        "hist_W": c(i["L0_xattn_hist_W"]), "ctx_W1": c(i["L0_xattn_ctx_W1"]),
        "kg_W1": c(i["L0_xattn_kg_W1"]), "kg_W2": c(i["L0_xattn_kg_W2"]),
        "Wq": c(i["L0_xattn_Wq"]), "Wk": c(i["L0_xattn_Wk"]), "Wv": c(i["L0_xattn_Wv"]),
        "proj_W": c(i["L0_xattn_proj_W"]),
        "vecs": c(np.concatenate(rows).reshape(1, NVEC)),
        "wrT": c(router.T),
        "mask": c(i["mask_SxS_bc0"]).view(np.int32),
        "w1T": c(i["L0_ffn_w1"].transpose(2, 0, 1)),
        "w2T": c(i["L0_ffn_w2"].transpose(2, 0, 1)),
    }
```
